# Optimizing a Trainium2 kernel written in Bass

```python
import numpy as np
import jax
import jax.numpy as jnp

def _softmax(x, axis=-1):
    return jax.nn.softmax(x, axis=axis)
def _gelu(x):
    return jax.nn.gelu(x, approximate=True)
def _silu(x):
    return jax.nn.silu(x)
def _sigmoid(x):
    return jax.nn.sigmoid(x)
def _layernorm(x, axis=-1, eps=1e-5):
    m = jnp.mean(x, axis=axis, keepdims=True)
    v = jnp.var(x, axis=axis, keepdims=True)
    return (x - m) / jnp.sqrt(v + eps)
def _scatter_add(tgt, idx, src, axis=0):
    return tgt.at[idx].add(src)
def _segment_sum(src, seg, n):
    return jax.ops.segment_sum(src, seg, n)

kernel_name = 'mk_conv_preact_d2_conv_nchw192_8ced0e'

def setup_inputs(seed: int = 0):
    np.random.seed(seed)
    _w = jnp.asarray
    def _rec_inputs():
        import jax
        import jax.numpy as jnp
        _gk = jax.random.key(seed)
        x = -0.0001836 + 1 * jax.random.normal(jax.random.fold_in(_gk, 1), (4, 192, 256, 256), jnp.float32)
        return x
    x = _rec_inputs()
    def _L0_conv_setup():
        import jax, jax.numpy as jnp
        import numpy as np
        P = 8
        DIM = 192
        key = jax.random.key(seed)
        k1, k2 = jax.random.split(key)
        x = jax.random.normal(k1, (8, DIM, 256, 256), dtype=jnp.float32)
        w_proj = jax.random.normal(k2, (DIM, DIM), dtype=jnp.float32) * 0.05
        fft_filter = jnp.ones((DIM, 1, 1, P, P // 2 + 1), dtype=jnp.float32)
        return {'x': x, 'w_proj': w_proj, 'fft_filter': fft_filter}
    _L0_conv_all = _L0_conv_setup()
    _L0_conv_in = {k: v for k, v in _L0_conv_all.items() if k in ('w_proj', 'fft_filter', )}
    del _L0_conv_all

    def _L1_conv_setup():
        import jax, jax.numpy as jnp
        import numpy as np
        import math
        C64 = jnp.complex64

        def _fftconv_full(a, kern):
            L = a.shape[-1] + kern.shape[0] - 1
            A = jnp.fft.fft(a, n=L, axis=-1)
            K = jnp.fft.fft(kern.astype(a.dtype), n=L)
            return jnp.fft.ifft(A * K, axis=-1)

        def _centered_ifft(f):
            N = f.shape[-1]
            shft = (np.arange(N) + int(np.fix(N / 2))) % N
            inv = np.argsort(shft)
            g = jnp.fft.ifft(f[..., shft], axis=-1) * math.sqrt(N)
            return g[..., inv].astype(f.dtype)

        def _sincinterp(f):
            N = f.shape[-1]
            y = jnp.zeros(f.shape[:-1] + (2 * N - 1,), f.dtype).at[..., ::2].set(f)
            kern = jnp.asarray(np.sinc(np.arange(-(2 * N - 3), 2 * N - 2) / 2.0).astype(np.complex64))
            return _fftconv_full(y, kern)[..., 2 * N - 3:4 * N - 4]

        def _frft_chirp(f, a):
            N = f.shape[-1]
            alpha = a * math.pi / 2
            tana2, sina = (math.tan(alpha / 2), math.sin(alpha))
            fi = _sincinterp(f)
            pad = jnp.zeros(f.shape[:-1] + (N - 1,), f.dtype)
            fp = jnp.concatenate([pad, fi, pad], axis=-1)
            n = np.arange(-2 * N + 2, 2 * N - 1).astype(np.float64)
            chrp = jnp.asarray(np.exp(-1j * math.pi / N * tana2 / 4 * n ** 2).astype(np.complex64))
            fp = chrp * fp
            c = math.pi / N / sina / 4
            m = np.arange(-(4 * N - 4), 4 * N - 3).astype(np.float64)
            kern = jnp.asarray(np.exp(1j * c * m ** 2).astype(np.complex64))
            ret = _fftconv_full(fp, kern)[..., 4 * N - 4:8 * N - 7] * math.sqrt(c / math.pi)
            ret = chrp * ret
            phase = np.complex64(np.exp(-1j * (1 - a) * math.pi / 4))
            return phase * ret[..., N - 1:3 * N - 2:2]

        def _frft_last(f, a):
            if a < 0.5:
                f = _centered_ifft(f)
                a = a + 1.0
            return _frft_chirp(f, a)

        def _frft2d(x, a):
            t = _frft_last(x, a)
            return jnp.swapaxes(_frft_last(jnp.swapaxes(t, -1, -2), a), -1, -2)

        def _c1x1(x, w, b=None):
            y = jnp.einsum('nchw,oc->nohw', x, w)
            return y if b is None else y + b[None, :, None, None]

        def _c3x3(x, w, b):
            y = jax.lax.conv_general_dilated(x, w, (1, 1), 'SAME', dimension_numbers=('NCHW', 'OIHW', 'NCHW'))
            return y + b[None, :, None, None]

        def _forward(x, conv1_w, mag_s_w, mag_s_b, mag_f_w, mag_f_b, mag_w, mag_b, pha_w, pha_b, conv_0_w, conv_0_b, conv_1_w, conv_1_b, conv2_w):
            angle = 0.5
            alpha = math.cos(angle * math.pi / 2)
            N, C, H, W = x.shape
            H1, W1 = (int(H * alpha), int(W * alpha))
            x1 = _c1x1(x, conv1_w)
            C1, C0 = (C // 4, C // 4 // 3)
            x_0, x_05, x_1 = (x1[:, :C0], x1[:, C0:C1 - C0], x1[:, C1 - C0:C1])
            h0, w0 = ((H - H1) // 2, (W - W1) // 2)
            mask1 = jnp.zeros((H, W), jnp.float32).at[h0:h0 + H1, w0:w0 + W1].set(1.0)
            mask2 = 1.0 - mask1
            Fre = _frft2d(x_05.astype(C64), angle)
            mag, pha = (jnp.abs(Fre), jnp.angle(Fre))
            mag_out = _c1x1(_c3x3(mag * mask1, mag_s_w, mag_s_b) * mask1 + _c1x1(mag * mask2, mag_f_w, mag_f_b) * mask2, mag_w, mag_b)
            pha_out = _c1x1(pha, pha_w, pha_b)
            Fre_out = jax.lax.complex(mag_out * jnp.cos(pha_out), mag_out * jnp.sin(pha_out))
            ifrft = jnp.abs(_frft2d(Fre_out, -angle))
            fre = jnp.fft.rfft2(x_1)
            fm, fp = (jnp.abs(fre), jnp.angle(fre))
            mo = _c1x1(fm, conv_1_w, conv_1_b)
            po = _c1x1(fp, conv_1_w, conv_1_b)
            x_1o = jnp.fft.irfft2(jax.lax.complex(mo * jnp.cos(po), mo * jnp.sin(po)), s=(H, W))
            x_0o = _c1x1(x_0, conv_0_w, conv_0_b)
            return _c1x1(jnp.concatenate([x_0o, ifrft, x_1o], axis=1), conv2_w)
        key = jax.random.key(seed)
        ks = jax.random.split(key, 16)
        N, C, H, W, Co = (4, 192, 128, 128, 192)
        C1, C0 = (C // 4, C // 4 // 3)
        Cm = C1 - 2 * C0
        s = 0.05
        r = lambda k, sh: jax.random.normal(k, sh, jnp.float32)
        return {'x': r(ks[0], (N, C, H, W)), 'conv1_w': r(ks[1], (C1, C)) * s, 'mag_s_w': r(ks[2], (Cm, Cm, 3, 3)) * s, 'mag_s_b': r(ks[3], (Cm,)) * s, 'mag_f_w': r(ks[4], (Cm, Cm)) * s, 'mag_f_b': r(ks[5], (Cm,)) * s, 'mag_w': r(ks[6], (Cm, Cm)) * s, 'mag_b': r(ks[7], (Cm,)) * s, 'pha_w': r(ks[8], (Cm, Cm)) * s, 'pha_b': r(ks[9], (Cm,)) * s, 'conv_0_w': r(ks[10], (C0, C0)) * s, 'conv_0_b': r(ks[11], (C0,)) * s, 'conv_1_w': r(ks[12], (C0, C0)) * s, 'conv_1_b': r(ks[13], (C0,)) * s, 'conv2_w': r(ks[14], (Co, C1)) * s}
    _L1_conv_all = _L1_conv_setup()
    _L1_conv_in = {k: v for k, v in _L1_conv_all.items() if k in ('conv1_w', 'mag_s_w', 'mag_s_b', 'mag_f_w', 'mag_f_b', 'mag_w', 'mag_b', 'pha_w', 'pha_b', 'conv_0_w', 'conv_0_b', 'conv_1_w', 'conv_1_b', 'conv2_w', )}
    del _L1_conv_all

    return {
        "x": x,
        "L0_conv_w_proj": _L0_conv_in["w_proj"],
        "L0_conv_fft_filter": _L0_conv_in["fft_filter"],
        "L1_conv_conv1_w": _L1_conv_in["conv1_w"],
        "L1_conv_mag_s_w": _L1_conv_in["mag_s_w"],
        "L1_conv_mag_s_b": _L1_conv_in["mag_s_b"],
        "L1_conv_mag_f_w": _L1_conv_in["mag_f_w"],
        "L1_conv_mag_f_b": _L1_conv_in["mag_f_b"],
        "L1_conv_mag_w": _L1_conv_in["mag_w"],
        "L1_conv_mag_b": _L1_conv_in["mag_b"],
        "L1_conv_pha_w": _L1_conv_in["pha_w"],
        "L1_conv_pha_b": _L1_conv_in["pha_b"],
        "L1_conv_conv_0_w": _L1_conv_in["conv_0_w"],
        "L1_conv_conv_0_b": _L1_conv_in["conv_0_b"],
        "L1_conv_conv_1_w": _L1_conv_in["conv_1_w"],
        "L1_conv_conv_1_b": _L1_conv_in["conv_1_b"],
        "L1_conv_conv2_w": _L1_conv_in["conv2_w"],
    }

def reference(x, L0_conv_w_proj, L0_conv_fft_filter, L1_conv_conv1_w, L1_conv_mag_s_w, L1_conv_mag_s_b, L1_conv_mag_f_w, L1_conv_mag_f_b, L1_conv_mag_w, L1_conv_mag_b, L1_conv_pha_w, L1_conv_pha_b, L1_conv_conv_0_w, L1_conv_conv_0_b, L1_conv_conv_1_w, L1_conv_conv_1_b, L1_conv_conv2_w):
    import jax
    import jax.numpy as jnp
    def _L0_conv_ref(x, w_proj, fft_filter):
        import jax, jax.numpy as jnp
        import numpy as np
        P = 8
        DIM = 192
        y = jnp.einsum('oc,bchw->bohw', w_proj, x)
        b, c, h, w = y.shape
        h_n = (P - h % P) % P
        w_n = (P - w % P) % P
        y = jnp.pad(y, ((0, 0), (0, 0), (0, h_n), (0, w_n)), mode='reflect')
        H, W = (y.shape[2], y.shape[3])
        yp = y.reshape(b, c, H // P, P, W // P, P).transpose(0, 1, 2, 4, 3, 5)
        f = jnp.fft.rfft2(yp.astype(jnp.float32))
        f = f * fft_filter
        yp = jnp.fft.irfft2(f, s=(P, P))
        y = yp.transpose(0, 1, 2, 4, 3, 5).reshape(b, c, H, W)
        return y[:, :, :h, :w]

    def _L1_conv_ref(x, conv1_w, mag_s_w, mag_s_b, mag_f_w, mag_f_b, mag_w, mag_b, pha_w, pha_b, conv_0_w, conv_0_b, conv_1_w, conv_1_b, conv2_w):
        import jax, jax.numpy as jnp
        import numpy as np
        import math
        C64 = jnp.complex64

        def _fftconv_full(a, kern):
            L = a.shape[-1] + kern.shape[0] - 1
            A = jnp.fft.fft(a, n=L, axis=-1)
            K = jnp.fft.fft(kern.astype(a.dtype), n=L)
            return jnp.fft.ifft(A * K, axis=-1)

        def _centered_ifft(f):
            N = f.shape[-1]
            shft = (np.arange(N) + int(np.fix(N / 2))) % N
            inv = np.argsort(shft)
            g = jnp.fft.ifft(f[..., shft], axis=-1) * math.sqrt(N)
            return g[..., inv].astype(f.dtype)

        def _sincinterp(f):
            N = f.shape[-1]
            y = jnp.zeros(f.shape[:-1] + (2 * N - 1,), f.dtype).at[..., ::2].set(f)
            kern = jnp.asarray(np.sinc(np.arange(-(2 * N - 3), 2 * N - 2) / 2.0).astype(np.complex64))
            return _fftconv_full(y, kern)[..., 2 * N - 3:4 * N - 4]

        def _frft_chirp(f, a):
            N = f.shape[-1]
            alpha = a * math.pi / 2
            tana2, sina = (math.tan(alpha / 2), math.sin(alpha))
            fi = _sincinterp(f)
            pad = jnp.zeros(f.shape[:-1] + (N - 1,), f.dtype)
            fp = jnp.concatenate([pad, fi, pad], axis=-1)
            n = np.arange(-2 * N + 2, 2 * N - 1).astype(np.float64)
            chrp = jnp.asarray(np.exp(-1j * math.pi / N * tana2 / 4 * n ** 2).astype(np.complex64))
            fp = chrp * fp
            c = math.pi / N / sina / 4
            m = np.arange(-(4 * N - 4), 4 * N - 3).astype(np.float64)
            kern = jnp.asarray(np.exp(1j * c * m ** 2).astype(np.complex64))
            ret = _fftconv_full(fp, kern)[..., 4 * N - 4:8 * N - 7] * math.sqrt(c / math.pi)
            ret = chrp * ret
            phase = np.complex64(np.exp(-1j * (1 - a) * math.pi / 4))
            return phase * ret[..., N - 1:3 * N - 2:2]

        def _frft_last(f, a):
            if a < 0.5:
                f = _centered_ifft(f)
                a = a + 1.0
            return _frft_chirp(f, a)

        def _frft2d(x, a):
            t = _frft_last(x, a)
            return jnp.swapaxes(_frft_last(jnp.swapaxes(t, -1, -2), a), -1, -2)

        def _c1x1(x, w, b=None):
            y = jnp.einsum('nchw,oc->nohw', x, w)
            return y if b is None else y + b[None, :, None, None]

        def _c3x3(x, w, b):
            y = jax.lax.conv_general_dilated(x, w, (1, 1), 'SAME', dimension_numbers=('NCHW', 'OIHW', 'NCHW'))
            return y + b[None, :, None, None]

        def _forward(x, conv1_w, mag_s_w, mag_s_b, mag_f_w, mag_f_b, mag_w, mag_b, pha_w, pha_b, conv_0_w, conv_0_b, conv_1_w, conv_1_b, conv2_w):
            angle = 0.5
            alpha = math.cos(angle * math.pi / 2)
            N, C, H, W = x.shape
            H1, W1 = (int(H * alpha), int(W * alpha))
            x1 = _c1x1(x, conv1_w)
            C1, C0 = (C // 4, C // 4 // 3)
            x_0, x_05, x_1 = (x1[:, :C0], x1[:, C0:C1 - C0], x1[:, C1 - C0:C1])
            h0, w0 = ((H - H1) // 2, (W - W1) // 2)
            mask1 = jnp.zeros((H, W), jnp.float32).at[h0:h0 + H1, w0:w0 + W1].set(1.0)
            mask2 = 1.0 - mask1
            Fre = _frft2d(x_05.astype(C64), angle)
            mag, pha = (jnp.abs(Fre), jnp.angle(Fre))
            mag_out = _c1x1(_c3x3(mag * mask1, mag_s_w, mag_s_b) * mask1 + _c1x1(mag * mask2, mag_f_w, mag_f_b) * mask2, mag_w, mag_b)
            pha_out = _c1x1(pha, pha_w, pha_b)
            Fre_out = jax.lax.complex(mag_out * jnp.cos(pha_out), mag_out * jnp.sin(pha_out))
            ifrft = jnp.abs(_frft2d(Fre_out, -angle))
            fre = jnp.fft.rfft2(x_1)
            fm, fp = (jnp.abs(fre), jnp.angle(fre))
            mo = _c1x1(fm, conv_1_w, conv_1_b)
            po = _c1x1(fp, conv_1_w, conv_1_b)
            x_1o = jnp.fft.irfft2(jax.lax.complex(mo * jnp.cos(po), mo * jnp.sin(po)), s=(H, W))
            x_0o = _c1x1(x_0, conv_0_w, conv_0_b)
            return _c1x1(jnp.concatenate([x_0o, ifrft, x_1o], axis=1), conv2_w)
        return _forward(x, conv1_w, mag_s_w, mag_s_b, mag_f_w, mag_f_b, mag_w, mag_b, pha_w, pha_b, conv_0_w, conv_0_b, conv_1_w, conv_1_b, conv2_w)

    def _gn(v, G=32, eps=1e-5):
        B_, C_, H_, W_ = v.shape
        g = v.reshape(B_, G, C_ // G, H_, W_)
        m = jnp.mean(g, axis=(2, 3, 4), keepdims=True)
        s = jnp.var(g, axis=(2, 3, 4), keepdims=True)
        return ((g - m) / jnp.sqrt(s + eps)).reshape(v.shape)

    def _ln_c(v, eps=1e-6):
        m = jnp.mean(v, axis=1, keepdims=True)
        s = jnp.var(v, axis=1, keepdims=True)
        return (v - m) / jnp.sqrt(s + eps)

    def _ln_t(v, eps=1e-5):
        m = jnp.mean(v, axis=-1, keepdims=True)
        s = jnp.var(v, axis=-1, keepdims=True)
        return (v - m) / jnp.sqrt(s + eps)

    def _to_tokens(v):
        B_, C_, H_, W_ = v.shape
        return v.reshape(B_, C_, H_ * W_).transpose(0, 2, 1)
    def _from_tokens(t, like):
        B_, C_, H_, W_ = like.shape
        return t.transpose(0, 2, 1).reshape(B_, C_, H_, W_)

    x = x + _L0_conv_ref(_gn(x), L0_conv_w_proj, L0_conv_fft_filter)
    x = x + _L1_conv_ref(_gn(x), L1_conv_conv1_w, L1_conv_mag_s_w, L1_conv_mag_s_b, L1_conv_mag_f_w, L1_conv_mag_f_b, L1_conv_mag_w, L1_conv_mag_b, L1_conv_pha_w, L1_conv_pha_b, L1_conv_conv_0_w, L1_conv_conv_0_b, L1_conv_conv_1_w, L1_conv_conv_1_b, L1_conv_conv2_w)
    return x


_drawn_inputs = setup_inputs


def setup_inputs(seed=0):
    import zlib

    import numpy as np

    out = dict(_drawn_inputs(seed))
    spreads = {'L0_conv_fft_filter': (1.0, 0.2)}
    factors = {'L1_conv_mag_s_w': 8.0,
     'L1_conv_mag_s_b': 8.0,
     'L1_conv_mag_f_w': 8.0,
     'L1_conv_mag_f_b': 8.0,
     'L1_conv_mag_w': 8.0,
     'L1_conv_mag_b': 8.0,
     'L1_conv_pha_w': 8.0,
     'L1_conv_pha_b': 64.0,
     'L1_conv_conv_0_b': 5.67,
     'L1_conv_conv_1_w': 2.673,
     'L1_conv_conv_1_b': 31.543,
     'L1_conv_conv_0_w': 2.822}
    for name, (base, spread) in spreads.items():
        noise = np.random.default_rng([zlib.crc32(name.encode()), seed]).standard_normal(out[name].shape)
        drawn = base * np.exp(spread * noise) if base else spread * noise
        out[name] = jnp.asarray(drawn.astype(out[name].dtype))
    for name, factor in factors.items():
        out[name] = (out[name] * factor).astype(out[name].dtype)
    return out
```

```python
import math
from contextlib import ExitStack

import numpy as np

import concourse.bass as bass
from concourse import mybir

ALU = mybir.AluOpType
ACT = mybir.ActivationFunctionType
F32 = mybir.dt.float32
U8 = mybir.dt.uint8

P = 128
NB, C, SIDE = 4, 192, 256
HC = C // 2
PATCH = 8
STRIPES = SIDE // PATCH
SPX = PATCH * SIDE
TILES = SPX // P
QUADS = 4
GROUPS, GC = 32, C // 32
C0 = 16
C1 = 48
BLK = 8
NFREQ = SIDE // 2 + 1
LO = (SIDE - int(SIDE * math.cos(math.pi / 4))) // 2
HI = LO + int(SIDE * math.cos(math.pi / 4))
EPS = 1e-5


def frft_matrix():
    n_ = SIDE
    a = 0.5
    alpha = a * math.pi / 2
    n = np.arange(-2 * n_ + 2, 2 * n_ - 1).astype(np.float64)
    chirp = np.exp(-1j * math.pi / n_ * math.tan(alpha / 2) / 4 * n**2)
    c = math.pi / n_ / math.sin(alpha) / 4
    mid = slice(n_ - 1, 3 * n_ - 2)
    sinc = np.sinc((np.arange(2 * n_ - 1)[:, None] - 2 * np.arange(n_)[None, :]) / 2.0)
    outs = n[mid][::2]
    kern = np.exp(1j * c * (outs[:, None] - n[mid][None, :]) ** 2) * math.sqrt(c / math.pi)
    return np.exp(-1j * (1 - a) * math.pi / 4) * (
        chirp[mid][::2][:, None] * kern * chirp[mid][None, :] @ sinc)


def centered_ifft_matrix():
    shift = (np.arange(SIDE) + SIDE // 2) % SIDE
    inverse = np.argsort(shift)
    g = np.fft.ifft(np.eye(SIDE)[:, shift], axis=-1) * math.sqrt(SIDE)
    return g[:, inverse].T


def cos_sin(n):
    j = (np.arange(n)[:, None] * np.arange(n)[None, :]) % n
    c, s = np.cos(2 * np.pi * j / n), np.sin(2 * np.pi * j / n)
    quarter = (4 * j) % n == 0
    c[quarter], s[quarter] = np.round(c[quarter]), np.round(s[quarter])
    return c, s


def patch_basis():
    y, x = np.meshgrid(np.arange(PATCH), np.arange(PATCH), indexing="ij")
    basis, taps = [], []
    for kx in range(PATCH // 2 + 1):
        for ky in range(PATCH):
            edge = kx in (0, PATCH // 2)
            if edge and ky > PATCH // 2:
                continue
            phase = 2 * np.pi * ((ky * y + kx * x) % PATCH) / PATCH
            tap = np.zeros((PATCH, PATCH // 2 + 1))
            tap[ky, kx] += 0.5
            tap[(-ky) % PATCH if edge else ky, kx] += 0.5
            alone = edge and ky in (0, PATCH // 2)
            norm = 1 / PATCH if alone else math.sqrt(2) / PATCH
            basis.append(np.cos(phase) * norm)
            taps.append(tap)
            if not alone:
                basis.append(np.sin(phase) * norm)
                taps.append(tap)
    return np.array(basis).reshape(64, 64), np.array(taps).reshape(64, 40).T


def two_rows(m):
    return m.reshape(2, P, -1).transpose(1, 0, 2)


def constants():
    basis, taps = patch_basis()
    d = np.zeros((2, 64, PATCH, 2, PATCH))
    for i in range(2):
        d[i, :, :, i, :] = basis.reshape(64, PATCH, PATCH)
    d = d.reshape(P, P)
    ch, part = np.arange(C), np.arange(P)
    a, b = frft_matrix(), frft_matrix() @ centered_ifft_matrix()
    cos, sin = cos_sin(SIDE)
    windows = lambda m: two_rows(np.concatenate([-m.imag.T, m.real.T, m.imag.T], 1))
    k = np.arange(P)[:, None] * np.arange(SIDE)[None, :] % SIDE
    twice = np.where(np.arange(P) == 0, 1.0, 2.0)[:, None] / SIDE**2
    back_re = twice * cos[1][k]
    back_im = -twice * sin[1][k]
    back_im[0] = (-1.0) ** np.arange(SIDE) / SIDE**2
    u = np.arange(P) // C0
    band = lambda off: (u[:, None] == np.arange(BLK)[None, :] + off).astype(float)
    out = {
        "c_basis": np.stack([d.T, d], 1),
        "c_taps": np.concatenate([taps, taps], 1),
        "c_group_x": (part[:, None] // 4 == part[None, :] // 4) / 4.0,
        "c_group_x_ch": (part[:, None] // 4 == ch[None, :] // GC) / 4.0,
        "c_group_ch": (np.arange(HC)[:, None] // GC == np.arange(HC)[None, :] // GC) / float(GC),
        "c_eye": np.eye(P),
        "c_frft": windows(a),
        "c_ifrft": windows(b),
        "c_dft": two_rows(np.concatenate([-sin, cos, sin, cos, -sin], 1)),
        "c_rfft": two_rows(np.concatenate([cos[:, :NFREQ], -sin[:, :NFREQ]], 1)),
        "c_irfft": np.stack([back_re, back_im], 1),
        "c_rep": np.tile(np.eye(C0), (1, BLK)),
        "c_band": np.stack([band(-1), band(0), band(1),
                            (u[:, None] == BLK - 1) * (np.arange(BLK)[None, :] == 0) * 1.0,
                            (u[:, None] == 0) * (np.arange(BLK)[None, :] == BLK - 1) * 1.0], 1),
    }
    return {n: np.ascontiguousarray(v, dtype=np.float32) for n, v in out.items()}


class Core:

    def __init__(self, nc, dram):
        self.nc, self.dram = nc, dram
        self.stack = ExitStack()

    def sbuf(self, stack, name, shape, dtype=F32):
        return stack.enter_context(self.nc.sbuf_tensor(name, shape, dtype))

    def psum(self, stack, name, shape):
        return stack.enter_context(self.nc.psum_tensor(name, shape, F32))

    def sem(self, name):
        return self.stack.enter_context(self.nc.semaphore(name))


def bcast(ap, axis, n):
    shape = list(ap.shape)
    view = ap.unsqueeze(axis)
    return view.to_broadcast(shape[:axis] + [n] + shape[axis:])


def input_statistics(k):
    nc, d = k.nc, k.dram
    CHUNK = 6144
    RECORD = 512
    PER = GC * SIDE * SIDE // 4
    CH = PER // CHUNK
    RECS = CHUNK // RECORD
    with ExitStack() as st:
        ring = k.sbuf(st, "stat_ring", [P, 2, CHUNK])
        recs = k.sbuf(st, "stat_recs", [P, NB, CH, RECS, 6])
        mv = k.sbuf(st, "stat_mv", [P, NB, 2])
        dev = k.sbuf(st, "stat_dev", [P, NB])
        pair = k.sbuf(st, "stat_pair", [P, 2, NB])
        avg = k.sbuf(st, "avg_quarters", [P, P])
        avg_ch = k.sbuf(st, "avg_channels", [P, C])
        taps = k.sbuf(st, "taps", [40, P])
        filt = k.sbuf(st, "filt", [40, C])
        flat = k.sbuf(st, "flat_sb", [HC, 2])
        w_raw = k.sbuf(st, "w_proj_raw", [HC, 2, C])
        chan = k.sbuf(st, "chan_stats", [HC, 2, 2, NB])
        var = k.sbuf(st, "chan_var", [HC, 2, NB])
        root = k.sbuf(st, "chan_root", [HC, 2, NB])
        ratio = k.sbuf(st, "chan_ratio", [HC, 2, NB])
        scale = k.sbuf(st, "chan_scale", [HC, 2, NB])
        ps_mean = k.psum(st, "ps_mean", [P, NB])
        ps_chan = k.psum(st, "ps_chan", [HC, 2, 2, NB])
        ps_gain = k.psum(st, "ps_gain", [P, C])
        ps_bias = k.psum(st, "ps_bias", [HC, 2, NB])
        loaded = [k.sem("s0_loaded0"), k.sem("s0_loaded1")]
        chunk_done = k.sem("s0_chunk_done")
        consts = k.sem("s0_consts")
        chain = k.sem("s0_chain")
        mm = k.sem("s0_mm")
        rooted = k.sem("s0_rooted")
        xv = d["x"].rearrange("n (g c) h w -> n (g c h w)", g=GROUPS).rearrange(
            "n (p j f) -> n j p f", p=P, f=CHUNK)
        N_CONST = 8
        ROOT_AT = 6

        with nc.Block() as block:

            @block.sync
            def _(sp):
                for dst, src in ((avg[:, :], d["c_group_x"]), (avg_ch[:, :], d["c_group_x_ch"]),
                                 (taps[:, :], d["c_taps"]), (filt[:, :], d["filter_t"]),
                                 (flat[:, :], d["flat_gain"]),
                                 (w_raw[:, :, :], d["w_proj_t"].rearrange("(h c) o -> c h o", h=2)),
                                 (k.basis[:, :, :], d["c_basis"]), (k.avg_c[:, :], d["c_group_ch"])):
                    sp.dma_start(dst, src).then_inc(consts, 16)
                with sp.Fori(0, NB) as n:
                    with sp.Fori(0, CH // 2) as j:
                        for slot in range(2):
                            sp.wait_ge(chunk_done, n * CH + j * 2 + slot + 1)
                            sp.dma_start(ring[:, slot, :], xv[n, j * 2 + slot]).then_inc(loaded[slot], 16)

            @block.vector
            def _(dve):
                dve.sem_inc(chunk_done, 2)
                with dve.Fori(0, NB) as n:
                    with dve.Fori(0, CH // 2) as j:
                        for slot in range(2):
                            dve.wait_ge(loaded[slot], n * (CH // 2 * 16) + j * 16 + 16)
                            for r in range(RECS):
                                ins = nc.vector.bn_stats(recs[:, n, j * 2 + slot, r, :],
                                                         ring[:, slot, r * RECORD:(r + 1) * RECORD])
                            ins.then_inc(chunk_done, 1)
                dve.wait_ge(chunk_done, 2 + NB * CH)
                done = [0]

                def link(ins):
                    done[0] += 1
                    ins.then_inc(chain, 1)
                    dve.wait_ge(chain, done[0])

                for n in range(NB):
                    link(nc.vector.bn_aggr(mv[:, n, :], recs[:, n].rearrange("p a b c -> p (a b c)")))
                dve.wait_ge(mm, 1)
                link(nc.vector.tensor_tensor(dev[:, :], mv[:, :, 0], ps_mean[:, :], ALU.subtract))
                nc.vector.tensor_copy(pair[:, 0, :], ps_mean[:, :])
                link(nc.vector.tensor_tensor(dev[:, :], dev[:, :], dev[:, :], ALU.mult))
                link(nc.vector.tensor_tensor(pair[:, 1, :], dev[:, :], mv[:, :, 1], ALU.add))
                dve.wait_ge(mm, 2)
                link(nc.vector.tensor_copy(chan[:, :, :, :], ps_chan[:, :, :, :]))
                link(nc.vector.tensor_scalar(var[:, :, :], chan[:, :, 1, :], EPS, None, ALU.add))
                link(nc.vector.tensor_copy(k.gain[:, :], ps_gain[:, :]))
                dve.wait_ge(rooted, 1)
                link(nc.vector.reciprocal(ratio[:, :, :], root[:, :, :]))
                link(nc.vector.tensor_tensor(ratio[:, :, :], ratio[:, :, :], var[:, :, :], ALU.mult))
                link(nc.vector.tensor_tensor(root[:, :, :], root[:, :, :], ratio[:, :, :], ALU.add))
                link(nc.vector.tensor_scalar(root[:, :, :], root[:, :, :], 0.5, None, ALU.mult))
                link(nc.vector.reciprocal(scale[:, :, :], root[:, :, :]))
                for n in range(NB):
                    for h in range(2):
                        ins = nc.vector.tensor_scalar(k.w_proj[:, n, h, :], w_raw[:, h, :],
                                                      scale[:, h, n:n + 1], None, ALU.mult)
                link(ins)
                dve.wait_ge(mm, 3)
                for h in range(2):
                    ins = nc.vector.tensor_scalar(k.bias0[:, h, :], ps_bias[:, h, :], flat[:, h:h + 1], -1.0,
                                                  ALU.mult, ALU.mult)
                link(ins)

            @block.scalar
            def _(act):
                act.wait_ge(chain, NB + 5)
                nc.scalar.activation(root[:, :, :], var[:, :, :], ACT.Sqrt).then_inc(rooted, 1)

            @block.tensor
            def _(pe):
                pe.wait_ge(consts, 16 * N_CONST)
                pe.wait_ge(chain, NB)
                nc.tensor.matmul(ps_mean[:, :], avg[:, :], mv[:, :, 0], start=True, stop=True).then_inc(mm, 1)
                pe.wait_ge(chain, NB + 3)
                nc.tensor.matmul(ps_gain[:, :], taps[:, :], filt[:, :], start=True, stop=True)
                for h in range(2):
                    ins = nc.tensor.matmul(ps_chan[:, h, :, :], avg_ch[:, h * HC:(h + 1) * HC],
                                           pair[:, :, :], start=True, stop=True)
                ins.then_inc(mm, 1)
                pe.wait_ge(chain, NB + 12)
                for ho in range(2):
                    for n in range(NB):
                        for h in range(2):
                            ins = nc.tensor.matmul(ps_bias[:, ho, n:n + 1], k.w_proj[:, n, h, ho * HC:(ho + 1) * HC],
                                                   chan[:, h, 0, n:n + 1], start=(h == 0), stop=(h == 1))
                ins.then_inc(mm, 1)


def patch_filter(k):
    nc, d = k.nc, k.dram
    GPS = QUADS
    GPI = STRIPES * GPS
    TQ = TILES // QUADS
    COLS = TQ * 16
    with ExitStack() as st:
        xt = k.sbuf(st, "x_rows", [HC, 2, 2, SPX])
        xr = k.sbuf(st, "x_tiles", [HC, 2, 2, SPX])
        y_sb = k.sbuf(st, "y_px", [P, 2, TQ * C])
        z_sb = k.sbuf(st, "z_basis", [P, 2, TQ * C])
        y_ps = k.psum(st, "ps_y", [P, 2, 512])
        z_ps = k.psum(st, "ps_z", [P, 2, 512])
        o_ps = k.psum(st, "ps_o", [HC, 2, 512])
        loaded = [k.sem("p_loaded0"), k.sem("p_loaded1")]
        stored = [k.sem("p_stored0"), k.sem("p_stored1")]
        tiled = k.sem("p_tiled")
        y_made, y_moved = k.sem("p_y_made"), k.sem("p_y_moved")
        z_made, z_moved = k.sem("p_z_made"), k.sem("p_z_moved")
        o_made, o_added = k.sem("p_o_made"), k.sem("p_o_added")
        measured = k.sem("p_measured")
        Y_MOVED, Z_MADE, Z_MOVED, O_MADE, O_ADDED = 1, 2, 1, 2, 1
        xv = d["x"].rearrange("n (h c) (s r) w -> n s c h (r w)", h=2, r=PATCH)
        x1v = d["x1"].rearrange("n (h c) (s r) w -> n s c h (r w)", h=2, r=PATCH)

        with nc.Block() as block:

            @block.sync
            def _(sp):
                for slot in range(2):
                    sp.dma_start(xt[:, slot, :, :], xv[0, slot]).then_inc(loaded[slot], 16)

                def turn(n, i, load_n, load_i):
                    for slot in range(2):
                        sp.wait_ge(o_added, n * GPI + i * (2 * GPS) + slot * GPS + GPS + O_ADDED)
                        sp.dma_start(x1v[n, i * 2 + slot], xt[:, slot, :, :]).then_inc(stored[slot], 16)
                        if load_n is not None:
                            sp.wait_ge(measured, n * GPI + i * (2 * GPS) + slot * GPS + GPS)
                            sp.wait_ge(stored[slot], n * (8 * STRIPES) + i * 16 + 16)
                            sp.dma_start(xt[:, slot, :, :], xv[load_n, load_i * 2 + slot]).then_inc(loaded[slot], 16)

                LAST = STRIPES // 2 - 1
                with sp.Fori(0, NB - 1) as n:
                    with sp.Fori(0, LAST) as i:
                        turn(n, i, n, i + 1)
                    turn(n, LAST, n + 1, 0)
                with sp.Fori(0, LAST) as i:
                    turn(NB - 1, i, NB - 1, i + 1)
                turn(NB - 1, LAST, None, None)
                for slot in range(2):
                    sp.wait_ge(stored[slot], NB * 8 * STRIPES)

            @block.tensor
            def _(pe):
                pe.sem_inc(z_made, Z_MADE)
                pe.sem_inc(o_made, O_MADE)

                def to_pixels(n, g, at):
                    slot, q = at // GPS % 2, at % GPS
                    pe.wait_ge(tiled, n * GPI + g + 1)
                    pe.wait_ge(y_moved, n * GPI + g + Y_MOVED)
                    for t in range(TQ):
                        for h in range(2):
                            px = (q * TQ + t) * P
                            ins = nc.tensor.matmul(y_ps[:, t // 2, t % 2 * C:(t % 2 + 1) * C],
                                                   xr[:, slot, h, px:px + P], k.w_proj[:, n, h, :],
                                                   start=(h == 0), stop=(h == 1))
                    ins.then_inc(y_made, 1)

                def to_basis(n, g, at):
                    pe.wait_ge(y_moved, n * GPI + g + 1 + Y_MOVED)
                    pe.wait_ge(z_moved, n * GPI + g + Z_MOVED)
                    for j in range(2):
                        w = TQ * C // 2
                        ins = nc.tensor.matmul(z_ps[:, j, 0:w], k.basis[:, 0, :], y_sb[:, at % 2, j * w:(j + 1) * w],
                                               start=True, stop=True)
                    ins.then_inc(z_made, 1)

                def to_channels(n, g, at):
                    pe.wait_ge(z_moved, n * GPI + g + 1 + Z_MOVED)
                    pe.wait_ge(o_added, n * GPI + g + O_ADDED)
                    for h in range(2):
                        rows = o_ps[:, h, :].rearrange("o (y t x) -> o y t x", y=PATCH, t=TQ)
                        for t in range(TQ):
                            at_z = t * C + h * HC
                            ins = nc.tensor.matmul(rows[:, :, t, :], z_sb[:, at % 2, at_z:at_z + HC],
                                                   k.basis[:, 1, :], start=True, stop=True)
                    ins.then_inc(o_made, 1)

                with pe.Fori(0, NB) as n:
                    to_pixels(n, 0, 0)
                    to_pixels(n, 1, 1)
                    to_basis(n, 0, 0)
                    with pe.Fori(0, STRIPES // 2 - 1) as i:
                        for at in range(2 * GPS):
                            g = i * (2 * GPS) + at
                            to_pixels(n, g + 2, at + 2)
                            to_basis(n, g + 1, at + 1)
                            to_channels(n, g, at)
                    for at in range(2 * GPS):
                        g = GPI - 2 * GPS + at
                        if g + 2 < GPI:
                            to_pixels(n, g + 2, at + 2)
                        if g + 1 < GPI:
                            to_basis(n, g + 1, at + 1)
                        to_channels(n, g, at)

            @block.scalar
            def _(act):
                act.sem_inc(y_moved, Y_MOVED)
                halves = [[v[:, slot, h, :] for h in range(2)] for slot in range(2) for v in (xt, xr)]

                def to_tiles(slot, q):
                    for h in range(2):
                        rows, tiles = halves[2 * slot][h], halves[2 * slot + 1][h]
                        ins = nc.scalar.activation(
                            tiles.rearrange("c (t y x) -> c t y x", t=TILES, y=PATCH)[:, q * TQ:(q + 1) * TQ],
                            rows.rearrange("c (y t x) -> c t y x", t=TILES, y=PATCH)[:, q * TQ:(q + 1) * TQ],
                            ACT.Copy)
                    ins.then_inc(tiled, 1)

                def turn(i, last):
                    for at in range(2 * GPS):
                        slot, q = at // GPS, at % GPS
                        act.wait_ge(y_made, i * (2 * GPS) + at + 1)
                        act.wait_ge(z_made, i * (2 * GPS) + at - 1 + Z_MADE)
                        nc.scalar.activation(y_sb[:, at % 2, :].rearrange("p (b f) -> p b f", b=2),
                                             y_ps[:, :, 0:TQ * C // 2], ACT.Copy).then_inc(y_moved, 1)
                        if q >= GPS // 2 and not (last and slot == 1):
                            if q == GPS // 2:
                                act.wait_ge(loaded[1 - slot], (i + slot) * 16 + 16)
                            for piece in (2 * q - GPS, 2 * q - GPS + 1):
                                to_tiles(1 - slot, piece)

                act.wait_ge(loaded[0], 16)
                for q in range(GPS):
                    to_tiles(0, q)
                with act.Fori(0, NB * STRIPES // 2 - 1) as i:
                    turn(i, False)
                turn(NB * STRIPES // 2 - 1, True)

            @block.vector
            def _(dve):
                dve.sem_inc(z_moved, Z_MOVED)
                dve.sem_inc(o_added, O_ADDED)

                def times_filter(n, g, at):
                    dve.wait_ge(z_made, n * GPI + g + 1 + Z_MADE)
                    dve.wait_ge(o_made, n * GPI + g - 1 + O_MADE)
                    half = z_ps[:, :, 0:TQ * C // 2].rearrange("p b (t o) -> p b t o", o=C)
                    nc.vector.tensor_tensor(z_sb[:, at % 2, :].rearrange("p (b t o) -> p b t o", b=2, o=C), half,
                                            bcast(bcast(k.gain[:, :], 1, 2), 1, 2), ALU.mult).then_inc(z_moved, 1)

                def add_x(n, g, at):
                    dve.wait_ge(o_made, n * GPI + g + 1 + O_MADE)
                    slot, q = at // GPS % 2, at % GPS
                    for h in range(2):
                        part = xt[:, slot, h, :].rearrange("c (y x) -> c y x", y=PATCH)[:, :, q * COLS:(q + 1) * COLS]
                        ins = nc.vector.scalar_tensor_tensor(
                            out=part, in0=o_ps[:, h, :].rearrange("c (y x) -> c y x", y=PATCH),
                            scalar=k.bias0[:, h, bass.ds(n, 1)], in1=part, op0=ALU.add, op1=ALU.add)
                    ins.then_inc(o_added, 1)

                def measure(n, g, at, stripe):
                    slot, q = at // GPS % 2, at % GPS
                    dve.wait_ge(o_added, n * GPI + g + 1 + O_ADDED)
                    for h in range(2):
                        part = xt[:, slot, h, :].rearrange("c (y x) -> c y x", y=PATCH)[:, :, q * COLS:(q + 1) * COLS]
                        ins = nc.vector.bn_stats(k.x1_recs[:, n, h, stripe, q, :], part)
                    ins.then_inc(measured, 1)

                with dve.Fori(0, NB) as n:
                    times_filter(n, 0, 0)
                    with dve.Fori(0, STRIPES // 2 - 1) as i:
                        for at in range(2 * GPS):
                            g = i * (2 * GPS) + at
                            times_filter(n, g + 1, at + 1)
                            add_x(n, g, at)
                            measure(n, g, at, i * 2 + at // GPS)
                    for at in range(2 * GPS):
                        g = GPI - 2 * GPS + at
                        if g + 1 < GPI:
                            times_filter(n, g + 1, at + 1)
                        add_x(n, g, at)
                        measure(n, g, at, STRIPES - 2 + at // GPS)



TAPS = 9
IN_BLOCK, FROM_PREV, FROM_NEXT, OUTER, ANGLE, FOURIER = 0, 3, 6, 9, 10, 11
B_INNER, B_OUTER, B_ANGLE, B_FOURIER, B_FOURIER_TURNS = range(5)


def mixing_weights(k):
    nc, d = k.nc, k.dram
    N_SMALL = TAPS + 3
    with ExitStack() as st:
        conv_s = k.sbuf(st, "mag_s_w_sb", [C0, C0, TAPS])
        mag_t = k.sbuf(st, "mag_w_sb", [C0, C0])
        mag_f = k.sbuf(st, "mag_f_w_sb", [C0, C0])
        first = k.sbuf(st, "conv1_first", [C0, C])
        conv0_t = k.sbuf(st, "conv0_sb", [C0, C0])
        bias_in = k.sbuf(st, "bias_in", [C0, 5])
        conv0_b = k.sbuf(st, "conv0_b_sb", [1, C0])
        small = k.sbuf(st, "small", [C0, N_SMALL, C0])
        bias = k.sbuf(st, "bias_small", [C0, 5])
        rep = k.sbuf(st, "rep", [C0, P])
        band = k.sbuf(st, "band", [P, 5, BLK])
        wide = k.sbuf(st, "wide", [P, N_SMALL, C0])
        part = k.sbuf(st, "part", [P, P])
        zero = k.sbuf(st, "zero_row", [P, SIDE])
        ones = k.sbuf(st, "ones_rows", [HC, P])
        mv = k.sbuf(st, "x1_mv", [HC, NB, 2, 2])
        dev = k.sbuf(st, "x1_dev", [HC, NB, 2])
        spread = k.sbuf(st, "x1_spread", [HC, NB, 2])
        mean = k.sbuf(st, "x1_mean", [HC, NB, 2])
        var = k.sbuf(st, "x1_var", [HC, NB, 2])
        root = k.sbuf(st, "x1_root", [HC, NB, 2])
        ratio = k.sbuf(st, "x1_ratio", [HC, NB, 2])
        scale = k.sbuf(st, "x1_scale", [HC, NB, 2])
        minus = k.sbuf(st, "x1_minus_mean", [HC, NB, 2, P])
        w_raw = k.sbuf(st, "conv1_raw", [HC, 2, C1])
        ps_small = k.psum(st, "ps_small", [C0, TAPS + 1, C0])
        ps_b = k.psum(st, "ps_small_b", [C0, 2])
        ps_w0 = k.psum(st, "ps_w0", [HC, 2, C0])
        ps_wide = k.psum(st, "ps_wide", [P, N_SMALL, C0])
        ps_wb = k.psum(st, "ps_wide_b", [P, 5])
        ps_mean = k.psum(st, "ps_x1_mean", [HC, NB, 2])
        ps_var = k.psum(st, "ps_x1_var", [HC, NB, 2])
        ps_row = k.psum(st, "ps_bias_row", [P, NB, C1])
        consts, cleared, chain, mm, rooted = (k.sem("m_" + s) for s in
                                              ("consts", "cleared", "chain", "products", "rooted"))
        placed = k.sem("m_placed")
        col = lambda name: d[name].rearrange("(p o) -> p o", o=1)
        loads = [(conv_s[:, :, :], d["mag_s_w"].rearrange("m c a b -> m c (a b)")),
                 (mag_t[:, :], d["mag_w_t"]), (mag_f[:, :], d["mag_f_w"]), (first[:, :], d["conv1_w"][0:C0, :]),
                 (conv0_t[:, :], d["conv_0_w_t"]), (conv0_b[:, :], d["conv_0_b"].rearrange("(o p) -> o p", o=1)),
                 (small[:, TAPS + 1, :], d["pha_w_t"]), (small[:, TAPS + 2, :], d["conv_1_w_t"]),
                 (rep[:, :], d["c_rep"]), (band[:, :, :], d["c_band"]),
                 (w_raw[:, :, C0:C1], d["conv1_w_t"].rearrange("(h c) o -> c h o", h=2)[:, :, C0:C1])]
        loads += [(bias_in[:, i:i + 1], col(b)) for i, b in
                  enumerate(("mag_s_b", "mag_f_b", "mag_b", "pha_b", "conv_1_b"))]
        mark = {}

        with nc.Block() as block:

            @block.sync
            def _(sp):
                for dst, src in loads:
                    sp.dma_start(dst, src).then_inc(consts, 16)
                sp.wait_ge(cleared, 1)
                for s in range(2):
                    sp.dma_start(k.mix2[s * C1:(s + 1) * C1, :, s * 64:(s + 1) * 64],
                                 d["conv2_w_t"].rearrange("k (q o) -> k q o", q=3)).then_inc(placed, 16)
                sp.wait_ge(placed, 32)

            @block.vector
            def _(dve):
                done = [0]

                def link(ins, name=None):
                    done[0] += 1
                    ins.then_inc(chain, 1)
                    dve.wait_ge(chain, done[0])
                    if name:
                        mark[name] = done[0]

                v = nc.vector
                v.memset(k.mix2[:, :, :], 0.0).then_inc(cleared, 1)
                link(v.memset(ones[:, :], 1.0))
                link(v.memset(zero[:, :], 0.0))
                for n in range(NB):
                    for h in range(2):
                        ins = v.bn_aggr(mv[:, n, h, :], k.x1_recs[:, n, h].rearrange("c s q r -> c (s q r)"))
                link(ins, "means")
                dve.wait_ge(mm, 1)
                link(v.tensor_copy(mean[:, :, :], ps_mean[:, :, :]))
                link(v.tensor_tensor(dev[:, :, :], mv[:, :, :, 0], mean[:, :, :], ALU.subtract))
                link(v.tensor_tensor(dev[:, :, :], dev[:, :, :], dev[:, :, :], ALU.mult))
                link(v.tensor_tensor(spread[:, :, :], dev[:, :, :], mv[:, :, :, 1], ALU.add), "spread")
                dve.wait_ge(mm, 2)
                link(v.tensor_scalar(var[:, :, :], ps_var[:, :, :], EPS, None, ALU.add), "var")
                dve.wait_ge(rooted, 1)
                link(v.reciprocal(ratio[:, :, :], root[:, :, :]))
                link(v.tensor_tensor(ratio[:, :, :], ratio[:, :, :], var[:, :, :], ALU.mult))
                link(v.tensor_tensor(root[:, :, :], root[:, :, :], ratio[:, :, :], ALU.add))
                link(v.tensor_scalar(root[:, :, :], root[:, :, :], 0.5, None, ALU.mult))
                link(v.reciprocal(scale[:, :, :], root[:, :, :]))
                dve.wait_ge(consts, 16 * len(loads))
                dve.wait_ge(mm, 3)
                link(v.tensor_copy(w_raw[:, :, 0:C0], ps_w0[:, :, :]))
                link(v.tensor_copy(small[:, 0:TAPS + 1, :], ps_small[:, :, :]))
                for i in range(2):
                    link(v.tensor_scalar(bias[:, i:i + 1], ps_b[:, i:i + 1], bias_in[:, 2:3], None, ALU.add))
                link(v.tensor_scalar(bias[:, B_ANGLE:B_ANGLE + 1], bias_in[:, 3:4], 1 / (2 * math.pi), None, ALU.mult))
                link(v.tensor_copy(bias[:, B_FOURIER:B_FOURIER + 1], bias_in[:, 4:5]))
                link(v.tensor_scalar(bias[:, B_FOURIER_TURNS:5], bias_in[:, 4:5], 1 / (2 * math.pi), None, ALU.mult),
                     "small")
                for n in range(NB):
                    for h in range(2):
                        v.tensor_scalar(k.w1[:, n, h, :], w_raw[:, h, :], scale[:, n, h:h + 1], None, ALU.mult)
                        ins = v.tensor_scalar(minus[:, n, h, :], ones[:, :], mean[:, n, h:h + 1], -1.0,
                                              ALU.mult, ALU.mult)
                link(ins, "w1")
                dve.wait_ge(mm, 4)
                link(v.tensor_copy(wide[:, :, :], ps_wide[:, :, :]))
                link(v.tensor_copy(k.mix_bias[:, :], ps_wb[:, :]))

                def place(dst, small_index, band_index):
                    return v.tensor_tensor(dst.rearrange("p (u o) -> p u o", u=BLK),
                                           bcast(wide[:, small_index, :], 1, BLK),
                                           bcast(band[:, band_index, :], 2, C0), ALU.mult)

                for dy in range(3):
                    link(place(k.mix[:, IN_BLOCK + dy, :], dy * 3 + 1, 1))
                    for dx in (0, 2):
                        link(place(part[:, :], dy * 3 + dx, dx))
                        link(v.tensor_tensor(k.mix[:, IN_BLOCK + dy, :], k.mix[:, IN_BLOCK + dy, :], part[:, :],
                                             ALU.add))
                    link(place(k.mix[:, FROM_PREV + dy, :], dy * 3 + 0, 3))
                    link(place(k.mix[:, FROM_NEXT + dy, :], dy * 3 + 2, 4))
                for i in range(3):
                    link(place(k.mix[:, OUTER + i, :], TAPS + i, 1))
                for row, (a, b) in enumerate(((B_INNER, B_OUTER), (B_OUTER, B_OUTER))):
                    link(v.tensor_scalar(k.bias_row[:, row, :], zero[:, :], k.mix_bias[:, b:b + 1], None, ALU.add))
                    link(v.tensor_scalar(k.bias_row[:, row, LO:HI], zero[:, LO:HI], k.mix_bias[:, a:a + 1], None,
                                         ALU.add))
                dve.wait_ge(mm, 5)
                link(v.tensor_copy(k.conv1_row[:, :, :], ps_row[:, :, :]))

            @block.scalar
            def _(act):
                act.wait_ge(chain, mark["var"])
                nc.scalar.activation(root[:, :, :], var[:, :, :], ACT.Sqrt).then_inc(rooted, 1)

            @block.tensor
            def _(pe):
                t = nc.tensor
                pe.wait_ge(chain, mark["means"])
                t.matmul(ps_mean[:, :, :], k.avg_c[:, :], mv[:, :, :, 0], start=True, stop=True).then_inc(mm, 1)
                pe.wait_ge(chain, mark["spread"])
                t.matmul(ps_var[:, :, :], k.avg_c[:, :], spread[:, :, :], start=True, stop=True).then_inc(mm, 1)
                pe.wait_ge(consts, 16 * len(loads))
                for tap in range(TAPS):
                    t.matmul(ps_small[:, tap, :], conv_s[:, :, tap], mag_t[:, :], start=True, stop=True)
                t.matmul(ps_small[:, TAPS, :], mag_f[:, :], mag_t[:, :], start=True, stop=True)
                t.matmul(ps_b[:, :], mag_t[:, :], bias_in[:, 0:2], start=True, stop=True)
                for h in range(2):
                    ins = t.matmul(ps_w0[:, h, :], first[:, h * HC:(h + 1) * HC], conv0_t[:, :], start=True, stop=True)
                ins.then_inc(mm, 1)
                pe.wait_ge(chain, mark["small"])
                t.matmul(ps_wide[:, :, :], rep[:, :], small[:, :, :], start=True, stop=True)
                t.matmul(ps_wb[:, :], rep[:, :], bias[:, :], start=True, stop=True).then_inc(mm, 1)
                pe.wait_ge(chain, mark["w1"])
                for n in range(NB):
                    t.matmul(ps_row[:, n, :], minus[:, n, 0, :], k.w1[:, n, 0, :], start=True, stop=False)
                    t.matmul(ps_row[:, n, 0:C0], ones[0:1, :], conv0_b[:, :], start=False, stop=False)
                    ins = t.matmul(ps_row[:, n, :], minus[:, n, 1, :], k.w1[:, n, 1, :], start=False, stop=True)
                ins.then_inc(mm, 1)


def row_transforms(k):
    nc, d = k.nc, k.dram
    F, R = 2 * SIDE, 2 * NFREQ
    with ExitStack() as st:
        xt = k.sbuf(st, "x1_rows", [HC, 2, 2, SPX])
        s_sb = k.sbuf(st, "conv1_px", [P, 2, 2, 3, P])
        frft = k.sbuf(st, "frft_rows", [P, 2, 3 * SIDE])
        rfft = k.sbuf(st, "rfft_rows", [P, 2, R])
        eye = k.sbuf(st, "eye_rows", [P, P])
        f_sb = k.sbuf(st, "rows_f", [P, 2, F])
        r_sb = k.sbuf(st, "rows_r", [P, 2, R])
        i_sb = k.sbuf(st, "rows_i", [P, 2, SIDE])
        s_ps = k.psum(st, "ps_conv1", [P, 2, 512])
        f_ps = k.psum(st, "ps_rows_f", [P, F])
        r_ps = k.psum(st, "ps_rows_r", [P, 512])
        i_ps = k.psum(st, "ps_rows_i", [P, 512])
        consts = k.sem("r_consts")
        loaded = [k.sem("r_loaded0"), k.sem("r_loaded1")]
        stored = [[k.sem(f"r_stored_{b}{slot}") for slot in range(2)] for b in "fri"]
        conv_made, conv_moved, rows_made, rows_moved = (
            k.sem("r_" + s) for s in ("conv_made", "conv_moved", "rows_made", "rows_moved"))
        CONV_MADE, CONV_MOVED, ROWS_MADE, ROWS_MOVED, STORED = 2, 1, 2, 1, 16
        x1v = d["x1"].rearrange("n (h c) (s r) w -> n s c h (r w)", h=2, r=PATCH)
        out_v = [d[name].rearrange("n (s y) c f -> n s (y c) f", y=PATCH) for name in ("t_f", "t_r", "r_0")]
        stage = [(f_sb, f_ps, F), (r_sb, r_ps, R), (i_sb, i_ps, SIDE)]

        with nc.Block() as block:

            @block.sync
            def _(sp):
                sp.dma_start(frft[:, :, :], d["c_frft"]).then_inc(consts, 16)
                sp.dma_start(rfft[:, :, :], d["c_rfft"]).then_inc(consts, 16)
                sp.dma_start(eye[:, :], d["c_eye"]).then_inc(consts, 16)
                with sp.Fori(0, NB) as n:
                    with sp.Fori(0, STRIPES // 2) as i:
                        for slot in range(2):
                            sp.wait_ge(conv_made, n * STRIPES + i * 2 + slot - 1 + CONV_MADE)
                            sp.dma_start(xt[:, slot, :, :], x1v[n, i * 2 + slot]).then_inc(loaded[slot], 16)

            @block.tensor
            def _(pe):
                pe.sem_inc(conv_made, CONV_MADE)
                pe.sem_inc(rows_made, ROWS_MADE)

                def conv1(n, i, slot):
                    s = n * STRIPES + i * 2 + slot
                    pe.wait_ge(loaded[slot], n * (8 * STRIPES) + i * 16 + 16)
                    pe.wait_ge(conv_moved, s + CONV_MOVED)
                    for y in range(PATCH):
                        for xh in range(2):
                            for h in range(2):
                                px = y * SIDE + xh * P
                                ins = nc.tensor.matmul(s_ps[:, xh, y * C1:(y + 1) * C1], xt[:, slot, h, px:px + P],
                                                       k.w1[:, n, h, :], start=(h == 0), stop=(h == 1))
                    ins.then_inc(conv_made, 1)

                def rows(n, i, slot):
                    s = n * STRIPES + i * 2 + slot
                    pe.wait_ge(conv_moved, s + 1 + CONV_MOVED)
                    pe.wait_ge(rows_moved, s + ROWS_MOVED)
                    for xh in range(2):
                        nc.tensor.matmul(f_ps[:, :], s_sb[:, slot, xh, 1, :], frft[:, xh, SIDE:3 * SIDE],
                                         start=(xh == 0), stop=(xh == 1))
                    for xh in range(2):
                        nc.tensor.matmul(r_ps[:, 0:R], s_sb[:, slot, xh, 2, :], rfft[:, xh, :],
                                         start=(xh == 0), stop=(xh == 1))
                    for xh in range(2):
                        ins = nc.tensor.transpose(i_ps[:, xh * P:(xh + 1) * P], s_sb[:, slot, xh, 0, :], eye[:, :])
                    ins.then_inc(rows_made, 1)

                pe.wait_ge(consts, 48)
                with pe.Fori(0, NB) as n:
                    conv1(n, 0, 0)
                    with pe.Fori(0, STRIPES // 2 - 1) as i:
                        conv1(n, i, 1)
                        rows(n, i, 0)
                        conv1(n, i + 1, 0)
                        rows(n, i, 1)
                    conv1(n, STRIPES // 2 - 1, 1)
                    rows(n, STRIPES // 2 - 1, 0)
                    rows(n, STRIPES // 2 - 1, 1)

            @block.vector
            def _(dve):
                dve.sem_inc(conv_moved, CONV_MOVED)
                with dve.Fori(0, NB) as n:
                    with dve.Fori(0, STRIPES // 2) as i:
                        for slot in range(2):
                            s = n * STRIPES + i * 2 + slot
                            dve.wait_ge(conv_made, s + 1 + CONV_MADE)
                            dve.wait_ge(rows_made, s - 1 + ROWS_MADE)
                            for xh in range(2):
                                ins = nc.vector.tensor_tensor(
                                    s_sb[:, slot, xh].rearrange("p b (y c) -> p b y c", y=PATCH),
                                    s_ps[:, xh, 0:PATCH * C1].rearrange("p (y b c) -> p b y c", y=PATCH, b=3),
                                    bcast(k.conv1_row[:, n, :].rearrange("p (b c) -> p b c", b=3), 2, PATCH), ALU.add)
                            ins.then_inc(conv_moved, 1)

            @block.scalar
            def _(act):
                act.sem_inc(rows_moved, ROWS_MOVED)
                for b in range(3):
                    for slot in range(2):
                        act.sem_inc(stored[b][slot], STORED)
                with act.Fori(0, NB) as n:
                    with act.Fori(0, STRIPES // 2) as i:
                        for slot in range(2):
                            s = n * STRIPES + i * 2 + slot
                            act.wait_ge(rows_made, s + 1 + ROWS_MADE)
                            for b, (sb, ps, w) in enumerate(stage):
                                act.wait_ge(stored[b][slot], n * (8 * STRIPES) + i * 16 + STORED)
                                ins = nc.scalar.activation(sb[:, slot, :], ps[:, 0:w], ACT.Copy)
                            ins.then_inc(rows_moved, 1)
                            act.wait_ge(rows_moved, s + 1 + ROWS_MOVED)
                            for b, (sb, ps, w) in enumerate(stage):
                                act.dma_start(out_v[b][n, i * 2 + slot], sb[:, slot, :]).then_inc(stored[b][slot], 16)
                for b in range(3):
                    for slot in range(2):
                        act.wait_ge(stored[b][slot], NB * 8 * STRIPES + STORED)


N_F = 33
N_R = 17
F_RUNS = ((0, 5, 0), (5, 23, LO), (28, 4, HI), (32, 1, SIDE - BLK))
R_LAST = NFREQ - BLK
IN_LAST = HI - (LO + 22 * BLK)
OUT_LAST = LO - 4 * BLK
MAGIC = 1.5 * 2.0**23
TURN = 6.2831850
FRFT, DFT, IFRFT, IRFFT = range(4)


def paired(eng, first, count, body):
    if count > 2:
        with eng.Fori(0, count // 2) as i:
            for p in range(2):
                body(i * 2 + p, (first + p) % 2)
    else:
        for j in range(count // 2 * 2):
            body(j, (first + j) % 2)
    if count % 2:
        body(count - 1, (first + count - 1) % 2)


def spectra(k):
    nc, d = k.nc, k.dram
    COLS_A_F, COLS_A_R, COLS_C_F, COLS_C_R = 0, N_F, N_F + N_R, N_F + N_R + STRIPES
    N_COLS = N_F + N_R + 2 * STRIPES
    N_ROOT = N_F + N_R + STRIPES
    N_MIX = N_F + N_R
    OUT_C_F, OUT_C_R = N_MIX, N_MIX + STRIPES
    N_OUT = N_MIX + 2 * STRIPES
    assert N_COLS % 2 == 0 and N_MIX % 2 == 0 and N_OUT % 2 == 0
    with ExitStack() as st:
        plane = k.sbuf(st, "plane", [P, 2, C0 * 2 * SIDE])
        mag = k.sbuf(st, "magnitude", [P, N_F, SIDE])
        half_tan = k.sbuf(st, "half_tangent", [P, N_F, SIDE])
        left = k.sbuf(st, "real_negative", [P, N_F, SIDE], U8)
        frft = k.sbuf(st, "frft_cols", [P, 2, 3 * SIDE])
        ifrft = k.sbuf(st, "ifrft_cols", [P, 2, 3 * SIDE])
        dft = k.sbuf(st, "dft_cols", [P, 2, 5 * SIDE])
        irfft = k.sbuf(st, "irfft_rows", [P, 2, SIDE])
        eye = k.sbuf(st, "eye_cols", [P, P])
        quarter = k.sbuf(st, "quarter_turn", [P, 1])
        ones = k.sbuf(st, "ones_channels", [P, C0])
        cols = k.sbuf(st, "cols", [P, 2, 2, 2, P])
        squares = k.sbuf(st, "squares", [P, 2, 2 * SIDE])
        angle = k.sbuf(st, "half_angle", [P, 2, SIDE])
        work = k.sbuf(st, "work", [P, SIDE])
        phase = k.sbuf(st, "phase", [P, 2, SIDE])
        mixed_mag = k.sbuf(st, "mixed_mag", [P, SIDE])
        turns = k.sbuf(st, "turns", [P, SIDE])
        whole = k.sbuf(st, "whole_turns", [P, SIDE])
        rest = k.sbuf(st, "rest", [P, 2, 2, SIDE])
        wave = k.sbuf(st, "wave", [P, 2, 2, SIDE])
        flip = k.sbuf(st, "flipped", [P, 2, 2, 2, P])
        out_sb = k.sbuf(st, "out_rows", [P, 2, 2 * SIDE])
        cols_ps = k.psum(st, "ps_cols", [P, 2, 2 * SIDE])
        mix_ps = k.psum(st, "ps_mix", [P, 2, 2, SIDE])
        flip_ps = k.psum(st, "ps_flip", [P, 2, 2, P])
        back_ps = k.psum(st, "ps_back", [P, 2 * SIDE])
        S = lambda name: k.sem("c_" + name)
        consts, plane_in, quartered = S("consts"), S("plane_in"), S("quarter")
        staged, made, squared, added, rooted, freed, chain_a = (
            S(n) for n in ("staged", "made", "squared", "added", "rooted", "freed", "chain_a"))
        angled, phased, mixed, turned, waved, formed, flipped, spread, backed, rowed = (
            S(n) for n in ("angled", "phased", "mixed", "turned", "waved", "formed", "flipped", "spread",
                           "backed", "rowed"))
        chain_phase, chain_turn = S("chain_phase"), S("chain_turn")
        sent = [S("sent0"), S("sent1")]
        nyquist_sent = S("nyquist_sent")
        MADE, FREED, PHASED, MIXED, TURNED, WAVED, FLIPPED, BACKED = (2,) * 8
        SPREAD, ROWED, FORMED = 1, 1, 1
        SENT = 16
        plane_f = lambda h: plane[:, h, :].rearrange("p (c r w) -> p r w c", c=C0, r=2)
        plane_r = lambda h: plane[:, h, 0:C0 * 2 * NFREQ].rearrange("p (c r w) -> p r w c", c=C0, r=2)
        flat_f = d["w_f"].rearrange("n u c f -> n (u c) f")
        flat_r = d["w_r"].rearrange("n u c f -> n (u c) f")
        rows_f = d["r_f"].rearrange("n y c x -> n (y c) x")
        rows_r = d["r_r"].rearrange("n y c x -> n (y c) x")

        half_rows = lambda name, n: d[name][n].rearrange("(h u) c f -> u h (c f)", h=2)

        def sent_before(n, out, j, slot):
            p = (slot - out) % 2
            return n * (N_OUT // 2 * 16) + (j - p) * 8 + (out + p - slot) // 2 * 16 + SENT

        with nc.Block() as block:

            @block.sync
            def _(sp):
                for dst, src in ((frft, "c_frft"), (ifrft, "c_ifrft"), (dft, "c_dft"), (irfft, "c_irfft")):
                    sp.dma_start(dst[:, :, :], d[src]).then_inc(consts, 16)
                sp.dma_start(eye[:, :], d["c_eye"]).then_inc(consts, 16)
                for slot in range(2):
                    sp.sem_inc(sent[slot], SENT)

                def rows_out(n, out, j, slot, dst, lo=0, hi=P):
                    sp.dma_start(dst, out_sb[lo:hi, slot, 0:dst.shape[-1]]).then_inc(sent[slot], 16)

                with sp.Fori(0, NB) as n:
                    sp.wait_ge(made, n * N_COLS + MADE)
                    sp.dma_start(plane[:, :, :], half_rows("t_f", n)).then_inc(plane_in, 16)
                    sp.wait_ge(made, n * N_COLS + COLS_A_R + MADE)
                    sp.dma_start(plane[:, :, 0:C0 * 2 * NFREQ], half_rows("t_r", n)).then_inc(plane_in, 16)
                    for first, count, u0 in F_RUNS:
                        def store(j, slot, first=first, u0=u0, lo=0, hi=P):
                            b = first + j
                            sp.wait_ge(rowed, n * N_MIX + b + 1 + ROWED)
                            rows_out(n, b, 0, slot, flat_f[n, bass.ds((u0 + j * BLK) * C0 + lo, hi - lo), :], lo, hi)

                        if first == 0:
                            paired(sp, 0, 4, store)
                            store(4, 0, hi=OUT_LAST * C0)
                        elif first == 5:
                            paired(sp, 5, 22, store)
                            store(22, 1, hi=IN_LAST * C0)
                        elif first == 28:
                            paired(sp, 28, 4, store)
                        else:
                            store(0, 0, lo=(HI + 4 * BLK - u0) * C0)
                    def store_r(j, slot):
                        sp.wait_ge(rowed, n * N_MIX + N_F + j + 1 + ROWED)
                        sp.dma_start(flat_r[n, bass.ds(j * (BLK * C0), P), :], out_sb[:, slot, :]).then_inc(sent[slot], 16)

                    sp.wait_ge(rowed, n * N_MIX + N_F + 1 + ROWED)
                    sp.dma_start(flat_r[n, 0:P, 0:SIDE], out_sb[:, 1, 0:SIDE]).then_inc(sent[1], 16)
                    sp.dma_start(flat_r[n, C0:P, SIDE:2 * SIDE], out_sb[C0:P, 1, SIDE:2 * SIDE]).then_inc(nyquist_sent, 16)
                    paired(sp, N_F + 1, N_R - 2, lambda j, slot: store_r(j + 1, slot))
                    sp.wait_ge(rowed, n * N_MIX + N_MIX + ROWED)
                    sp.dma_start(flat_r[n, 0:C0, SIDE:2 * SIDE], out_sb[P - C0:P, 1, 0:SIDE]).then_inc(sent[1], 16)

                    def store_c(j, slot):
                        sp.wait_ge(rooted, n * N_ROOT + COLS_C_F + j + 1)
                        sp.dma_start(rows_f[n, bass.ds(j * P, P), :], out_sb[:, slot, 0:SIDE]).then_inc(sent[slot], 16)

                    paired(sp, OUT_C_F, STRIPES, store_c)
                    def store_cr(j, slot):
                        sp.wait_ge(freed, n * N_COLS + COLS_C_R + j + 1 + FREED)
                        sp.dma_start(rows_r[n, bass.ds(j * P, P), :], out_sb[:, slot, 0:SIDE]).then_inc(sent[slot], 16)

                    paired(sp, OUT_C_R, STRIPES, store_cr)
                for slot in range(2):
                    sp.wait_ge(sent[slot], NB * (N_OUT // 2) * 16 + SENT)

            @block.gpsimd
            def _(pool):
                nc.gpsimd.memset(quarter[:, :], math.pi / 2).then_inc(quartered, 1)
                nc.gpsimd.memset(ones[:, :], 1.0).then_inc(quartered, 1)
                pool.wait_ge(quartered, 2)

                def stage(n, number, slot, source, halves, pos, planes):
                    pool.wait_ge(plane_in, n * 64 + planes * 16)
                    pool.wait_ge(made, n * N_COLS + number - 1 + MADE)
                    for h in range(halves):
                        dst = cols[:, slot, h, :, :].rearrange("p r (u c) -> p r u c", c=C0)
                        src = source(h)[:, :, bass.ds(pos, BLK), :]
                        if h == 0:
                            ins = nc.gpsimd.tensor_tensor(dst, src, bcast(bcast(ones[:, :], 1, BLK), 1, 2), ALU.mult)
                        else:
                            ins = nc.gpsimd.tensor_copy(dst, src)
                    ins.then_inc(staged, 1)

                with pool.Fori(0, NB) as n:
                    for first, count, u0 in F_RUNS:
                        paired(pool, first, count, lambda j, slot: stage(n, first + j, slot, plane_f, 2, u0 + j * BLK, 1))
                    paired(pool, COLS_A_R, 16, lambda j, slot: stage(n, COLS_A_R + j, slot, plane_r, 2, j * BLK, 2))
                    stage(n, COLS_A_R + 16, 1, plane_r, 2, R_LAST, 2)
                    paired(pool, COLS_C_F, STRIPES, lambda j, slot: stage(n, COLS_C_F + j, slot, plane_f, 2, j * BLK, 3))
                    paired(pool, COLS_C_R, STRIPES, lambda j, slot: stage(n, COLS_C_R + j, slot, plane_f, 1, j * BLK, 4))

            @block.tensor
            def _(pe):
                mm = nc.tensor.matmul
                for s, credit in ((made, MADE), (mixed, MIXED), (flipped, FLIPPED), (backed, BACKED)):
                    pe.sem_inc(s, credit)
                wide = {FRFT: (frft, SIDE, 0), DFT: (dft, 3 * SIDE, 2 * SIDE), IFRFT: (ifrft, SIDE, 0)}

                def columns(n, number, slot, transform):
                    pe.wait_ge(staged, n * N_COLS + number + 1)
                    pe.wait_ge(freed, n * N_COLS + number - 1 + FREED)
                    if transform == IRFFT:
                        for ri in range(2):
                            ins = mm(cols_ps[:, slot, 0:SIDE], cols[:, slot, 0, ri, :], irfft[:, ri, :],
                                     start=(ri == 0), stop=(ri == 1))
                    else:
                        table, re, im = wide[transform]
                        for h in range(2):
                            for ri, at in enumerate((re, im)):
                                ins = mm(cols_ps[:, slot, :], cols[:, slot, h, ri, :],
                                         table[:, h, at:at + 2 * SIDE], start=(h + ri == 0), stop=(h + ri == 2))
                    ins.then_inc(made, 1)

                def mix(n, b, slot, kind, base=0):
                    pe.wait_ge(phased, n * N_MIX + base + b + 1 + PHASED)
                    pe.wait_ge(turned, n * N_MIX + base + b - 1 + TURNED)
                    out = lambda lo, hi: mix_ps[:, slot, 0, lo:hi]
                    if kind in ("first", "inner", "last"):
                        rows = IN_LAST * C0 if kind == "last" else P
                        terms = [(rows, IN_BLOCK, b)]
                        if kind != "first":
                            terms.append((P, FROM_PREV, b - 1))
                        if kind != "last":
                            terms.append((P, FROM_NEXT, b + 1))
                        todo = [(r, w + dy, at, dy) for r, w, at in terms for dy in (1, 0, 2)]
                        for i, (r, w, at, dy) in enumerate(todo):
                            lo, hi = LO + (dy == 0), HI - (dy == 2)
                            mm(out(lo, hi), k.mix[0:r, w, :], mag[0:r, at, lo + dy - 1:hi + dy - 1],
                               start=(i == 0), stop=(i == len(todo) - 1))
                        for lo, hi in ((0, LO), (HI, SIDE)):
                            mm(out(lo, hi), k.mix[:, OUTER, :], mag[:, b, lo:hi], start=True, stop=True)
                    else:
                        w = FOURIER if kind == "fourier" else OUTER
                        mm(out(0, SIDE), k.mix[:, w, :], mag[:, b, :], start=True, stop=True)
                    w = FOURIER if kind == "fourier" else ANGLE
                    mm(mix_ps[:, slot, 1, :], k.mix[:, w, :], phase[:, slot, :],
                       start=True, stop=True).then_inc(mixed, 1)

                def back(n, b, slot, table, re, im):
                    pe.wait_ge(formed, n * N_MIX + b + 1 + FORMED)
                    pe.wait_ge(spread, n * N_MIX + b + SPREAD)
                    for h in range(2):
                        for ri in range(2):
                            ins = nc.tensor.transpose(flip_ps[:, h, ri, :], wave[:, slot, ri, h * P:(h + 1) * P],
                                                      eye[:, :])
                    ins.then_inc(flipped, 1)
                    pe.wait_ge(spread, n * N_MIX + b + 1 + SPREAD)
                    pe.wait_ge(rowed, n * N_MIX + b + ROWED)
                    for h in range(2):
                        for ri, at in enumerate((re, im)):
                            ins = mm(back_ps[:, :], flip[:, slot, h, ri, :], table[:, h, at:at + 2 * SIDE],
                                     start=(h + ri == 0), stop=(h + ri == 2))
                    ins.then_inc(backed, 1)

                pe.wait_ge(consts, 80)
                with pe.Fori(0, NB) as n:
                    for first, count, u0 in F_RUNS:
                        paired(pe, first, count, lambda j, slot: columns(n, first + j, slot, FRFT))

                    def step_f(b, slot, kind):
                        mix(n, b, slot, kind)
                        back(n, b - 1, 1 - slot, ifrft, SIDE, 0)

                    mix(n, 0, 0, "outer")
                    paired(pe, 1, 4, lambda j, slot: step_f(j + 1, slot, "outer"))
                    step_f(5, 1, "first")
                    paired(pe, 6, 21, lambda j, slot: step_f(j + 6, slot, "inner"))
                    step_f(27, 1, "last")
                    paired(pe, 28, 5, lambda j, slot: step_f(j + 28, slot, "outer"))
                    back(n, N_F - 1, 0, ifrft, SIDE, 0)

                    paired(pe, COLS_A_R, 16, lambda j, slot: columns(n, COLS_A_R + j, slot, DFT))
                    columns(n, COLS_A_R + 16, 1, DFT)
                    mix(n, 0, 1, "fourier", base=N_F)

                    def step_r(j, slot):
                        mix(n, j, slot, "fourier", base=N_F)
                        back(n, N_F + j - 1, 1 - slot, dft, SIDE, 0)

                    paired(pe, N_F + 1, 15, lambda j, slot: step_r(j + 1, slot))
                    step_r(16, 1)
                    back(n, N_F + 16, 1, dft, SIDE, 0)

                    paired(pe, COLS_C_F, STRIPES, lambda j, slot: columns(n, COLS_C_F + j, slot, IFRFT))
                    paired(pe, COLS_C_R, STRIPES, lambda j, slot: columns(n, COLS_C_R + j, slot, IRFFT))

            @block.scalar
            def _(act):
                a = nc.scalar.activation
                for s, credit in ((waved, WAVED), (spread, SPREAD), (rowed, ROWED)):
                    act.sem_inc(s, credit)
                act.wait_ge(quartered, 2)

                def root(n, number, slot, dst, out=None, j=None):
                    act.wait_ge(made, n * N_COLS + number + 1 + MADE)
                    a(squares[:, slot, :], cols_ps[:, slot, :], ACT.Square).then_inc(squared, 1)
                    if out is not None:
                        act.wait_ge(sent[slot], sent_before(n, out, j, slot))
                    act.wait_ge(added, n * N_ROOT + number + 1)
                    if out is None:
                        a(squares[:, slot, SIDE:2 * SIDE], cols_ps[:, slot, 0:SIDE], ACT.Abs)
                    a(dst, squares[:, slot, 0:SIDE], ACT.Sqrt).then_inc(rooted, 1)

                def half_angle(n, b, slot, base):
                    act.wait_ge(phased, n * N_MIX + base + b - 1 + PHASED)
                    a(angle[:, slot, :], half_tan[:, b, :], ACT.Arctan).then_inc(angled, 1)

                def waves(n, b, slot):
                    act.wait_ge(turned, n * N_MIX + b + 1 + TURNED)
                    act.wait_ge(flipped, n * N_MIX + b - 1 + FLIPPED)
                    a(wave[:, slot, 0, :], rest[:, slot, 1, :], ACT.Sin, scale=-TURN, bias=quarter[:, :])
                    a(wave[:, slot, 1, :], rest[:, slot, 0, :], ACT.Sin, scale=TURN).then_inc(waved, 1)

                def move_flip(n, b, slot):
                    act.wait_ge(flipped, n * N_MIX + b + 1 + FLIPPED)
                    act.wait_ge(backed, n * N_MIX + b - 1 + BACKED)
                    a(flip[:, slot, :, :, :], flip_ps[:, :, :, :], ACT.Copy).then_inc(spread, 1)

                def move_back(n, base, j, slot, nyquist=False):
                    act.wait_ge(backed, n * N_MIX + base + j + 1 + BACKED)
                    act.wait_ge(sent[slot], sent_before(n, base, j, slot))
                    if nyquist:
                        act.wait_ge(nyquist_sent, n * 16 + 16)
                    a(out_sb[:, slot, :], back_ps[:, :], ACT.Copy).then_inc(rowed, 1)

                with act.Fori(0, NB) as n:
                    for first, count, u0 in F_RUNS:
                        paired(act, first, count,
                               lambda j, slot: root(n, first + j, slot, mag[:, first + j, :]))

                    def turn_f(b, slot, ahead=True):
                        waves(n, b, slot)
                        move_back(n, 0, b - 1, 1 - slot)
                        if ahead:
                            half_angle(n, b + 2, slot, 0)
                        move_flip(n, b, slot)

                    act.wait_ge(freed, n * N_COLS + COLS_A_R + FREED)
                    half_angle(n, 0, 0, 0)
                    half_angle(n, 1, 1, 0)
                    waves(n, 0, 0)
                    half_angle(n, 2, 0, 0)
                    move_flip(n, 0, 0)
                    paired(act, 1, 30, lambda j, slot: turn_f(j + 1, slot))
                    turn_f(31, 1, False)
                    turn_f(32, 0, False)
                    move_back(n, 0, 32, 0)

                    paired(act, COLS_A_R, 16, lambda j, slot: root(n, COLS_A_R + j, slot, mag[:, j, :]))
                    root(n, COLS_A_R + 16, 1, mag[:, 16, :])
                    act.wait_ge(freed, n * N_COLS + COLS_C_F + FREED)
                    for slot in range(2):
                        act.wait_ge(sent[slot], n * (N_OUT // 2 * 16) + (N_F + 1 - slot) // 2 * 16 + SENT)
                    act.dma_start(plane[:, :, :], half_rows("w_f", n)).then_inc(plane_in, 16)

                    def turn_r(j, slot, ahead=True, nyquist=True):
                        waves(n, N_F + j, slot)
                        move_back(n, N_F, j - 1, 1 - slot, nyquist=nyquist)
                        if ahead:
                            half_angle(n, j + 2, slot, N_F)
                        move_flip(n, N_F + j, slot)

                    half_angle(n, 0, 1, N_F)
                    half_angle(n, 1, 0, N_F)
                    waves(n, N_F, 1)
                    half_angle(n, 2, 1, N_F)
                    move_flip(n, N_F, 1)
                    turn_r(1, 0, nyquist=False)
                    paired(act, N_F + 2, 12, lambda j, slot: turn_r(j + 2, slot))
                    turn_r(14, 1, ahead=True)
                    turn_r(15, 0, ahead=False)
                    turn_r(16, 1, ahead=False)
                    move_back(n, N_F, 16, 1, nyquist=True)

                    paired(act, COLS_C_F, STRIPES,
                           lambda j, slot: root(n, COLS_C_F + j, slot, out_sb[:, slot, 0:SIDE], out=OUT_C_F, j=j))
                    for slot in range(2):
                        act.wait_ge(sent[slot], n * (N_OUT // 2 * 16) + N_MIX // 2 * 16 + SENT)
                    act.wait_ge(nyquist_sent, n * 16 + 16)
                    act.dma_start(plane[:, 0, :], d["w_r"][n].rearrange("u c f -> u (c f)")).then_inc(plane_in, 16)

            @block.vector
            def _(dve):
                v = nc.vector
                for s, credit in ((freed, FREED), (phased, PHASED), (turned, TURNED), (formed, FORMED)):
                    dve.sem_inc(s, credit)

                def polar(n, number, slot, b):
                    dve.wait_ge(squared, n * N_ROOT + number + 1)
                    v.tensor_tensor(squares[:, slot, 0:SIDE], squares[:, slot, 0:SIDE],
                                    squares[:, slot, SIDE:2 * SIDE], ALU.add).then_inc(added, 1)
                    dve.wait_ge(rooted, n * N_ROOT + number + 1)
                    dve.wait_ge(freed, n * N_COLS + number + FREED)
                    link = n * (2 * N_MIX) + number * 2
                    v.tensor_scalar(left[:, b, :], cols_ps[:, slot, 0:SIDE], 0.0, None, ALU.is_lt)
                    v.scalar_tensor_tensor(out=work[:, :], in0=squares[:, slot, SIDE:2 * SIDE], scalar=1e-30,
                                           in1=mag[:, b, :], op0=ALU.max, op1=ALU.add).then_inc(chain_a, 1)
                    dve.wait_ge(chain_a, link + 1)
                    v.reciprocal(work[:, :], work[:, :]).then_inc(chain_a, 1)
                    dve.wait_ge(chain_a, link + 2)
                    v.tensor_tensor(half_tan[:, b, :], cols_ps[:, slot, SIDE:2 * SIDE], work[:, :],
                                    ALU.mult).then_inc(freed, 1)

                def full_angle(n, b, slot, base):
                    dve.wait_ge(angled, n * N_MIX + base + b + 1)
                    dve.wait_ge(mixed, n * N_MIX + base + b - 1 + MIXED)
                    dve.wait_ge(phased, n * N_MIX + base + b + PHASED)
                    link = (n * N_MIX + base + b) * 3
                    v.tensor_scalar(work[:, :], half_tan[:, b, :], 0.0, 2 * math.pi, ALU.is_ge,
                                    ALU.mult).then_inc(chain_phase, 1)
                    dve.wait_ge(chain_phase, link + 1)
                    v.scalar_tensor_tensor(out=work[:, :], in0=angle[:, slot, :], scalar=-4.0, in1=work[:, :],
                                           op0=ALU.mult, op1=ALU.add).then_inc(chain_phase, 1)
                    dve.wait_ge(chain_phase, link + 2)
                    v.scalar_tensor_tensor(out=work[:, :], in0=work[:, :], scalar=-math.pi, in1=left[:, b, :],
                                           op0=ALU.add, op1=ALU.mult).then_inc(chain_phase, 1)
                    dve.wait_ge(chain_phase, link + 3)
                    v.scalar_tensor_tensor(out=phase[:, slot, :], in0=angle[:, slot, :], scalar=2.0,
                                           in1=work[:, :], op0=ALU.mult, op1=ALU.add).then_inc(phased, 1)

                def turn_of(n, b, slot, row):
                    dve.wait_ge(mixed, n * N_MIX + b + 1 + MIXED)
                    dve.wait_ge(waved, n * N_MIX + b - 1 + WAVED)
                    dve.wait_ge(formed, n * N_MIX + b + FORMED)
                    link = (n * N_MIX + b) * 3
                    if row is None:
                        v.tensor_scalar(mixed_mag[:, :], mix_ps[:, slot, 0, :],
                                        k.mix_bias[:, B_FOURIER:B_FOURIER + 1], None, ALU.add)
                        shift = k.mix_bias[:, B_FOURIER_TURNS:B_FOURIER_TURNS + 1]
                    else:
                        v.tensor_tensor(mixed_mag[:, :], mix_ps[:, slot, 0, :], k.bias_row[:, row, :], ALU.add)
                        shift = k.mix_bias[:, B_ANGLE:B_ANGLE + 1]
                    v.tensor_scalar(turns[:, :], mix_ps[:, slot, 1, :], 1 / (2 * math.pi), shift, ALU.mult,
                                    ALU.add).then_inc(chain_turn, 1)
                    dve.wait_ge(chain_turn, link + 1)
                    v.tensor_scalar(whole[:, :], turns[:, :], MAGIC, MAGIC, ALU.add,
                                    ALU.subtract).then_inc(chain_turn, 1)
                    dve.wait_ge(chain_turn, link + 2)
                    v.tensor_tensor(rest[:, slot, 0, :], turns[:, :], whole[:, :],
                                    ALU.subtract).then_inc(chain_turn, 1)
                    dve.wait_ge(chain_turn, link + 3)
                    v.scalar_tensor_tensor(out=rest[:, slot, 1, :], in0=rest[:, slot, 0, :], scalar=-1.0,
                                           in1=rest[:, slot, 0, :], op0=ALU.mult, op1=ALU.max).then_inc(turned, 1)

                def form(n, b, slot):
                    dve.wait_ge(waved, n * N_MIX + b + 1 + WAVED)
                    v.tensor_tensor(wave[:, slot, :, :], wave[:, slot, :, :], bcast(mixed_mag[:, :], 1, 2),
                                    ALU.mult).then_inc(formed, 1)

                def turn(n, base, j, slot, row, ahead=True):
                    turn_of(n, base + j, slot, row)
                    form(n, base + j, slot)
                    if ahead:
                        full_angle(n, j + 2, slot, base)

                with dve.Fori(0, NB) as n:
                    for first, count, u0 in F_RUNS:
                        paired(dve, first, count, lambda j, slot: polar(n, first + j, slot, first + j))
                    full_angle(n, 0, 0, 0)
                    full_angle(n, 1, 1, 0)
                    paired(dve, 0, 5, lambda j, slot: turn(n, 0, j, slot, 1))
                    paired(dve, 5, 23, lambda j, slot: turn(n, 0, j + 5, slot, 0))
                    paired(dve, 28, 3, lambda j, slot: turn(n, 0, j + 28, slot, 1))
                    turn(n, 0, 31, 1, 1, ahead=False)
                    turn(n, 0, 32, 0, 1, ahead=False)

                    paired(dve, COLS_A_R, 16, lambda j, slot: polar(n, COLS_A_R + j, slot, j))
                    polar(n, COLS_A_R + 16, 1, 16)
                    full_angle(n, 0, 1, N_F)
                    full_angle(n, 1, 0, N_F)
                    paired(dve, N_F, 14, lambda j, slot: turn(n, N_F, j, slot, None))
                    turn(n, N_F, 14, 1, None, ahead=True)
                    turn(n, N_F, 15, 0, None, ahead=False)
                    turn(n, N_F, 16, 1, None, ahead=False)

                    def sum_squares(j, slot):
                        dve.wait_ge(squared, n * N_ROOT + COLS_C_F + j + 1)
                        v.tensor_tensor(squares[:, slot, 0:SIDE], squares[:, slot, 0:SIDE],
                                        squares[:, slot, SIDE:2 * SIDE], ALU.add).then_inc(added, 1)
                        dve.wait_ge(added, n * N_ROOT + COLS_C_F + j + 1)
                        dve.sem_inc(freed, 1)

                    paired(dve, COLS_C_F, STRIPES, sum_squares)

                    def move_row(j, slot):
                        dve.wait_ge(made, n * N_COLS + COLS_C_R + j + 1 + MADE)
                        dve.wait_ge(sent[slot], sent_before(n, OUT_C_R, j, slot))
                        v.tensor_copy(out_sb[:, slot, 0:SIDE], cols_ps[:, slot, 0:SIDE]).then_inc(freed, 1)

                    paired(dve, COLS_C_R, STRIPES, move_row)


def output(k):
    nc, d = k.nc, k.dram
    SLOTS, HALF = 4, SPX // 2
    with ExitStack() as st:
        br = k.sbuf(st, "branches", [2 * C1, SLOTS, HALF])
        xt = k.sbuf(st, "x1_out", [P, SLOTS, 3, HALF])
        ps = k.psum(st, "ps_out", [P, 2, 3, 512])
        loaded = [k.sem(f"o_loaded{s}") for s in range(SLOTS)]
        stored = [k.sem(f"o_stored{s}") for s in range(SLOTS)]
        made, summed = k.sem("o_made"), k.sem("o_summed")
        SUMMED, MADE, STORED = 2, 2 * SLOTS, 32
        view = lambda name: d[name].rearrange("n (q o) (s r) w -> n s o q (r w)", q=3, r=PATCH // 2)
        x1v, outv = view("x1"), view("out")
        brv = [d[name].rearrange("n (s r) c w -> n s c r w", r=PATCH // 2) for name in ("r_0", "r_f", "r_r")]

        with nc.Block() as block:

            @block.sync
            def _(sp):
                with sp.Fori(0, NB) as n:
                    with sp.Fori(0, STRIPES // SLOTS) as i:
                        for slot in range(SLOTS):
                            s = i * SLOTS + slot
                            sp.wait_ge(made, n * (2 * STRIPES) + s * 2 + 2 - 2 * SLOTS + MADE)
                            sp.wait_ge(stored[slot], n * (STRIPES // SLOTS * 32) + i * 32 + STORED)
                            for half in range(2):
                                for b in range(3):
                                    at = half * C1 + b * C0
                                    sp.dma_start(br[at:at + C0, slot, :].rearrange("c (r w) -> c r w", w=SIDE),
                                                 brv[b][n, s * 2 + half]).then_inc(loaded[slot], 16)
                                sp.dma_start(xt[half * 64:(half + 1) * 64, slot, :, :],
                                             x1v[n, s * 2 + half]).then_inc(loaded[slot], 16)

            @block.tensor
            def _(pe):
                pe.sem_inc(made, MADE)
                with pe.Fori(0, NB) as n:
                    with pe.Fori(0, STRIPES // SLOTS) as i:
                        for slot in range(SLOTS):
                            s = i * SLOTS + slot
                            pe.wait_ge(loaded[slot], n * (STRIPES // SLOTS * 128) + i * 128 + 128)
                            for part in range(2):
                                pe.wait_ge(summed, n * (2 * STRIPES) + s * 2 + part - 1 + SUMMED)
                                for q in range(3):
                                    ins = nc.tensor.matmul(ps[:, part, q, :], k.mix2[:, q, :],
                                                           br[:, slot, part * 512:(part + 1) * 512],
                                                           start=True, stop=True)
                                ins.then_inc(made, 1)

            @block.vector
            def _(dve):
                dve.sem_inc(summed, SUMMED)
                with dve.Fori(0, NB) as n:
                    with dve.Fori(0, STRIPES // SLOTS) as i:
                        for slot in range(SLOTS):
                            s = i * SLOTS + slot
                            for part in range(2):
                                dve.wait_ge(made, n * (2 * STRIPES) + s * 2 + part + 1 + MADE)
                                x1p = xt[:, slot, :, part * 512:(part + 1) * 512]
                                nc.vector.tensor_tensor(x1p, ps[:, part, :, :], x1p, ALU.add).then_inc(summed, 1)

            @block.scalar
            def _(act):
                for slot in range(SLOTS):
                    act.sem_inc(stored[slot], STORED)
                with act.Fori(0, NB) as n:
                    with act.Fori(0, STRIPES // SLOTS) as i:
                        for slot in range(SLOTS):
                            s = i * SLOTS + slot
                            act.wait_ge(summed, n * (2 * STRIPES) + s * 2 + 2 + SUMMED)
                            for half in range(2):
                                act.dma_start(outv[n, s * 2 + half],
                                              xt[half * 64:(half + 1) * 64, slot, :, :]).then_inc(stored[slot], 16)
                for slot in range(SLOTS):
                    act.wait_ge(stored[slot], NB * (STRIPES // SLOTS) * 32 + STORED)


def build(nc, dram):
    k = Core(nc, dram)
    with k.stack:
        k.mix2 = k.sbuf(k.stack, "mix_conv2", [2 * C1, 3, P])
        k.mix = k.sbuf(k.stack, "mix", [P, TAPS + 3, P])
        k.mix_bias = k.sbuf(k.stack, "mix_bias", [P, 5])
        k.bias_row = k.sbuf(k.stack, "bias_row", [P, 2, SIDE])
        k.w1 = k.sbuf(k.stack, "w_conv1", [HC, NB, 2, C1])
        k.conv1_row = k.sbuf(k.stack, "conv1_row", [P, NB, C1])
        with ExitStack() as first:
            k.basis = k.sbuf(first, "basis", [P, 2, P])
            k.avg_c = k.sbuf(first, "avg_group", [HC, HC])
            k.gain = k.sbuf(first, "gain", [P, C])
            k.w_proj = k.sbuf(first, "w_proj", [HC, NB, 2, C])
            k.bias0 = k.sbuf(first, "bias0", [HC, 2, NB])
            k.x1_recs = k.sbuf(first, "x1_recs", [HC, NB, 2, STRIPES, QUADS, 6])
            input_statistics(k)
            patch_filter(k)
            mixing_weights(k)
        row_transforms(k)
        spectra(k)
        output(k)


def layout(inputs):
    flat = inputs["L0_conv_fft_filter"].reshape(C, -1)
    w = {n[8:]: a for n, a in inputs.items() if n.startswith("L1_conv_")}
    arrays = {
        "x": inputs["x"], "filter_t": flat.T, "flat_gain": flat[:, 0].reshape(2, HC).T,
        "w_proj_t": inputs["L0_conv_w_proj"].T, "conv1_w": w["conv1_w"], "conv1_w_t": w["conv1_w"].T,
        "mag_s_w": w["mag_s_w"], "mag_w_t": w["mag_w"].T, "mag_f_w": w["mag_f_w"], "pha_w_t": w["pha_w"].T,
        "conv_0_w_t": w["conv_0_w"].T, "conv_1_w_t": w["conv_1_w"].T, "conv2_w_t": w["conv2_w"].T,
    }
    for name in ("mag_s_b", "mag_f_b", "mag_b", "pha_b", "conv_0_b", "conv_1_b"):
        arrays[name] = w[name]
    return arrays


SCRATCH = {
    "x1": [NB, C, SIDE, SIDE],
    "t_f": [NB, SIDE, C0, 2 * SIDE], "t_r": [NB, SIDE, C0, 2 * NFREQ],
    "w_f": [NB, SIDE, C0, 2 * SIDE], "w_r": [NB, P, C0, 2 * SIDE],
    "r_0": [NB, SIDE, C0, SIDE], "r_f": [NB, SIDE, C0, SIDE], "r_r": [NB, SIDE, C0, SIDE],
}


def kernel(**inputs):
    import concourse.bacc as bacc
    from concourse.bass_utils import run_bass_kernel_spmd

    nc = bacc.Bacc("TRN2", target_bir_lowering=False, num_devices=1)
    inputs = {n: np.asarray(a) for n, a in inputs.items()}
    arrays = {n: np.ascontiguousarray(a) for n, a in {**layout(inputs), **constants()}.items()}
    dram = {n: nc.dram_tensor(n, a.shape, mybir.dt.from_np(a.dtype), kind="ExternalInput").ap()
            for n, a in arrays.items()}
    for n, shape in SCRATCH.items():
        dram[n] = nc.dram_tensor(n, shape, F32).ap()
    dram["out"] = nc.dram_tensor("out", [NB, C, SIDE, SIDE], F32, kind="ExternalOutput").ap()
    build(nc, dram)
    result = run_bass_kernel_spmd(nc, [arrays], core_ids=[0])
    return result.results[0]["out"]
```

```python
import math
from contextlib import ExitStack

import numpy as np

import concourse.bass as bass
from concourse import mybir

ALU = mybir.AluOpType
ACT = mybir.ActivationFunctionType
F32 = mybir.dt.float32
U8 = mybir.dt.uint8

P = 128
NB, C, SIDE = 4, 192, 256
HC = C // 2
PATCH = 8
STRIPES = SIDE // PATCH
SPX = PATCH * SIDE
TILES = SPX // P
QUADS = 4
GROUPS, GC = 32, C // 32
C0 = 16
C1 = 48
BLK = 8
NFREQ = SIDE // 2 + 1
LO = (SIDE - int(SIDE * math.cos(math.pi / 4))) // 2
HI = LO + int(SIDE * math.cos(math.pi / 4))
EPS = 1e-5


def frft_matrix():
    n_ = SIDE
    a = 0.5
    alpha = a * math.pi / 2
    n = np.arange(-2 * n_ + 2, 2 * n_ - 1).astype(np.float64)
    chirp = np.exp(-1j * math.pi / n_ * math.tan(alpha / 2) / 4 * n**2)
    c = math.pi / n_ / math.sin(alpha) / 4
    mid = slice(n_ - 1, 3 * n_ - 2)
    sinc = np.sinc((np.arange(2 * n_ - 1)[:, None] - 2 * np.arange(n_)[None, :]) / 2.0)
    outs = n[mid][::2]
    kern = np.exp(1j * c * (outs[:, None] - n[mid][None, :]) ** 2) * math.sqrt(c / math.pi)
    return np.exp(-1j * (1 - a) * math.pi / 4) * (
        chirp[mid][::2][:, None] * kern * chirp[mid][None, :] @ sinc)


def centered_ifft_matrix():
    shift = (np.arange(SIDE) + SIDE // 2) % SIDE
    inverse = np.argsort(shift)
    g = np.fft.ifft(np.eye(SIDE)[:, shift], axis=-1) * math.sqrt(SIDE)
    return g[:, inverse].T


def cos_sin(n):
    j = (np.arange(n)[:, None] * np.arange(n)[None, :]) % n
    c, s = np.cos(2 * np.pi * j / n), np.sin(2 * np.pi * j / n)
    quarter = (4 * j) % n == 0
    c[quarter], s[quarter] = np.round(c[quarter]), np.round(s[quarter])
    return c, s


def patch_basis():
    y, x = np.meshgrid(np.arange(PATCH), np.arange(PATCH), indexing="ij")
    basis, taps = [], []
    for kx in range(PATCH // 2 + 1):
        for ky in range(PATCH):
            edge = kx in (0, PATCH // 2)
            if edge and ky > PATCH // 2:
                continue
            phase = 2 * np.pi * ((ky * y + kx * x) % PATCH) / PATCH
            tap = np.zeros((PATCH, PATCH // 2 + 1))
            tap[ky, kx] += 0.5
            tap[(-ky) % PATCH if edge else ky, kx] += 0.5
            alone = edge and ky in (0, PATCH // 2)
            norm = 1 / PATCH if alone else math.sqrt(2) / PATCH
            basis.append(np.cos(phase) * norm)
            taps.append(tap)
            if not alone:
                basis.append(np.sin(phase) * norm)
                taps.append(tap)
    return np.array(basis).reshape(64, 64), np.array(taps).reshape(64, 40).T


def two_rows(m):
    return m.reshape(2, P, -1).transpose(1, 0, 2)


def constants():
    basis, taps = patch_basis()
    d = np.zeros((2, 64, PATCH, 2, PATCH))
    for i in range(2):
        d[i, :, :, i, :] = basis.reshape(64, PATCH, PATCH)
    d = d.reshape(P, P)
    ch, part = np.arange(C), np.arange(P)
    a, b = frft_matrix(), frft_matrix() @ centered_ifft_matrix()
    cos, sin = cos_sin(SIDE)
    windows = lambda m: two_rows(np.concatenate([-m.imag.T, m.real.T, m.imag.T], 1))
    k = np.arange(P)[:, None] * np.arange(SIDE)[None, :] % SIDE
    twice = np.where(np.arange(P) == 0, 1.0, 2.0)[:, None] / SIDE**2
    back_re = twice * cos[1][k]
    back_im = -twice * sin[1][k]
    back_im[0] = (-1.0) ** np.arange(SIDE) / SIDE**2
    u = np.arange(P) // C0
    band = lambda off: (u[:, None] == np.arange(BLK)[None, :] + off).astype(float)
    out = {
        "c_basis": np.stack([d.T, d], 1),
        "c_taps": np.concatenate([taps, taps], 1),
        "c_group_x": (part[:, None] // 4 == part[None, :] // 4) / 4.0,
        "c_group_x_ch": (part[:, None] // 4 == ch[None, :] // GC) / 4.0,
        "c_group_ch": (np.arange(HC)[:, None] // GC == np.arange(HC)[None, :] // GC) / float(GC),
        "c_eye": np.eye(P),
        "c_frft": windows(a),
        "c_ifrft": windows(b),
        "c_dft": two_rows(np.concatenate([-sin, cos, sin, cos, -sin], 1)),
        "c_rfft": two_rows(np.concatenate([cos[:, :NFREQ], -sin[:, :NFREQ]], 1)),
        "c_irfft": np.stack([back_re, back_im], 1),
        "c_rep": np.tile(np.eye(C0), (1, BLK)),
        "c_band": np.stack([band(-1), band(0), band(1),
                            (u[:, None] == BLK - 1) * (np.arange(BLK)[None, :] == 0) * 1.0,
                            (u[:, None] == 0) * (np.arange(BLK)[None, :] == BLK - 1) * 1.0], 1),
    }
    return {n: np.ascontiguousarray(v, dtype=np.float32) for n, v in out.items()}


class Core:

    def __init__(self, nc, dram):
        self.nc, self.dram = nc, dram
        self.stack = ExitStack()

    def sbuf(self, stack, name, shape, dtype=F32):
        return stack.enter_context(self.nc.sbuf_tensor(name, shape, dtype))

    def psum(self, stack, name, shape):
        return stack.enter_context(self.nc.psum_tensor(name, shape, F32))

    def sem(self, name):
        return self.stack.enter_context(self.nc.semaphore(name))


def bcast(ap, axis, n):
    shape = list(ap.shape)
    view = ap.unsqueeze(axis)
    return view.to_broadcast(shape[:axis] + [n] + shape[axis:])


STAT_CHUNK = 3072
RECORD = 512
STAT_CHUNKS = C * SIDE * SIDE // P // STAT_CHUNK
STAT_RECS = STAT_CHUNK // RECORD
CHAIN, AT_MEANS, AT_PAIR, AT_VAR, AT_SCALED = 13, 1, 4, 6, 12


class InputNorm:

    def __init__(self, k, st):
        self.k, self.nc = k, k.nc
        self.ring = k.sbuf(st, "stat_ring", [P, 2, STAT_CHUNK])
        self.recs = k.sbuf(st, "stat_recs", [P, STAT_CHUNKS, STAT_RECS, 6])
        self.mv = k.sbuf(st, "stat_mv", [P, 2])
        self.dev = k.sbuf(st, "stat_dev", [P, 1])
        self.pair = k.sbuf(st, "stat_pair", [P, 2])
        self.avg = k.sbuf(st, "avg_quarters", [P, P])
        self.avg_ch = k.sbuf(st, "avg_channels", [P, C])
        self.w_raw = k.sbuf(st, "w_proj_raw", [HC, 2, C])
        self.w_now = k.sbuf(st, "w_proj_now", [HC, 2, C])
        self.flat = k.sbuf(st, "flat_sb", [HC, 2])
        self.chan = k.sbuf(st, "chan_stats", [HC, 2, 2])
        self.var = k.sbuf(st, "chan_var", [HC, 2])
        self.root = k.sbuf(st, "chan_root", [HC, 2])
        self.ratio = k.sbuf(st, "chan_ratio", [HC, 2])
        self.scale = k.sbuf(st, "chan_scale", [HC, 2])
        ps = k.psum(st, "ps_norm", [P, 512])
        self.ps_mean = ps[:, 0:1]
        self.ps_chan = ps[0:HC, 4:8].rearrange("c (h s) -> c h s", h=2)
        self.ps_bias = ps[0:HC, 8:10]
        self.loaded_first = [k.sem("s_first0"), k.sem("s_first1")]
        self.loaded_ahead = [k.sem("s_ahead0"), k.sem("s_ahead1")]
        self.chunk_done = k.sem("s_chunk_done")
        self.chain, self.mm, self.rooted = k.sem("s_chain"), k.sem("s_products"), k.sem("s_rooted")
        self.xv = k.dram["x"].rearrange("n (g c) h w -> n (g c h w)", g=GROUPS).rearrange(
            "n (p j f) -> n j p f", p=P, f=STAT_CHUNK)

    def load(self, eng, loaded, m, j, slot):
        eng.wait_ge(self.chunk_done, m * STAT_CHUNKS + j + 1)
        eng.dma_start(self.ring[:, slot, :], self.xv[m, j]).then_inc(loaded[slot], 16)

    def wait_chunk(self, dve, loaded, before, j_half, slot):
        dve.wait_ge(loaded[slot], before * (STAT_CHUNKS // 2 * 16) + j_half * 16 + 16)

    def records(self, j, slot, first, last):
        for r in range(first, last):
            ins = self.nc.vector.bn_stats(self.recs[:, j, r, :], self.ring[:, slot, r * RECORD:(r + 1) * RECORD])
        if last == STAT_RECS:
            ins.then_inc(self.chunk_done, 1)

    def link(self, dve, m, number, ins):
        ins.then_inc(self.chain, 1)
        dve.wait_ge(self.chain, m * CHAIN + number)

    def wait_records(self, dve, m):
        dve.wait_ge(self.chunk_done, 2 + m * STAT_CHUNKS + STAT_CHUNKS)

    def quarter_means(self, dve, m):
        self.link(dve, m, AT_MEANS, self.nc.vector.bn_aggr(
            self.mv[:, :], self.recs[:, :, :, :].rearrange("p a b c -> p (a b c)")))

    def pe_group_means(self, pe, m):
        pe.wait_ge(self.chain, m * CHAIN + AT_MEANS)
        self.nc.tensor.matmul(self.ps_mean, self.avg[:, :], self.mv[:, 0:1], start=True,
                              stop=True).then_inc(self.mm, 1)

    def quarter_spread(self, dve, m):
        v = self.nc.vector
        dve.wait_ge(self.mm, m * 3 + 1)
        v.tensor_copy(self.pair[:, 0:1], self.ps_mean)
        self.link(dve, m, 2, v.tensor_tensor(self.dev[:, :], self.mv[:, 0:1], self.ps_mean, ALU.subtract))
        self.link(dve, m, 3, v.tensor_tensor(self.dev[:, :], self.dev[:, :], self.dev[:, :], ALU.mult))
        self.link(dve, m, AT_PAIR, v.tensor_tensor(self.pair[:, 1:2], self.dev[:, :], self.mv[:, 1:2], ALU.add))

    def pe_channels(self, pe, m):
        pe.wait_ge(self.chain, m * CHAIN + AT_PAIR)
        for h in range(2):
            ins = self.nc.tensor.matmul(self.ps_chan[:, h, :], self.avg_ch[:, h * HC:(h + 1) * HC],
                                        self.pair[:, :], start=True, stop=True)
        ins.then_inc(self.mm, 1)

    def channel_var(self, dve, m):
        v = self.nc.vector
        dve.wait_ge(self.mm, m * 3 + 2)
        self.link(dve, m, 5, v.tensor_copy(self.chan[:, :, :], self.ps_chan))
        self.link(dve, m, AT_VAR, v.tensor_scalar(self.var[:, :], self.chan[:, :, 1], EPS, None, ALU.add))

    def act_root(self, act, m):
        act.wait_ge(self.chain, m * CHAIN + AT_VAR)
        self.nc.scalar.activation(self.root[:, :], self.var[:, :], ACT.Sqrt).then_inc(self.rooted, 1)

    def scaled_weights(self, dve, m):
        v, k = self.nc.vector, self.k
        dve.wait_ge(self.rooted, m + 1)
        self.link(dve, m, 7, v.reciprocal(self.ratio[:, :], self.root[:, :]))
        self.link(dve, m, 8, v.tensor_tensor(self.ratio[:, :], self.ratio[:, :], self.var[:, :], ALU.mult))
        self.link(dve, m, 9, v.tensor_tensor(self.root[:, :], self.root[:, :], self.ratio[:, :], ALU.add))
        self.link(dve, m, 10, v.tensor_scalar(self.root[:, :], self.root[:, :], 0.5, None, ALU.mult))
        self.link(dve, m, 11, v.reciprocal(self.scale[:, :], self.root[:, :]))
        for h in range(2):
            v.tensor_scalar(k.w_proj[:, m, h, :], self.w_raw[:, h, :], self.scale[:, h:h + 1], None, ALU.mult)
            ins = v.tensor_scalar(self.w_now[:, h, :], self.w_raw[:, h, :], self.scale[:, h:h + 1], None, ALU.mult)
        self.link(dve, m, AT_SCALED, ins)

    def pe_bias(self, pe, m):
        pe.wait_ge(self.chain, m * CHAIN + AT_SCALED)
        for ho in range(2):
            for h in range(2):
                ins = self.nc.tensor.matmul(self.ps_bias[:, ho:ho + 1], self.w_now[:, h, ho * HC:(ho + 1) * HC],
                                            self.chan[:, h, 0:1], start=(h == 0), stop=(h == 1))
        ins.then_inc(self.mm, 1)

    def bias(self, dve, m):
        dve.wait_ge(self.mm, m * 3 + 3)
        for h in range(2):
            ins = self.nc.vector.tensor_scalar(self.k.bias0[:, h, bass.ds(m, 1)], self.ps_bias[:, h:h + 1],
                                               self.flat[:, h:h + 1], -1.0, ALU.mult, ALU.mult)
        self.link(dve, m, CHAIN, ins)


def first_statistics(k, norm):
    nc, d = k.nc, k.dram
    with ExitStack() as st:
        taps = k.sbuf(st, "taps", [40, P])
        filt = k.sbuf(st, "filt", [40, C])
        ps_gain = k.psum(st, "ps_gain", [P, C])
        consts, gains, gains_moved = k.sem("s_consts"), k.sem("s_gains"), k.sem("s_gains_moved")
        loads = ((taps[:, :], d["c_taps"]), (filt[:, :], d["filter_t"]), (norm.avg[:, :], d["c_group_x"]),
                 (norm.avg_ch[:, :], d["c_group_x_ch"]), (norm.flat[:, :], d["flat_gain"]),
                 (norm.w_raw[:, :, :], d["w_proj_t"].rearrange("(h c) o -> c h o", h=2)),
                 (k.basis[:, :, :], d["c_basis"]), (k.avg_c[:, :], d["c_group_ch"]))

        with nc.Block() as block:

            @block.sync
            def _(sp):
                with sp.Fori(0, STAT_CHUNKS // 2) as j:
                    for slot in range(2):
                        norm.load(sp, norm.loaded_first, 0, j * 2 + slot, slot)

            @block.vector
            def _(dve):
                dve.sem_inc(norm.chunk_done, 2)
                with dve.Fori(0, STAT_CHUNKS // 2) as j:
                    for slot in range(2):
                        norm.wait_chunk(dve, norm.loaded_first, 0, j, slot)
                        norm.records(j * 2 + slot, slot, 0, STAT_RECS)
                norm.wait_records(dve, 0)
                norm.quarter_means(dve, 0)
                norm.quarter_spread(dve, 0)
                norm.channel_var(dve, 0)
                dve.wait_ge(gains, 1)
                nc.vector.tensor_copy(k.gain[:, :], ps_gain[:, :]).then_inc(gains_moved, 1)
                norm.scaled_weights(dve, 0)
                norm.bias(dve, 0)
                dve.wait_ge(gains_moved, 1)

            @block.scalar
            def _(act):
                for dst, src in loads:
                    act.dma_start(dst, src).then_inc(consts, 16)
                norm.act_root(act, 0)

            @block.tensor
            def _(pe):
                pe.wait_ge(consts, 16 * len(loads))
                nc.tensor.matmul(ps_gain[:, :], taps[:, :], filt[:, :], start=True, stop=True).then_inc(gains, 1)
                norm.pe_group_means(pe, 0)
                norm.pe_channels(pe, 0)
                norm.pe_bias(pe, 0)


def patch_filter(k, norm):
    nc, d = k.nc, k.dram
    GPS = QUADS
    GPI = STRIPES * GPS
    TQ = TILES // QUADS
    COLS = TQ * 16
    SLOTS = 4
    BODY = SLOTS * GPS
    with ExitStack() as st:
        xt = k.sbuf(st, "x_rows", [HC, SLOTS, 2, SPX])
        xr = k.sbuf(st, "x_tiles", [HC, 2, 2, SPX])
        y_sb = k.sbuf(st, "y_px", [P, 2, TQ * C])
        z_sb = k.sbuf(st, "z_basis", [P, 2, TQ * C])
        y_ps = k.psum(st, "ps_y", [P, 2, 512])
        z_ps = k.psum(st, "ps_z", [P, 2, 512])
        o_ps = k.psum(st, "ps_o", [HC, 2, 512])
        loaded = [k.sem(f"p_loaded{s}") for s in range(SLOTS)]
        stored = [k.sem(f"p_stored{s}") for s in range(SLOTS)]
        tiled = k.sem("p_tiled")
        y_made, y_moved = k.sem("p_y_made"), k.sem("p_y_moved")
        z_made, z_moved = k.sem("p_z_made"), k.sem("p_z_moved")
        o_made, o_added = k.sem("p_o_made"), k.sem("p_o_added")
        measured = k.sem("p_measured")
        Y_MOVED, Z_MADE, Z_MOVED, O_MADE, O_ADDED = 1, 2, 1, 2, 1
        xv = d["x"].rearrange("n (h c) (s r) w -> n s c h (r w)", h=2, r=PATCH)
        x1v = d["x1"].rearrange("n (h c) (s r) w -> n s c h (r w)", h=2, r=PATCH)

        with nc.Block() as block:

            @block.sync
            def _(sp):
                for slot in range(SLOTS):
                    sp.dma_start(xt[:, slot, :, :], xv[0, slot]).then_inc(loaded[slot], 16)

                def turn(n, i, load_n, load_i):
                    for slot in range(SLOTS):
                        sp.wait_ge(measured, n * GPI + i * BODY + slot * GPS + GPS)
                        sp.dma_start(x1v[n, i * SLOTS + slot], xt[:, slot, :, :]).then_inc(stored[slot], 16)
                        if load_n is not None:
                            sp.wait_ge(stored[slot], n * (STRIPES // SLOTS * 16) + i * 16 + 16)
                            sp.dma_start(xt[:, slot, :, :], xv[load_n, load_i * SLOTS + slot]).then_inc(loaded[slot], 16)

                LAST = STRIPES // SLOTS - 1
                with sp.Fori(0, NB - 1) as n:
                    with sp.Fori(0, LAST) as i:
                        turn(n, i, n, i + 1)
                    turn(n, LAST, n + 1, 0)
                with sp.Fori(0, LAST) as i:
                    turn(NB - 1, i, NB - 1, i + 1)
                turn(NB - 1, LAST, None, None)
                for slot in range(SLOTS):
                    sp.wait_ge(stored[slot], NB * (STRIPES // SLOTS * 16))

            @block.gpsimd
            def _(pool):
                with pool.Fori(1, NB) as m:
                    with pool.Fori(0, STAT_CHUNKS // 2) as j:
                        for slot in range(2):
                            norm.load(pool, norm.loaded_ahead, m, j * 2 + slot, slot)

            @block.tensor
            def _(pe):
                pe.sem_inc(z_made, Z_MADE)
                pe.sem_inc(o_made, O_MADE)

                def to_pixels(n, g, at):
                    slot, q = at // GPS % 2, at % GPS
                    pe.wait_ge(tiled, n * GPI + g + 1)
                    pe.wait_ge(y_moved, n * GPI + g + Y_MOVED)
                    for t in range(TQ):
                        for h in range(2):
                            px = (q * TQ + t) * P
                            ins = nc.tensor.matmul(y_ps[:, t // 2, t % 2 * C:(t % 2 + 1) * C],
                                                   xr[:, slot, h, px:px + P], k.w_proj[:, n, h, :],
                                                   start=(h == 0), stop=(h == 1))
                    ins.then_inc(y_made, 1)

                def to_basis(n, g, at):
                    pe.wait_ge(y_moved, n * GPI + g + 1 + Y_MOVED)
                    pe.wait_ge(z_moved, n * GPI + g + Z_MOVED)
                    for j in range(2):
                        w = TQ * C // 2
                        ins = nc.tensor.matmul(z_ps[:, j, 0:w], k.basis[:, 0, :], y_sb[:, at % 2, j * w:(j + 1) * w],
                                               start=True, stop=True)
                    ins.then_inc(z_made, 1)

                def to_channels(n, g, at):
                    pe.wait_ge(z_moved, n * GPI + g + 1 + Z_MOVED)
                    pe.wait_ge(o_added, n * GPI + g + O_ADDED)
                    for h in range(2):
                        rows = o_ps[:, h, :].rearrange("o (y t x) -> o y t x", y=PATCH, t=TQ)
                        for t in range(TQ):
                            at_z = t * C + h * HC
                            ins = nc.tensor.matmul(rows[:, :, t, :], z_sb[:, at % 2, at_z:at_z + HC],
                                                   k.basis[:, 1, :], start=True, stop=True)
                    ins.then_inc(o_made, 1)

                def image(n, more):
                    pe.wait_ge(norm.chain, n * CHAIN + AT_SCALED)
                    to_pixels(n, 0, 0)
                    to_pixels(n, 1, 1)
                    to_basis(n, 0, 0)
                    with pe.Fori(0, STRIPES // SLOTS - 1) as i:
                        for at in range(BODY):
                            g = i * BODY + at
                            to_pixels(n, g + 2, at + 2)
                            to_basis(n, g + 1, at + 1)
                            to_channels(n, g, at)
                    for at in range(BODY):
                        g = GPI - BODY + at
                        if g + 2 < GPI:
                            to_pixels(n, g + 2, at + 2)
                        if g + 1 < GPI:
                            to_basis(n, g + 1, at + 1)
                        to_channels(n, g, at)
                        if more and at == BODY - 6:
                            norm.pe_group_means(pe, n + 1)
                        if more and at == BODY - 4:
                            norm.pe_channels(pe, n + 1)
                    if more:
                        norm.pe_bias(pe, n + 1)

                with pe.Fori(0, NB - 1) as n:
                    image(n, True)
                image(NB - 1, False)

            @block.scalar
            def _(act):
                act.sem_inc(y_moved, Y_MOVED)
                def to_tiles(slot, q):
                    for h in range(2):
                        ins = nc.scalar.activation(
                            xr[:, slot % 2, h, :].rearrange("c (t y x) -> c t y x", t=TILES, y=PATCH)[:, q * TQ:(q + 1) * TQ],
                            xt[:, slot, h, :].rearrange("c (y t x) -> c t y x", t=TILES, y=PATCH)[:, q * TQ:(q + 1) * TQ],
                            ACT.Copy)
                    ins.then_inc(tiled, 1)

                def turn(n, i, tail, more):
                    for at in range(BODY):
                        slot, q = at // GPS, at % GPS
                        act.wait_ge(y_made, n * GPI + i * BODY + at + 1)
                        act.wait_ge(z_made, n * GPI + i * BODY + at - 1 + Z_MADE)
                        nc.scalar.activation(y_sb[:, at % 2, :].rearrange("p (b f) -> p b f", b=2),
                                             y_ps[:, :, 0:TQ * C // 2], ACT.Copy).then_inc(y_moved, 1)
                        if q >= GPS // 2 and (more or not tail or slot < SLOTS - 1):
                            to = (slot + 1) % SLOTS
                            if q == GPS // 2:
                                act.wait_ge(loaded[to], n * (STRIPES // SLOTS * 16) + (i + (slot + 1) // SLOTS) * 16 + 16)
                            for piece in (2 * q - GPS, 2 * q - GPS + 1):
                                to_tiles(to, piece)
                        if tail and more and at == BODY - 2:
                            norm.act_root(act, n + 1)

                act.wait_ge(loaded[0], 16)
                for q in range(GPS):
                    to_tiles(0, q)
                LAST = STRIPES // SLOTS - 1
                with act.Fori(0, NB - 1) as n:
                    with act.Fori(0, LAST) as i:
                        turn(n, i, False, True)
                    turn(n, LAST, True, True)
                with act.Fori(0, LAST) as i:
                    turn(NB - 1, i, False, False)
                turn(NB - 1, LAST, True, False)

            @block.vector
            def _(dve):
                dve.sem_inc(z_moved, Z_MOVED)
                dve.sem_inc(o_added, O_ADDED)

                def times_filter(n, g, at):
                    dve.wait_ge(z_made, n * GPI + g + 1 + Z_MADE)
                    dve.wait_ge(o_made, n * GPI + g - 1 + O_MADE)
                    half = z_ps[:, :, 0:TQ * C // 2].rearrange("p b (t o) -> p b t o", o=C)
                    nc.vector.tensor_tensor(z_sb[:, at % 2, :].rearrange("p (b t o) -> p b t o", b=2, o=C), half,
                                            bcast(bcast(k.gain[:, :], 1, 2), 1, 2), ALU.mult).then_inc(z_moved, 1)

                def add_x(n, g, at):
                    dve.wait_ge(o_made, n * GPI + g + 1 + O_MADE)
                    slot, q = at // GPS % SLOTS, at % GPS
                    for h in range(2):
                        part = xt[:, slot, h, :].rearrange("c (y x) -> c y x", y=PATCH)[:, :, q * COLS:(q + 1) * COLS]
                        ins = nc.vector.scalar_tensor_tensor(
                            out=part, in0=o_ps[:, h, :].rearrange("c (y x) -> c y x", y=PATCH),
                            scalar=k.bias0[:, h, bass.ds(n, 1)], in1=part, op0=ALU.add, op1=ALU.add)
                    ins.then_inc(o_added, 1)

                def measure(n, g, at, stripe):
                    slot, q = at // GPS % SLOTS, at % GPS
                    dve.wait_ge(o_added, n * GPI + g + 1 + O_ADDED)
                    for h in range(2):
                        part = xt[:, slot, h, :].rearrange("c (y x) -> c y x", y=PATCH)[:, :, q * COLS:(q + 1) * COLS]
                        ins = nc.vector.bn_stats(k.x1_recs[:, n, h, stripe, q, :], part)
                    ins.then_inc(measured, 1)

                def ahead(n, i, at):
                    if isinstance(i, int):
                        chunk, part = at // 2, at % 2
                        pieces = ((0, 3), (3, 6))[part]
                        if chunk >= SLOTS:
                            return
                    else:
                        chunk, part = at // GPS, at % GPS
                        pieces = ((0, 2), (2, 3), (3, 5), (5, 6))[part]
                    if part == 0:
                        norm.wait_chunk(dve, norm.loaded_ahead, n, i * (SLOTS // 2) + chunk // 2, chunk % 2)
                    norm.records(i * SLOTS + chunk, chunk % 2, *pieces)

                def image(n, more):
                    times_filter(n, 0, 0)
                    with dve.Fori(0, STRIPES // SLOTS - 1) as i:
                        for at in range(BODY):
                            g = i * BODY + at
                            times_filter(n, g + 1, at + 1)
                            add_x(n, g, at)
                            measure(n, g, at, i * SLOTS + at // GPS)
                            if more:
                                ahead(n, i, at)
                    for at in range(BODY):
                        g = GPI - BODY + at
                        if more and at == BODY - 8:
                            norm.wait_records(dve, n + 1)
                        if g + 1 < GPI:
                            times_filter(n, g + 1, at + 1)
                        add_x(n, g, at)
                        measure(n, g, at, STRIPES - SLOTS + at // GPS)
                        if more:
                            ahead(n, STRIPES // SLOTS - 1, at)
                            if at == BODY - 8:
                                norm.quarter_means(dve, n + 1)
                            if at == BODY - 5:
                                norm.quarter_spread(dve, n + 1)
                            if at == BODY - 3:
                                norm.channel_var(dve, n + 1)
                            if at == BODY - 1:
                                norm.scaled_weights(dve, n + 1)
                    if more:
                        norm.bias(dve, n + 1)

                with dve.Fori(0, NB - 1) as n:
                    image(n, True)
                image(NB - 1, False)


TAPS = 9
IN_BLOCK, FROM_PREV, FROM_NEXT, OUTER, ANGLE, FOURIER = 0, 3, 6, 9, 10, 11
B_INNER, B_OUTER, B_ANGLE, B_FOURIER, B_FOURIER_TURNS = range(5)


def mixing_weights(k):
    nc, d = k.nc, k.dram
    N_SMALL = TAPS + 3
    with ExitStack() as st:
        conv_s = k.sbuf(st, "mag_s_w_sb", [C0, C0, TAPS])
        mag_t = k.sbuf(st, "mag_w_sb", [C0, C0])
        mag_f = k.sbuf(st, "mag_f_w_sb", [C0, C0])
        first = k.sbuf(st, "conv1_first", [C0, C])
        conv0_t = k.sbuf(st, "conv0_sb", [C0, C0])
        bias_in = k.sbuf(st, "bias_in", [C0, 5])
        conv0_b = k.sbuf(st, "conv0_b_sb", [1, C0])
        small = k.sbuf(st, "small", [C0, N_SMALL, C0])
        bias = k.sbuf(st, "bias_small", [C0, 5])
        rep = k.sbuf(st, "rep", [C0, P])
        band = k.sbuf(st, "band", [P, 5, BLK])
        wide = k.sbuf(st, "wide", [P, N_SMALL, C0])
        part = k.sbuf(st, "part", [P, P])
        zero = k.sbuf(st, "zero_row", [P, SIDE])
        ones = k.sbuf(st, "ones_rows", [HC, P])
        mv = k.sbuf(st, "x1_mv", [HC, NB, 2, 2])
        dev = k.sbuf(st, "x1_dev", [HC, NB, 2])
        spread = k.sbuf(st, "x1_spread", [HC, NB, 2])
        mean = k.sbuf(st, "x1_mean", [HC, NB, 2])
        var = k.sbuf(st, "x1_var", [HC, NB, 2])
        root = k.sbuf(st, "x1_root", [HC, NB, 2])
        ratio = k.sbuf(st, "x1_ratio", [HC, NB, 2])
        scale = k.sbuf(st, "x1_scale", [HC, NB, 2])
        minus = k.sbuf(st, "x1_minus_mean", [HC, NB, 2, P])
        w_raw = k.sbuf(st, "conv1_raw", [HC, 2, C1])
        ps_small = k.psum(st, "ps_small", [C0, TAPS + 1, C0])
        ps_b = k.psum(st, "ps_small_b", [C0, 2])
        ps_w0 = k.psum(st, "ps_w0", [HC, 2, C0])
        ps_wide = k.psum(st, "ps_wide", [P, N_SMALL, C0])
        ps_wb = k.psum(st, "ps_wide_b", [P, 5])
        ps_mean = k.psum(st, "ps_x1_mean", [HC, NB, 2])
        ps_var = k.psum(st, "ps_x1_var", [HC, NB, 2])
        ps_row = k.psum(st, "ps_bias_row", [P, NB, C1])
        consts, cleared, chain, mm, rooted = (k.sem("m_" + s) for s in
                                              ("consts", "cleared", "chain", "products", "rooted"))
        placed = k.sem("m_placed")
        col = lambda name: d[name].rearrange("(p o) -> p o", o=1)
        loads = [(conv_s[:, :, :], d["mag_s_w"].rearrange("m c a b -> m c (a b)")),
                 (mag_t[:, :], d["mag_w_t"]), (mag_f[:, :], d["mag_f_w"]), (first[:, :], d["conv1_w"][0:C0, :]),
                 (conv0_t[:, :], d["conv_0_w_t"]), (conv0_b[:, :], d["conv_0_b"].rearrange("(o p) -> o p", o=1)),
                 (small[:, TAPS + 1, :], d["pha_w_t"]), (small[:, TAPS + 2, :], d["conv_1_w_t"]),
                 (rep[:, :], d["c_rep"]), (band[:, :, :], d["c_band"]),
                 (w_raw[:, :, C0:C1], d["conv1_w_t"].rearrange("(h c) o -> c h o", h=2)[:, :, C0:C1])]
        loads += [(bias_in[:, i:i + 1], col(b)) for i, b in
                  enumerate(("mag_s_b", "mag_f_b", "mag_b", "pha_b", "conv_1_b"))]
        mark = {}

        with nc.Block() as block:

            @block.sync
            def _(sp):
                for dst, src in loads:
                    sp.dma_start(dst, src).then_inc(consts, 16)
                sp.wait_ge(cleared, 1)
                for s in range(2):
                    sp.dma_start(k.mix2[s * C1:(s + 1) * C1, :, s * 64:(s + 1) * 64],
                                 d["conv2_w_t"].rearrange("k (q o) -> k q o", q=3)).then_inc(placed, 16)
                sp.wait_ge(placed, 32)

            @block.vector
            def _(dve):
                done = [0]

                def link(ins, name=None):
                    done[0] += 1
                    ins.then_inc(chain, 1)
                    dve.wait_ge(chain, done[0])
                    if name:
                        mark[name] = done[0]

                v = nc.vector
                v.memset(k.mix2[:, :, :], 0.0).then_inc(cleared, 1)
                link(v.memset(ones[:, :], 1.0))
                link(v.memset(zero[:, :], 0.0))
                for n in range(NB):
                    for h in range(2):
                        ins = v.bn_aggr(mv[:, n, h, :], k.x1_recs[:, n, h].rearrange("c s q r -> c (s q r)"))
                link(ins, "means")
                dve.wait_ge(mm, 1)
                link(v.tensor_copy(mean[:, :, :], ps_mean[:, :, :]))
                link(v.tensor_tensor(dev[:, :, :], mv[:, :, :, 0], mean[:, :, :], ALU.subtract))
                link(v.tensor_tensor(dev[:, :, :], dev[:, :, :], dev[:, :, :], ALU.mult))
                link(v.tensor_tensor(spread[:, :, :], dev[:, :, :], mv[:, :, :, 1], ALU.add), "spread")
                dve.wait_ge(mm, 2)
                link(v.tensor_scalar(var[:, :, :], ps_var[:, :, :], EPS, None, ALU.add), "var")
                dve.wait_ge(rooted, 1)
                link(v.reciprocal(ratio[:, :, :], root[:, :, :]))
                link(v.tensor_tensor(ratio[:, :, :], ratio[:, :, :], var[:, :, :], ALU.mult))
                link(v.tensor_tensor(root[:, :, :], root[:, :, :], ratio[:, :, :], ALU.add))
                link(v.tensor_scalar(root[:, :, :], root[:, :, :], 0.5, None, ALU.mult))
                link(v.reciprocal(scale[:, :, :], root[:, :, :]))
                dve.wait_ge(consts, 16 * len(loads))
                dve.wait_ge(mm, 3)
                link(v.tensor_copy(w_raw[:, :, 0:C0], ps_w0[:, :, :]))
                link(v.tensor_copy(small[:, 0:TAPS + 1, :], ps_small[:, :, :]))
                for i in range(2):
                    link(v.tensor_scalar(bias[:, i:i + 1], ps_b[:, i:i + 1], bias_in[:, 2:3], None, ALU.add))
                link(v.tensor_scalar(bias[:, B_ANGLE:B_ANGLE + 1], bias_in[:, 3:4], 1 / (2 * math.pi), None, ALU.mult))
                link(v.tensor_copy(bias[:, B_FOURIER:B_FOURIER + 1], bias_in[:, 4:5]))
                link(v.tensor_scalar(bias[:, B_FOURIER_TURNS:5], bias_in[:, 4:5], 1 / (2 * math.pi), None, ALU.mult),
                     "small")
                for n in range(NB):
                    for h in range(2):
                        v.tensor_scalar(k.w1[:, n, h, :], w_raw[:, h, :], scale[:, n, h:h + 1], None, ALU.mult)
                        ins = v.tensor_scalar(minus[:, n, h, :], ones[:, :], mean[:, n, h:h + 1], -1.0,
                                              ALU.mult, ALU.mult)
                link(ins, "w1")
                dve.wait_ge(mm, 4)
                link(v.tensor_copy(wide[:, :, :], ps_wide[:, :, :]))
                link(v.tensor_copy(k.mix_bias[:, :], ps_wb[:, :]))

                def place(dst, small_index, band_index):
                    return v.tensor_tensor(dst.rearrange("p (u o) -> p u o", u=BLK),
                                           bcast(wide[:, small_index, :], 1, BLK),
                                           bcast(band[:, band_index, :], 2, C0), ALU.mult)

                for dy in range(3):
                    link(place(k.mix[:, IN_BLOCK + dy, :], dy * 3 + 1, 1))
                    for dx in (0, 2):
                        link(place(part[:, :], dy * 3 + dx, dx))
                        link(v.tensor_tensor(k.mix[:, IN_BLOCK + dy, :], k.mix[:, IN_BLOCK + dy, :], part[:, :],
                                             ALU.add))
                    link(place(k.mix[:, FROM_PREV + dy, :], dy * 3 + 0, 3))
                    link(place(k.mix[:, FROM_NEXT + dy, :], dy * 3 + 2, 4))
                for i in range(3):
                    link(place(k.mix[:, OUTER + i, :], TAPS + i, 1))
                for row, (a, b) in enumerate(((B_INNER, B_OUTER), (B_OUTER, B_OUTER))):
                    link(v.tensor_scalar(k.bias_row[:, row, :], zero[:, :], k.mix_bias[:, b:b + 1], None, ALU.add))
                    link(v.tensor_scalar(k.bias_row[:, row, LO:HI], zero[:, LO:HI], k.mix_bias[:, a:a + 1], None,
                                         ALU.add))
                dve.wait_ge(mm, 5)
                link(v.tensor_copy(k.conv1_row[:, :, :], ps_row[:, :, :]))

            @block.scalar
            def _(act):
                act.wait_ge(chain, mark["var"])
                nc.scalar.activation(root[:, :, :], var[:, :, :], ACT.Sqrt).then_inc(rooted, 1)

            @block.tensor
            def _(pe):
                t = nc.tensor
                pe.wait_ge(chain, mark["means"])
                t.matmul(ps_mean[:, :, :], k.avg_c[:, :], mv[:, :, :, 0], start=True, stop=True).then_inc(mm, 1)
                pe.wait_ge(chain, mark["spread"])
                t.matmul(ps_var[:, :, :], k.avg_c[:, :], spread[:, :, :], start=True, stop=True).then_inc(mm, 1)
                pe.wait_ge(consts, 16 * len(loads))
                for tap in range(TAPS):
                    t.matmul(ps_small[:, tap, :], conv_s[:, :, tap], mag_t[:, :], start=True, stop=True)
                t.matmul(ps_small[:, TAPS, :], mag_f[:, :], mag_t[:, :], start=True, stop=True)
                t.matmul(ps_b[:, :], mag_t[:, :], bias_in[:, 0:2], start=True, stop=True)
                for h in range(2):
                    ins = t.matmul(ps_w0[:, h, :], first[:, h * HC:(h + 1) * HC], conv0_t[:, :], start=True, stop=True)
                ins.then_inc(mm, 1)
                pe.wait_ge(chain, mark["small"])
                t.matmul(ps_wide[:, :, :], rep[:, :], small[:, :, :], start=True, stop=True)
                t.matmul(ps_wb[:, :], rep[:, :], bias[:, :], start=True, stop=True).then_inc(mm, 1)
                pe.wait_ge(chain, mark["w1"])
                for n in range(NB):
                    t.matmul(ps_row[:, n, :], minus[:, n, 0, :], k.w1[:, n, 0, :], start=True, stop=False)
                    t.matmul(ps_row[:, n, 0:C0], ones[0:1, :], conv0_b[:, :], start=False, stop=False)
                    ins = t.matmul(ps_row[:, n, :], minus[:, n, 1, :], k.w1[:, n, 1, :], start=False, stop=True)
                ins.then_inc(mm, 1)


def row_transforms(k):
    nc, d = k.nc, k.dram
    F, R = 2 * SIDE, 2 * NFREQ
    SLOTS = 4
    with ExitStack() as st:
        xt = k.sbuf(st, "x1_rows", [HC, SLOTS, 2, SPX])
        s_sb = k.sbuf(st, "conv1_px", [P, 2, 2, 3, P])
        frft = k.sbuf(st, "frft_rows", [P, 2, 3 * SIDE])
        rfft = k.sbuf(st, "rfft_rows", [P, 2, R])
        eye = k.sbuf(st, "eye_rows", [P, P])
        f_sb = k.sbuf(st, "rows_f", [P, 2, F])
        r_sb = k.sbuf(st, "rows_r", [P, 2, R])
        i_sb = k.sbuf(st, "rows_i", [P, 2, SIDE])
        s_ps = k.psum(st, "ps_conv1", [P, 2, 512])
        f_ps = k.psum(st, "ps_rows_f", [P, F])
        r_ps = k.psum(st, "ps_rows_r", [P, 512])
        i_ps = k.psum(st, "ps_rows_i", [P, 512])
        consts = k.sem("r_consts")
        loaded = [k.sem(f"r_loaded{s}") for s in range(SLOTS)]
        stored = [[k.sem(f"r_stored_{b}{slot}") for slot in range(2)] for b in "fri"]
        conv_made, conv_moved, rows_made, rows_moved = (
            k.sem("r_" + s) for s in ("conv_made", "conv_moved", "rows_made", "rows_moved"))
        CONV_MADE, CONV_MOVED, ROWS_MADE, ROWS_MOVED, STORED = SLOTS, 1, 2, 1, 16
        x1v = d["x1"].rearrange("n (h c) (s r) w -> n s c h (r w)", h=2, r=PATCH)
        out_v = [d[name].rearrange("n (s y) c f -> n s (y c) f", y=PATCH) for name in ("t_f", "t_r", "r_0")]
        stage = [(f_sb, f_ps, F), (r_sb, r_ps, R), (i_sb, i_ps, SIDE)]

        with nc.Block() as block:

            @block.sync
            def _(sp):
                sp.dma_start(frft[:, :, :], d["c_frft"]).then_inc(consts, 16)
                sp.dma_start(rfft[:, :, :], d["c_rfft"]).then_inc(consts, 16)
                sp.dma_start(eye[:, :], d["c_eye"]).then_inc(consts, 16)
                with sp.Fori(0, NB) as n:
                    with sp.Fori(0, STRIPES // SLOTS) as i:
                        for slot in range(SLOTS):
                            sp.wait_ge(conv_made, n * STRIPES + i * SLOTS + slot + 1 - SLOTS + CONV_MADE)
                            sp.dma_start(xt[:, slot, :, :], x1v[n, i * SLOTS + slot]).then_inc(loaded[slot], 16)

            @block.tensor
            def _(pe):
                pe.sem_inc(conv_made, CONV_MADE)
                pe.sem_inc(rows_made, ROWS_MADE)

                def conv1(n, i, slot):
                    s = n * STRIPES + i * SLOTS + slot
                    pe.wait_ge(loaded[slot], n * (STRIPES // SLOTS * 16) + i * 16 + 16)
                    pe.wait_ge(conv_moved, s + CONV_MOVED)
                    for y in range(PATCH):
                        for xh in range(2):
                            for h in range(2):
                                px = y * SIDE + xh * P
                                ins = nc.tensor.matmul(s_ps[:, xh, y * C1:(y + 1) * C1], xt[:, slot, h, px:px + P],
                                                       k.w1[:, n, h, :], start=(h == 0), stop=(h == 1))
                    ins.then_inc(conv_made, 1)

                def rows(n, i, slot):
                    s = n * STRIPES + i * SLOTS + slot
                    slot = slot % 2
                    pe.wait_ge(conv_moved, s + 1 + CONV_MOVED)
                    pe.wait_ge(rows_moved, s + ROWS_MOVED)
                    for xh in range(2):
                        nc.tensor.matmul(f_ps[:, :], s_sb[:, slot, xh, 1, :], frft[:, xh, SIDE:3 * SIDE],
                                         start=(xh == 0), stop=(xh == 1))
                    for xh in range(2):
                        nc.tensor.matmul(r_ps[:, 0:R], s_sb[:, slot, xh, 2, :], rfft[:, xh, :],
                                         start=(xh == 0), stop=(xh == 1))
                    for xh in range(2):
                        ins = nc.tensor.transpose(i_ps[:, xh * P:(xh + 1) * P], s_sb[:, slot, xh, 0, :], eye[:, :])
                    ins.then_inc(rows_made, 1)

                pe.wait_ge(consts, 48)
                with pe.Fori(0, NB) as n:
                    conv1(n, 0, 0)
                    LAST = STRIPES // SLOTS - 1
                    with pe.Fori(0, LAST) as i:
                        for slot in range(SLOTS):
                            conv1(n, i + (slot + 1) // SLOTS, (slot + 1) % SLOTS)
                            rows(n, i, slot)
                    for slot in range(SLOTS):
                        if slot + 1 < SLOTS:
                            conv1(n, LAST, slot + 1)
                        rows(n, LAST, slot)

            @block.vector
            def _(dve):
                dve.sem_inc(conv_moved, CONV_MOVED)
                with dve.Fori(0, NB) as n:
                    with dve.Fori(0, STRIPES // 2) as i:
                        for slot in range(2):
                            s = n * STRIPES + i * 2 + slot
                            dve.wait_ge(conv_made, s + 1 + CONV_MADE)
                            dve.wait_ge(rows_made, s - 1 + ROWS_MADE)
                            for xh in range(2):
                                ins = nc.vector.tensor_tensor(
                                    s_sb[:, slot, xh].rearrange("p b (y c) -> p b y c", y=PATCH),
                                    s_ps[:, xh, 0:PATCH * C1].rearrange("p (y b c) -> p b y c", y=PATCH, b=3),
                                    bcast(k.conv1_row[:, n, :].rearrange("p (b c) -> p b c", b=3), 2, PATCH), ALU.add)
                            ins.then_inc(conv_moved, 1)

            @block.scalar
            def _(act):
                act.sem_inc(rows_moved, ROWS_MOVED)
                for b in range(3):
                    for slot in range(2):
                        act.sem_inc(stored[b][slot], STORED)
                with act.Fori(0, NB) as n:
                    with act.Fori(0, STRIPES // 2) as i:
                        for slot in range(2):
                            s = n * STRIPES + i * 2 + slot
                            act.wait_ge(rows_made, s + 1 + ROWS_MADE)
                            for b, (sb, ps, w) in enumerate(stage):
                                act.wait_ge(stored[b][slot], n * (8 * STRIPES) + i * 16 + STORED)
                                ins = nc.scalar.activation(sb[:, slot, :], ps[:, 0:w], ACT.Copy)
                            ins.then_inc(rows_moved, 1)
                            act.wait_ge(rows_moved, s + 1 + ROWS_MOVED)
                            for b, (sb, ps, w) in enumerate(stage):
                                act.dma_start(out_v[b][n, i * 2 + slot], sb[:, slot, :]).then_inc(stored[b][slot], 16)
                for b in range(3):
                    for slot in range(2):
                        act.wait_ge(stored[b][slot], NB * 8 * STRIPES + STORED)


N_F = 33
N_R = 17
F_RUNS = ((0, 5, 0), (5, 23, LO), (28, 4, HI), (32, 1, SIDE - BLK))
R_LAST = NFREQ - BLK
IN_LAST = HI - (LO + 22 * BLK)
OUT_LAST = LO - 4 * BLK
MAGIC = 1.5 * 2.0**23
TURN = 6.2831850
FRFT, DFT, IFRFT, IRFFT = range(4)


def paired(eng, first, count, body):
    if count > 2:
        with eng.Fori(0, count // 2) as i:
            for p in range(2):
                body(i * 2 + p, (first + p) % 2)
    else:
        for j in range(count // 2 * 2):
            body(j, (first + j) % 2)
    if count % 2:
        body(count - 1, (first + count - 1) % 2)


def spectra(k):
    nc, d = k.nc, k.dram
    COLS_A_F, COLS_A_R, COLS_C_F, COLS_C_R = 0, N_F, N_F + N_R, N_F + N_R + STRIPES
    N_COLS = N_F + N_R + 2 * STRIPES
    N_ROOT = N_F + N_R + STRIPES
    N_MIX = N_F + N_R
    OUT_C_F, OUT_C_R = N_MIX, N_MIX + STRIPES
    N_OUT = N_MIX + 2 * STRIPES
    assert N_COLS % 2 == 0 and N_MIX % 2 == 0 and N_OUT % 2 == 0
    with ExitStack() as st:
        plane = k.sbuf(st, "plane", [P, 2, C0 * 2 * SIDE])
        mag = k.sbuf(st, "magnitude", [P, N_F, SIDE])
        half_tan = k.sbuf(st, "half_tangent", [P, N_F, SIDE])
        left = k.sbuf(st, "real_negative", [P, N_F, SIDE], U8)
        frft = k.sbuf(st, "frft_cols", [P, 2, 3 * SIDE])
        ifrft = k.sbuf(st, "ifrft_cols", [P, 2, 3 * SIDE])
        dft = k.sbuf(st, "dft_cols", [P, 2, 5 * SIDE])
        irfft = k.sbuf(st, "irfft_rows", [P, 2, SIDE])
        eye = k.sbuf(st, "eye_cols", [P, P])
        quarter = k.sbuf(st, "quarter_turn", [P, 1])
        ones = k.sbuf(st, "ones_channels", [P, C0])
        cols = k.sbuf(st, "cols", [P, 2, 2, 2, P])
        squares = k.sbuf(st, "squares", [P, 2, 2 * SIDE])
        angle = k.sbuf(st, "half_angle", [P, 2, SIDE])
        work = k.sbuf(st, "work", [P, SIDE])
        phase = k.sbuf(st, "phase", [P, 2, SIDE])
        mixed_mag = k.sbuf(st, "mixed_mag", [P, SIDE])
        turns = k.sbuf(st, "turns", [P, SIDE])
        whole = k.sbuf(st, "whole_turns", [P, SIDE])
        rest = k.sbuf(st, "rest", [P, 2, 2, SIDE])
        wave = k.sbuf(st, "wave", [P, 2, 2, SIDE])
        flip = k.sbuf(st, "flipped", [P, 2, 2, 2, P])
        out_sb = k.sbuf(st, "out_rows", [P, 2, 2 * SIDE])
        cols_ps = k.psum(st, "ps_cols", [P, 2, 2 * SIDE])
        mix_ps = k.psum(st, "ps_mix", [P, 2, 2, SIDE])
        flip_ps = k.psum(st, "ps_flip", [P, 2, 2, P])
        back_ps = k.psum(st, "ps_back", [P, 2 * SIDE])
        S = lambda name: k.sem("c_" + name)
        consts, plane_in, quartered = S("consts"), S("plane_in"), S("quarter")
        staged, made, squared, added, rooted, freed, chain_a = (
            S(n) for n in ("staged", "made", "squared", "added", "rooted", "freed", "chain_a"))
        angled, phased, mixed, turned, waved, formed, flipped, spread, backed, rowed = (
            S(n) for n in ("angled", "phased", "mixed", "turned", "waved", "formed", "flipped", "spread",
                           "backed", "rowed"))
        chain_phase, chain_turn = S("chain_phase"), S("chain_turn")
        sent = [S("sent0"), S("sent1")]
        nyquist_sent = S("nyquist_sent")
        MADE, FREED, PHASED, MIXED, TURNED, WAVED, FLIPPED, BACKED = (2,) * 8
        SPREAD, ROWED, FORMED = 1, 1, 1
        SENT = 16
        plane_f = lambda h: plane[:, h, :].rearrange("p (c r w) -> p r w c", c=C0, r=2)
        plane_r = lambda h: plane[:, h, 0:C0 * 2 * NFREQ].rearrange("p (c r w) -> p r w c", c=C0, r=2)
        flat_f = d["w_f"].rearrange("n u c f -> n (u c) f")
        flat_r = d["w_r"].rearrange("n u c f -> n (u c) f")
        rows_f = d["r_f"].rearrange("n y c x -> n (y c) x")
        rows_r = d["r_r"].rearrange("n y c x -> n (y c) x")

        half_rows = lambda name, n: d[name][n].rearrange("(h u) c f -> u h (c f)", h=2)

        def sent_before(n, out, j, slot):
            p = (slot - out) % 2
            return n * (N_OUT // 2 * 16) + (j - p) * 8 + (out + p - slot) // 2 * 16 + SENT

        with nc.Block() as block:

            @block.sync
            def _(sp):
                for dst, src in ((frft, "c_frft"), (ifrft, "c_ifrft"), (dft, "c_dft"), (irfft, "c_irfft")):
                    sp.dma_start(dst[:, :, :], d[src]).then_inc(consts, 16)
                sp.dma_start(eye[:, :], d["c_eye"]).then_inc(consts, 16)
                for slot in range(2):
                    sp.sem_inc(sent[slot], SENT)

                def rows_out(n, out, j, slot, dst, lo=0, hi=P):
                    sp.dma_start(dst, out_sb[lo:hi, slot, 0:dst.shape[-1]]).then_inc(sent[slot], 16)

                with sp.Fori(0, NB) as n:
                    sp.wait_ge(made, n * N_COLS + MADE)
                    sp.dma_start(plane[:, :, :], half_rows("t_f", n)).then_inc(plane_in, 16)
                    sp.wait_ge(made, n * N_COLS + COLS_A_R + MADE)
                    sp.dma_start(plane[:, :, 0:C0 * 2 * NFREQ], half_rows("t_r", n)).then_inc(plane_in, 16)
                    for first, count, u0 in F_RUNS:
                        def store(j, slot, first=first, u0=u0, lo=0, hi=P):
                            b = first + j
                            sp.wait_ge(rowed, n * N_MIX + b + 1 + ROWED)
                            rows_out(n, b, 0, slot, flat_f[n, bass.ds((u0 + j * BLK) * C0 + lo, hi - lo), :], lo, hi)

                        if first == 0:
                            paired(sp, 0, 4, store)
                            store(4, 0, hi=OUT_LAST * C0)
                        elif first == 5:
                            paired(sp, 5, 22, store)
                            store(22, 1, hi=IN_LAST * C0)
                        elif first == 28:
                            paired(sp, 28, 4, store)
                        else:
                            store(0, 0, lo=(HI + 4 * BLK - u0) * C0)
                    def store_r(j, slot):
                        sp.wait_ge(rowed, n * N_MIX + N_F + j + 1 + ROWED)
                        sp.dma_start(flat_r[n, bass.ds(j * (BLK * C0), P), :], out_sb[:, slot, :]).then_inc(sent[slot], 16)

                    sp.wait_ge(rowed, n * N_MIX + N_F + 1 + ROWED)
                    sp.dma_start(flat_r[n, 0:P, 0:SIDE], out_sb[:, 1, 0:SIDE]).then_inc(sent[1], 16)
                    sp.dma_start(flat_r[n, C0:P, SIDE:2 * SIDE], out_sb[C0:P, 1, SIDE:2 * SIDE]).then_inc(nyquist_sent, 16)
                    paired(sp, N_F + 1, N_R - 2, lambda j, slot: store_r(j + 1, slot))
                    sp.wait_ge(rowed, n * N_MIX + N_MIX + ROWED)
                    sp.dma_start(flat_r[n, 0:C0, SIDE:2 * SIDE], out_sb[P - C0:P, 1, 0:SIDE]).then_inc(sent[1], 16)

                    def store_c(j, slot):
                        sp.wait_ge(rooted, n * N_ROOT + COLS_C_F + j + 1)
                        sp.dma_start(rows_f[n, bass.ds(j * P, P), :], out_sb[:, slot, 0:SIDE]).then_inc(sent[slot], 16)

                    paired(sp, OUT_C_F, STRIPES, store_c)
                    def store_cr(j, slot):
                        sp.wait_ge(freed, n * N_COLS + COLS_C_R + j + 1 + FREED)
                        sp.dma_start(rows_r[n, bass.ds(j * P, P), :], out_sb[:, slot, 0:SIDE]).then_inc(sent[slot], 16)

                    paired(sp, OUT_C_R, STRIPES, store_cr)
                for slot in range(2):
                    sp.wait_ge(sent[slot], NB * (N_OUT // 2) * 16 + SENT)

            @block.gpsimd
            def _(pool):
                nc.gpsimd.memset(quarter[:, :], math.pi / 2).then_inc(quartered, 1)
                nc.gpsimd.memset(ones[:, :], 1.0).then_inc(quartered, 1)
                pool.wait_ge(quartered, 2)

                def stage(n, number, slot, source, halves, pos, planes):
                    pool.wait_ge(plane_in, n * 64 + planes * 16)
                    pool.wait_ge(made, n * N_COLS + number - 1 + MADE)
                    for h in range(halves):
                        dst = cols[:, slot, h, :, :].rearrange("p r (u c) -> p r u c", c=C0)
                        src = source(h)[:, :, bass.ds(pos, BLK), :]
                        if h == 0:
                            ins = nc.gpsimd.tensor_tensor(dst, src, bcast(bcast(ones[:, :], 1, BLK), 1, 2), ALU.mult)
                        else:
                            ins = nc.gpsimd.tensor_copy(dst, src)
                    ins.then_inc(staged, 1)

                with pool.Fori(0, NB) as n:
                    for first, count, u0 in F_RUNS:
                        paired(pool, first, count, lambda j, slot: stage(n, first + j, slot, plane_f, 2, u0 + j * BLK, 1))
                    paired(pool, COLS_A_R, 16, lambda j, slot: stage(n, COLS_A_R + j, slot, plane_r, 2, j * BLK, 2))
                    stage(n, COLS_A_R + 16, 1, plane_r, 2, R_LAST, 2)
                    paired(pool, COLS_C_F, STRIPES, lambda j, slot: stage(n, COLS_C_F + j, slot, plane_f, 2, j * BLK, 3))
                    paired(pool, COLS_C_R, STRIPES, lambda j, slot: stage(n, COLS_C_R + j, slot, plane_f, 1, j * BLK, 4))

            @block.tensor
            def _(pe):
                mm = nc.tensor.matmul
                for s, credit in ((made, MADE), (mixed, MIXED), (flipped, FLIPPED), (backed, BACKED)):
                    pe.sem_inc(s, credit)
                wide = {FRFT: (frft, SIDE, 0), DFT: (dft, 3 * SIDE, 2 * SIDE), IFRFT: (ifrft, SIDE, 0)}

                def columns(n, number, slot, transform):
                    pe.wait_ge(staged, n * N_COLS + number + 1)
                    pe.wait_ge(freed, n * N_COLS + number - 1 + FREED)
                    if transform == IRFFT:
                        for ri in range(2):
                            ins = mm(cols_ps[:, slot, 0:SIDE], cols[:, slot, 0, ri, :], irfft[:, ri, :],
                                     start=(ri == 0), stop=(ri == 1))
                    else:
                        table, re, im = wide[transform]
                        for h in range(2):
                            for ri, at in enumerate((re, im)):
                                ins = mm(cols_ps[:, slot, :], cols[:, slot, h, ri, :],
                                         table[:, h, at:at + 2 * SIDE], start=(h + ri == 0), stop=(h + ri == 2))
                    ins.then_inc(made, 1)

                def mix(n, b, slot, kind, base=0):
                    pe.wait_ge(phased, n * N_MIX + base + b + 1 + PHASED)
                    pe.wait_ge(turned, n * N_MIX + base + b - 1 + TURNED)
                    out = lambda lo, hi: mix_ps[:, slot, 0, lo:hi]
                    if kind in ("first", "inner", "last"):
                        rows = IN_LAST * C0 if kind == "last" else P
                        terms = [(rows, IN_BLOCK, b)]
                        if kind != "first":
                            terms.append((P, FROM_PREV, b - 1))
                        if kind != "last":
                            terms.append((P, FROM_NEXT, b + 1))
                        todo = [(r, w + dy, at, dy) for r, w, at in terms for dy in (1, 0, 2)]
                        for i, (r, w, at, dy) in enumerate(todo):
                            lo, hi = LO + (dy == 0), HI - (dy == 2)
                            mm(out(lo, hi), k.mix[0:r, w, :], mag[0:r, at, lo + dy - 1:hi + dy - 1],
                               start=(i == 0), stop=(i == len(todo) - 1))
                        for lo, hi in ((0, LO), (HI, SIDE)):
                            mm(out(lo, hi), k.mix[:, OUTER, :], mag[:, b, lo:hi], start=True, stop=True)
                    else:
                        w = FOURIER if kind == "fourier" else OUTER
                        mm(out(0, SIDE), k.mix[:, w, :], mag[:, b, :], start=True, stop=True)
                    w = FOURIER if kind == "fourier" else ANGLE
                    mm(mix_ps[:, slot, 1, :], k.mix[:, w, :], phase[:, slot, :],
                       start=True, stop=True).then_inc(mixed, 1)

                def back(n, b, slot, table, re, im):
                    pe.wait_ge(formed, n * N_MIX + b + 1 + FORMED)
                    pe.wait_ge(spread, n * N_MIX + b + SPREAD)
                    for h in range(2):
                        for ri in range(2):
                            ins = nc.tensor.transpose(flip_ps[:, h, ri, :], wave[:, slot, ri, h * P:(h + 1) * P],
                                                      eye[:, :])
                    ins.then_inc(flipped, 1)
                    pe.wait_ge(spread, n * N_MIX + b + 1 + SPREAD)
                    pe.wait_ge(rowed, n * N_MIX + b + ROWED)
                    for h in range(2):
                        for ri, at in enumerate((re, im)):
                            ins = mm(back_ps[:, :], flip[:, slot, h, ri, :], table[:, h, at:at + 2 * SIDE],
                                     start=(h + ri == 0), stop=(h + ri == 2))
                    ins.then_inc(backed, 1)

                pe.wait_ge(consts, 80)
                with pe.Fori(0, NB) as n:
                    for first, count, u0 in F_RUNS:
                        paired(pe, first, count, lambda j, slot: columns(n, first + j, slot, FRFT))

                    def step_f(b, slot, kind):
                        mix(n, b, slot, kind)
                        back(n, b - 1, 1 - slot, ifrft, SIDE, 0)

                    mix(n, 0, 0, "outer")
                    paired(pe, 1, 4, lambda j, slot: step_f(j + 1, slot, "outer"))
                    step_f(5, 1, "first")
                    paired(pe, 6, 21, lambda j, slot: step_f(j + 6, slot, "inner"))
                    step_f(27, 1, "last")
                    paired(pe, 28, 5, lambda j, slot: step_f(j + 28, slot, "outer"))
                    back(n, N_F - 1, 0, ifrft, SIDE, 0)

                    paired(pe, COLS_A_R, 16, lambda j, slot: columns(n, COLS_A_R + j, slot, DFT))
                    columns(n, COLS_A_R + 16, 1, DFT)
                    mix(n, 0, 1, "fourier", base=N_F)

                    def step_r(j, slot):
                        mix(n, j, slot, "fourier", base=N_F)
                        back(n, N_F + j - 1, 1 - slot, dft, SIDE, 0)

                    paired(pe, N_F + 1, 15, lambda j, slot: step_r(j + 1, slot))
                    step_r(16, 1)
                    back(n, N_F + 16, 1, dft, SIDE, 0)

                    paired(pe, COLS_C_F, STRIPES, lambda j, slot: columns(n, COLS_C_F + j, slot, IFRFT))
                    paired(pe, COLS_C_R, STRIPES, lambda j, slot: columns(n, COLS_C_R + j, slot, IRFFT))

            @block.scalar
            def _(act):
                a = nc.scalar.activation
                for s, credit in ((waved, WAVED), (spread, SPREAD), (rowed, ROWED)):
                    act.sem_inc(s, credit)
                act.wait_ge(quartered, 2)

                def root(n, number, slot, dst, out=None, j=None):
                    act.wait_ge(made, n * N_COLS + number + 1 + MADE)
                    a(squares[:, slot, :], cols_ps[:, slot, :], ACT.Square).then_inc(squared, 1)
                    if out is not None:
                        act.wait_ge(sent[slot], sent_before(n, out, j, slot))
                    act.wait_ge(added, n * N_ROOT + number + 1)
                    if out is None:
                        a(squares[:, slot, SIDE:2 * SIDE], cols_ps[:, slot, 0:SIDE], ACT.Abs)
                    a(dst, squares[:, slot, 0:SIDE], ACT.Sqrt).then_inc(rooted, 1)

                def half_angle(n, b, slot, base):
                    act.wait_ge(phased, n * N_MIX + base + b - 1 + PHASED)
                    a(angle[:, slot, :], half_tan[:, b, :], ACT.Arctan).then_inc(angled, 1)

                def waves(n, b, slot):
                    act.wait_ge(turned, n * N_MIX + b + 1 + TURNED)
                    act.wait_ge(flipped, n * N_MIX + b - 1 + FLIPPED)
                    a(wave[:, slot, 0, :], rest[:, slot, 1, :], ACT.Sin, scale=-TURN, bias=quarter[:, :])
                    a(wave[:, slot, 1, :], rest[:, slot, 0, :], ACT.Sin, scale=TURN).then_inc(waved, 1)

                def move_flip(n, b, slot):
                    act.wait_ge(flipped, n * N_MIX + b + 1 + FLIPPED)
                    act.wait_ge(backed, n * N_MIX + b - 1 + BACKED)
                    a(flip[:, slot, :, :, :], flip_ps[:, :, :, :], ACT.Copy).then_inc(spread, 1)

                def move_back(n, base, j, slot, nyquist=False):
                    act.wait_ge(backed, n * N_MIX + base + j + 1 + BACKED)
                    act.wait_ge(sent[slot], sent_before(n, base, j, slot))
                    if nyquist:
                        act.wait_ge(nyquist_sent, n * 16 + 16)
                    a(out_sb[:, slot, :], back_ps[:, :], ACT.Copy).then_inc(rowed, 1)

                with act.Fori(0, NB) as n:
                    for first, count, u0 in F_RUNS:
                        paired(act, first, count,
                               lambda j, slot: root(n, first + j, slot, mag[:, first + j, :]))

                    def turn_f(b, slot, ahead=True):
                        waves(n, b, slot)
                        move_back(n, 0, b - 1, 1 - slot)
                        if ahead:
                            half_angle(n, b + 2, slot, 0)
                        move_flip(n, b, slot)

                    act.wait_ge(freed, n * N_COLS + COLS_A_R + FREED)
                    half_angle(n, 0, 0, 0)
                    half_angle(n, 1, 1, 0)
                    waves(n, 0, 0)
                    half_angle(n, 2, 0, 0)
                    move_flip(n, 0, 0)
                    paired(act, 1, 30, lambda j, slot: turn_f(j + 1, slot))
                    turn_f(31, 1, False)
                    turn_f(32, 0, False)
                    move_back(n, 0, 32, 0)

                    paired(act, COLS_A_R, 16, lambda j, slot: root(n, COLS_A_R + j, slot, mag[:, j, :]))
                    root(n, COLS_A_R + 16, 1, mag[:, 16, :])
                    act.wait_ge(freed, n * N_COLS + COLS_C_F + FREED)
                    for slot in range(2):
                        act.wait_ge(sent[slot], n * (N_OUT // 2 * 16) + (N_F + 1 - slot) // 2 * 16 + SENT)
                    act.dma_start(plane[:, :, :], half_rows("w_f", n)).then_inc(plane_in, 16)

                    def turn_r(j, slot, ahead=True, nyquist=True):
                        waves(n, N_F + j, slot)
                        move_back(n, N_F, j - 1, 1 - slot, nyquist=nyquist)
                        if ahead:
                            half_angle(n, j + 2, slot, N_F)
                        move_flip(n, N_F + j, slot)

                    half_angle(n, 0, 1, N_F)
                    half_angle(n, 1, 0, N_F)
                    waves(n, N_F, 1)
                    half_angle(n, 2, 1, N_F)
                    move_flip(n, N_F, 1)
                    turn_r(1, 0, nyquist=False)
                    paired(act, N_F + 2, 12, lambda j, slot: turn_r(j + 2, slot))
                    turn_r(14, 1, ahead=True)
                    turn_r(15, 0, ahead=False)
                    turn_r(16, 1, ahead=False)
                    move_back(n, N_F, 16, 1, nyquist=True)

                    paired(act, COLS_C_F, STRIPES,
                           lambda j, slot: root(n, COLS_C_F + j, slot, out_sb[:, slot, 0:SIDE], out=OUT_C_F, j=j))
                    for slot in range(2):
                        act.wait_ge(sent[slot], n * (N_OUT // 2 * 16) + N_MIX // 2 * 16 + SENT)
                    act.wait_ge(nyquist_sent, n * 16 + 16)
                    act.dma_start(plane[:, 0, :], d["w_r"][n].rearrange("u c f -> u (c f)")).then_inc(plane_in, 16)

            @block.vector
            def _(dve):
                v = nc.vector
                for s, credit in ((freed, FREED), (phased, PHASED), (turned, TURNED), (formed, FORMED)):
                    dve.sem_inc(s, credit)

                def polar(n, number, slot, b):
                    dve.wait_ge(squared, n * N_ROOT + number + 1)
                    v.tensor_tensor(squares[:, slot, 0:SIDE], squares[:, slot, 0:SIDE],
                                    squares[:, slot, SIDE:2 * SIDE], ALU.add).then_inc(added, 1)
                    dve.wait_ge(rooted, n * N_ROOT + number + 1)
                    dve.wait_ge(freed, n * N_COLS + number + FREED)
                    link = n * (2 * N_MIX) + number * 2
                    v.tensor_scalar(left[:, b, :], cols_ps[:, slot, 0:SIDE], 0.0, None, ALU.is_lt)
                    v.scalar_tensor_tensor(out=work[:, :], in0=squares[:, slot, SIDE:2 * SIDE], scalar=1e-30,
                                           in1=mag[:, b, :], op0=ALU.max, op1=ALU.add).then_inc(chain_a, 1)
                    dve.wait_ge(chain_a, link + 1)
                    v.reciprocal(work[:, :], work[:, :]).then_inc(chain_a, 1)
                    dve.wait_ge(chain_a, link + 2)
                    v.tensor_tensor(half_tan[:, b, :], cols_ps[:, slot, SIDE:2 * SIDE], work[:, :],
                                    ALU.mult).then_inc(freed, 1)

                def full_angle(n, b, slot, base):
                    dve.wait_ge(angled, n * N_MIX + base + b + 1)
                    dve.wait_ge(mixed, n * N_MIX + base + b - 1 + MIXED)
                    dve.wait_ge(phased, n * N_MIX + base + b + PHASED)
                    link = (n * N_MIX + base + b) * 3
                    v.tensor_scalar(work[:, :], half_tan[:, b, :], 0.0, 2 * math.pi, ALU.is_ge,
                                    ALU.mult).then_inc(chain_phase, 1)
                    dve.wait_ge(chain_phase, link + 1)
                    v.scalar_tensor_tensor(out=work[:, :], in0=angle[:, slot, :], scalar=-4.0, in1=work[:, :],
                                           op0=ALU.mult, op1=ALU.add).then_inc(chain_phase, 1)
                    dve.wait_ge(chain_phase, link + 2)
                    v.scalar_tensor_tensor(out=work[:, :], in0=work[:, :], scalar=-math.pi, in1=left[:, b, :],
                                           op0=ALU.add, op1=ALU.mult).then_inc(chain_phase, 1)
                    dve.wait_ge(chain_phase, link + 3)
                    v.scalar_tensor_tensor(out=phase[:, slot, :], in0=angle[:, slot, :], scalar=2.0,
                                           in1=work[:, :], op0=ALU.mult, op1=ALU.add).then_inc(phased, 1)

                def turn_of(n, b, slot, row):
                    dve.wait_ge(mixed, n * N_MIX + b + 1 + MIXED)
                    dve.wait_ge(waved, n * N_MIX + b - 1 + WAVED)
                    dve.wait_ge(formed, n * N_MIX + b + FORMED)
                    link = (n * N_MIX + b) * 3
                    if row is None:
                        v.tensor_scalar(mixed_mag[:, :], mix_ps[:, slot, 0, :],
                                        k.mix_bias[:, B_FOURIER:B_FOURIER + 1], None, ALU.add)
                        shift = k.mix_bias[:, B_FOURIER_TURNS:B_FOURIER_TURNS + 1]
                    else:
                        v.tensor_tensor(mixed_mag[:, :], mix_ps[:, slot, 0, :], k.bias_row[:, row, :], ALU.add)
                        shift = k.mix_bias[:, B_ANGLE:B_ANGLE + 1]
                    v.tensor_scalar(turns[:, :], mix_ps[:, slot, 1, :], 1 / (2 * math.pi), shift, ALU.mult,
                                    ALU.add).then_inc(chain_turn, 1)
                    dve.wait_ge(chain_turn, link + 1)
                    v.tensor_scalar(whole[:, :], turns[:, :], MAGIC, MAGIC, ALU.add,
                                    ALU.subtract).then_inc(chain_turn, 1)
                    dve.wait_ge(chain_turn, link + 2)
                    v.tensor_tensor(rest[:, slot, 0, :], turns[:, :], whole[:, :],
                                    ALU.subtract).then_inc(chain_turn, 1)
                    dve.wait_ge(chain_turn, link + 3)
                    v.scalar_tensor_tensor(out=rest[:, slot, 1, :], in0=rest[:, slot, 0, :], scalar=-1.0,
                                           in1=rest[:, slot, 0, :], op0=ALU.mult, op1=ALU.max).then_inc(turned, 1)

                def form(n, b, slot):
                    dve.wait_ge(waved, n * N_MIX + b + 1 + WAVED)
                    v.tensor_tensor(wave[:, slot, :, :], wave[:, slot, :, :], bcast(mixed_mag[:, :], 1, 2),
                                    ALU.mult).then_inc(formed, 1)

                def turn(n, base, j, slot, row, ahead=True):
                    turn_of(n, base + j, slot, row)
                    form(n, base + j, slot)
                    if ahead:
                        full_angle(n, j + 2, slot, base)

                with dve.Fori(0, NB) as n:
                    for first, count, u0 in F_RUNS:
                        paired(dve, first, count, lambda j, slot: polar(n, first + j, slot, first + j))
                    full_angle(n, 0, 0, 0)
                    full_angle(n, 1, 1, 0)
                    paired(dve, 0, 5, lambda j, slot: turn(n, 0, j, slot, 1))
                    paired(dve, 5, 23, lambda j, slot: turn(n, 0, j + 5, slot, 0))
                    paired(dve, 28, 3, lambda j, slot: turn(n, 0, j + 28, slot, 1))
                    turn(n, 0, 31, 1, 1, ahead=False)
                    turn(n, 0, 32, 0, 1, ahead=False)

                    paired(dve, COLS_A_R, 16, lambda j, slot: polar(n, COLS_A_R + j, slot, j))
                    polar(n, COLS_A_R + 16, 1, 16)
                    full_angle(n, 0, 1, N_F)
                    full_angle(n, 1, 0, N_F)
                    paired(dve, N_F, 14, lambda j, slot: turn(n, N_F, j, slot, None))
                    turn(n, N_F, 14, 1, None, ahead=True)
                    turn(n, N_F, 15, 0, None, ahead=False)
                    turn(n, N_F, 16, 1, None, ahead=False)

                    def sum_squares(j, slot):
                        dve.wait_ge(squared, n * N_ROOT + COLS_C_F + j + 1)
                        v.tensor_tensor(squares[:, slot, 0:SIDE], squares[:, slot, 0:SIDE],
                                        squares[:, slot, SIDE:2 * SIDE], ALU.add).then_inc(added, 1)
                        dve.wait_ge(added, n * N_ROOT + COLS_C_F + j + 1)
                        dve.sem_inc(freed, 1)

                    paired(dve, COLS_C_F, STRIPES, sum_squares)

                    def move_row(j, slot):
                        dve.wait_ge(made, n * N_COLS + COLS_C_R + j + 1 + MADE)
                        dve.wait_ge(sent[slot], sent_before(n, OUT_C_R, j, slot))
                        v.tensor_copy(out_sb[:, slot, 0:SIDE], cols_ps[:, slot, 0:SIDE]).then_inc(freed, 1)

                    paired(dve, COLS_C_R, STRIPES, move_row)


def output(k):
    nc, d = k.nc, k.dram
    SLOTS, HALF = 4, SPX // 2
    with ExitStack() as st:
        br = k.sbuf(st, "branches", [2 * C1, SLOTS, HALF])
        xt = k.sbuf(st, "x1_out", [P, SLOTS, 3, HALF])
        ps = k.psum(st, "ps_out", [P, 2, 3, 512])
        loaded = [k.sem(f"o_loaded{s}") for s in range(SLOTS)]
        stored = [k.sem(f"o_stored{s}") for s in range(SLOTS)]
        made, summed = k.sem("o_made"), k.sem("o_summed")
        SUMMED, MADE, STORED = 2, 2 * SLOTS, 32
        view = lambda name: d[name].rearrange("n (q o) (s r) w -> n s o q (r w)", q=3, r=PATCH // 2)
        x1v, outv = view("x1"), view("out")
        brv = [d[name].rearrange("n (s r) c w -> n s c r w", r=PATCH // 2) for name in ("r_0", "r_f", "r_r")]

        with nc.Block() as block:

            @block.sync
            def _(sp):
                with sp.Fori(0, NB) as n:
                    with sp.Fori(0, STRIPES // SLOTS) as i:
                        for slot in range(SLOTS):
                            s = i * SLOTS + slot
                            sp.wait_ge(made, n * (2 * STRIPES) + s * 2 + 2 - 2 * SLOTS + MADE)
                            sp.wait_ge(stored[slot], n * (STRIPES // SLOTS * 32) + i * 32 + STORED)
                            for half in range(2):
                                for b in range(3):
                                    at = half * C1 + b * C0
                                    sp.dma_start(br[at:at + C0, slot, :].rearrange("c (r w) -> c r w", w=SIDE),
                                                 brv[b][n, s * 2 + half]).then_inc(loaded[slot], 16)
                                sp.dma_start(xt[half * 64:(half + 1) * 64, slot, :, :],
                                             x1v[n, s * 2 + half]).then_inc(loaded[slot], 16)

            @block.tensor
            def _(pe):
                pe.sem_inc(made, MADE)
                with pe.Fori(0, NB) as n:
                    with pe.Fori(0, STRIPES // SLOTS) as i:
                        for slot in range(SLOTS):
                            s = i * SLOTS + slot
                            pe.wait_ge(loaded[slot], n * (STRIPES // SLOTS * 128) + i * 128 + 128)
                            for part in range(2):
                                pe.wait_ge(summed, n * (2 * STRIPES) + s * 2 + part - 1 + SUMMED)
                                for q in range(3):
                                    ins = nc.tensor.matmul(ps[:, part, q, :], k.mix2[:, q, :],
                                                           br[:, slot, part * 512:(part + 1) * 512],
                                                           start=True, stop=True)
                                ins.then_inc(made, 1)

            @block.vector
            def _(dve):
                dve.sem_inc(summed, SUMMED)
                with dve.Fori(0, NB) as n:
                    with dve.Fori(0, STRIPES // SLOTS) as i:
                        for slot in range(SLOTS):
                            s = i * SLOTS + slot
                            for part in range(2):
                                dve.wait_ge(made, n * (2 * STRIPES) + s * 2 + part + 1 + MADE)
                                x1p = xt[:, slot, :, part * 512:(part + 1) * 512]
                                nc.vector.tensor_tensor(x1p, ps[:, part, :, :], x1p, ALU.add).then_inc(summed, 1)

            @block.scalar
            def _(act):
                for slot in range(SLOTS):
                    act.sem_inc(stored[slot], STORED)
                with act.Fori(0, NB) as n:
                    with act.Fori(0, STRIPES // SLOTS) as i:
                        for slot in range(SLOTS):
                            s = i * SLOTS + slot
                            act.wait_ge(summed, n * (2 * STRIPES) + s * 2 + 2 + SUMMED)
                            for half in range(2):
                                act.dma_start(outv[n, s * 2 + half],
                                              xt[half * 64:(half + 1) * 64, slot, :, :]).then_inc(stored[slot], 16)
                for slot in range(SLOTS):
                    act.wait_ge(stored[slot], NB * (STRIPES // SLOTS) * 32 + STORED)


def build(nc, dram):
    k = Core(nc, dram)
    with k.stack:
        k.mix2 = k.sbuf(k.stack, "mix_conv2", [2 * C1, 3, P])
        k.mix = k.sbuf(k.stack, "mix", [P, TAPS + 3, P])
        k.mix_bias = k.sbuf(k.stack, "mix_bias", [P, 5])
        k.bias_row = k.sbuf(k.stack, "bias_row", [P, 2, SIDE])
        k.w1 = k.sbuf(k.stack, "w_conv1", [HC, NB, 2, C1])
        k.conv1_row = k.sbuf(k.stack, "conv1_row", [P, NB, C1])
        with ExitStack() as first:
            k.basis = k.sbuf(first, "basis", [P, 2, P])
            k.avg_c = k.sbuf(first, "avg_group", [HC, HC])
            k.gain = k.sbuf(first, "gain", [P, C])
            k.w_proj = k.sbuf(first, "w_proj", [HC, NB, 2, C])
            k.bias0 = k.sbuf(first, "bias0", [HC, 2, NB])
            k.x1_recs = k.sbuf(first, "x1_recs", [HC, NB, 2, STRIPES, QUADS, 6])
            with ExitStack() as both:
                norm = InputNorm(k, both)
                first_statistics(k, norm)
                patch_filter(k, norm)
            mixing_weights(k)
        row_transforms(k)
        spectra(k)
        output(k)


def layout(inputs):
    flat = inputs["L0_conv_fft_filter"].reshape(C, -1)
    w = {n[8:]: a for n, a in inputs.items() if n.startswith("L1_conv_")}
    arrays = {
        "x": inputs["x"], "filter_t": flat.T, "flat_gain": flat[:, 0].reshape(2, HC).T,
        "w_proj_t": inputs["L0_conv_w_proj"].T, "conv1_w": w["conv1_w"], "conv1_w_t": w["conv1_w"].T,
        "mag_s_w": w["mag_s_w"], "mag_w_t": w["mag_w"].T, "mag_f_w": w["mag_f_w"], "pha_w_t": w["pha_w"].T,
        "conv_0_w_t": w["conv_0_w"].T, "conv_1_w_t": w["conv_1_w"].T, "conv2_w_t": w["conv2_w"].T,
    }
    for name in ("mag_s_b", "mag_f_b", "mag_b", "pha_b", "conv_0_b", "conv_1_b"):
        arrays[name] = w[name]
    return arrays


SCRATCH = {
    "x1": [NB, C, SIDE, SIDE],
    "t_f": [NB, SIDE, C0, 2 * SIDE], "t_r": [NB, SIDE, C0, 2 * NFREQ],
    "w_f": [NB, SIDE, C0, 2 * SIDE], "w_r": [NB, P, C0, 2 * SIDE],
    "r_0": [NB, SIDE, C0, SIDE], "r_f": [NB, SIDE, C0, SIDE], "r_r": [NB, SIDE, C0, SIDE],
}


def kernel(**inputs):
    import concourse.bacc as bacc
    from concourse.bass_utils import run_bass_kernel_spmd

    nc = bacc.Bacc("TRN2", target_bir_lowering=False, num_devices=1)
    inputs = {n: np.asarray(a) for n, a in inputs.items()}
    arrays = {n: np.ascontiguousarray(a) for n, a in {**layout(inputs), **constants()}.items()}
    dram = {n: nc.dram_tensor(n, a.shape, mybir.dt.from_np(a.dtype), kind="ExternalInput").ap()
            for n, a in arrays.items()}
    for n, shape in SCRATCH.items():
        dram[n] = nc.dram_tensor(n, shape, F32).ap()
    dram["out"] = nc.dram_tensor("out", [NB, C, SIDE, SIDE], F32, kind="ExternalOutput").ap()
    build(nc, dram)
    result = run_bass_kernel_spmd(nc, [arrays], core_ids=[0])
    return result.results[0]["out"]
```

```python
import math
from contextlib import ExitStack

import numpy as np

import concourse.bass as bass
from concourse import mybir

ALU = mybir.AluOpType
ACT = mybir.ActivationFunctionType
F32 = mybir.dt.float32
U8 = mybir.dt.uint8

P = 128
NB, C, SIDE = 4, 192, 256
HC = C // 2
PATCH = 8
STRIPES = SIDE // PATCH
SPX = PATCH * SIDE
TILES = SPX // P
QUADS = 4
GROUPS, GC = 32, C // 32
C0 = 16
C1 = 48
BLK = 8
NFREQ = SIDE // 2 + 1
LO = (SIDE - int(SIDE * math.cos(math.pi / 4))) // 2
HI = LO + int(SIDE * math.cos(math.pi / 4))
EPS = 1e-5


def frft_matrix():
    n_ = SIDE
    a = 0.5
    alpha = a * math.pi / 2
    n = np.arange(-2 * n_ + 2, 2 * n_ - 1).astype(np.float64)
    chirp = np.exp(-1j * math.pi / n_ * math.tan(alpha / 2) / 4 * n**2)
    c = math.pi / n_ / math.sin(alpha) / 4
    mid = slice(n_ - 1, 3 * n_ - 2)
    sinc = np.sinc((np.arange(2 * n_ - 1)[:, None] - 2 * np.arange(n_)[None, :]) / 2.0)
    outs = n[mid][::2]
    kern = np.exp(1j * c * (outs[:, None] - n[mid][None, :]) ** 2) * math.sqrt(c / math.pi)
    return np.exp(-1j * (1 - a) * math.pi / 4) * (
        chirp[mid][::2][:, None] * kern * chirp[mid][None, :] @ sinc)


def centered_ifft_matrix():
    shift = (np.arange(SIDE) + SIDE // 2) % SIDE
    inverse = np.argsort(shift)
    g = np.fft.ifft(np.eye(SIDE)[:, shift], axis=-1) * math.sqrt(SIDE)
    return g[:, inverse].T


def cos_sin(n):
    j = (np.arange(n)[:, None] * np.arange(n)[None, :]) % n
    c, s = np.cos(2 * np.pi * j / n), np.sin(2 * np.pi * j / n)
    quarter = (4 * j) % n == 0
    c[quarter], s[quarter] = np.round(c[quarter]), np.round(s[quarter])
    return c, s


def patch_basis():
    y, x = np.meshgrid(np.arange(PATCH), np.arange(PATCH), indexing="ij")
    basis, taps = [], []
    for kx in range(PATCH // 2 + 1):
        for ky in range(PATCH):
            edge = kx in (0, PATCH // 2)
            if edge and ky > PATCH // 2:
                continue
            phase = 2 * np.pi * ((ky * y + kx * x) % PATCH) / PATCH
            tap = np.zeros((PATCH, PATCH // 2 + 1))
            tap[ky, kx] += 0.5
            tap[(-ky) % PATCH if edge else ky, kx] += 0.5
            alone = edge and ky in (0, PATCH // 2)
            norm = 1 / PATCH if alone else math.sqrt(2) / PATCH
            basis.append(np.cos(phase) * norm)
            taps.append(tap)
            if not alone:
                basis.append(np.sin(phase) * norm)
                taps.append(tap)
    return np.array(basis).reshape(64, 64), np.array(taps).reshape(64, 40).T


def two_rows(m):
    return m.reshape(2, P, -1).transpose(1, 0, 2)


def constants():
    basis, taps = patch_basis()
    d = np.zeros((2, 64, PATCH, 2, PATCH))
    for i in range(2):
        d[i, :, :, i, :] = basis.reshape(64, PATCH, PATCH)
    d = d.reshape(P, P)
    ch, part = np.arange(C), np.arange(P)
    a, b = frft_matrix(), frft_matrix() @ centered_ifft_matrix()
    cos, sin = cos_sin(SIDE)
    windows = lambda m: two_rows(np.concatenate([-m.imag.T, m.real.T, m.imag.T], 1))
    k = np.arange(P)[:, None] * np.arange(SIDE)[None, :] % SIDE
    twice = np.where(np.arange(P) == 0, 1.0, 2.0)[:, None] / SIDE**2
    back_re = twice * cos[1][k]
    back_im = -twice * sin[1][k]
    back_im[0] = (-1.0) ** np.arange(SIDE) / SIDE**2
    u = np.arange(P) // C0
    band = lambda off: (u[:, None] == np.arange(BLK)[None, :] + off).astype(float)
    out = {
        "c_basis": np.stack([d.T, d], 1),
        "c_taps": np.concatenate([taps, taps], 1),
        "c_group_x": (part[:, None] // 4 == part[None, :] // 4) / 4.0,
        "c_group_x_ch": (part[:, None] // 4 == ch[None, :] // GC) / 4.0,
        "c_group_ch": (np.arange(HC)[:, None] // GC == np.arange(HC)[None, :] // GC) / float(GC),
        "c_eye": np.eye(P),
        "c_frft": windows(a),
        "c_ifrft": windows(b),
        "c_dft": two_rows(np.concatenate([-sin, cos, sin, cos, -sin], 1)),
        "c_rfft": two_rows(np.concatenate([cos[:, :NFREQ], -sin[:, :NFREQ]], 1)),
        "c_irfft": np.stack([back_re, back_im], 1),
        "c_rep": np.tile(np.eye(C0), (1, BLK)),
        "c_band": np.stack([band(-1), band(0), band(1),
                            (u[:, None] == BLK - 1) * (np.arange(BLK)[None, :] == 0) * 1.0,
                            (u[:, None] == 0) * (np.arange(BLK)[None, :] == BLK - 1) * 1.0], 1),
    }
    return {n: np.ascontiguousarray(v, dtype=np.float32) for n, v in out.items()}


class Core:

    def __init__(self, nc, dram):
        self.nc, self.dram = nc, dram
        self.stack = ExitStack()

        self.sems, self.tensors = {}, 0

    def sbuf(self, stack, name, shape, dtype=F32):
        self.tensors += 1
        return stack.enter_context(self.nc.sbuf_tensor(f"{name}_{self.tensors}", shape, dtype))

    def psum(self, stack, name, shape):
        self.tensors += 1
        return stack.enter_context(self.nc.psum_tensor(f"{name}_{self.tensors}", shape, F32))

    def sem(self, name):
        if name not in self.sems:
            self.sems[name] = self.stack.enter_context(self.nc.semaphore(name))
        return self.sems[name]


def bcast(ap, axis, n):
    shape = list(ap.shape)
    view = ap.unsqueeze(axis)
    return view.to_broadcast(shape[:axis] + [n] + shape[axis:])


STAT_CHUNK = 3072
RECORD = 512
STAT_CHUNKS = C * SIDE * SIDE // P // STAT_CHUNK
STAT_RECS = STAT_CHUNK // RECORD
CHAIN, AT_MEANS, AT_PAIR, AT_VAR, AT_SCALED = 13, 1, 4, 6, 12


class InputNorm:

    def __init__(self, k, st):
        self.k, self.nc = k, k.nc
        self.ring = k.sbuf(st, "stat_ring", [P, 2, STAT_CHUNK])
        self.recs = k.sbuf(st, "stat_recs", [P, STAT_CHUNKS, STAT_RECS, 6])
        self.mv = k.sbuf(st, "stat_mv", [P, 2])
        self.dev = k.sbuf(st, "stat_dev", [P, 1])
        self.pair = k.sbuf(st, "stat_pair", [P, 2])
        self.avg = k.sbuf(st, "avg_quarters", [P, P])
        self.avg_ch = k.sbuf(st, "avg_channels", [P, C])
        self.w_raw = k.sbuf(st, "w_proj_raw", [HC, 2, C])
        self.w_now = k.sbuf(st, "w_proj_now", [HC, 2, C])
        self.flat = k.sbuf(st, "flat_sb", [HC, 2])
        self.chan = k.sbuf(st, "chan_stats", [HC, 2, 2])
        self.var = k.sbuf(st, "chan_var", [HC, 2])
        self.root = k.sbuf(st, "chan_root", [HC, 2])
        self.ratio = k.sbuf(st, "chan_ratio", [HC, 2])
        self.scale = k.sbuf(st, "chan_scale", [HC, 2])
        ps = k.psum(st, "ps_norm", [P, 512])
        self.ps_mean = ps[:, 0:1]
        self.ps_chan = ps[0:HC, 4:8].rearrange("c (h s) -> c h s", h=2)
        self.ps_bias = ps[0:HC, 8:10]
        self.loaded_first = [k.sem("s_first0"), k.sem("s_first1")]
        self.loaded_ahead = [k.sem("s_ahead0"), k.sem("s_ahead1")]
        self.chunk_done = k.sem("s_chunk_done")
        self.chain, self.mm, self.rooted = k.sem("s_chain"), k.sem("s_products"), k.sem("s_rooted")
        self.xv = k.dram["x"].rearrange("n (g c) h w -> n (g c h w)", g=GROUPS).rearrange(
            "n (p j f) -> n j p f", p=P, f=STAT_CHUNK)

    def load(self, eng, loaded, m, j, slot):
        eng.wait_ge(self.chunk_done, m * STAT_CHUNKS + j + 1)
        eng.dma_start(self.ring[:, slot, :], self.xv[m, j]).then_inc(loaded[slot], 16)

    def wait_chunk(self, dve, loaded, before, j_half, slot):
        dve.wait_ge(loaded[slot], before * (STAT_CHUNKS // 2 * 16) + j_half * 16 + 16)

    def records(self, j, slot, first, last):
        for r in range(first, last):
            ins = self.nc.vector.bn_stats(self.recs[:, j, r, :], self.ring[:, slot, r * RECORD:(r + 1) * RECORD])
        if last == STAT_RECS:
            ins.then_inc(self.chunk_done, 1)

    def link(self, dve, m, number, ins):
        ins.then_inc(self.chain, 1)
        dve.wait_ge(self.chain, m * CHAIN + number)

    def wait_records(self, dve, m):
        dve.wait_ge(self.chunk_done, 2 + m * STAT_CHUNKS + STAT_CHUNKS)

    def quarter_means(self, dve, m):
        self.link(dve, m, AT_MEANS, self.nc.vector.bn_aggr(
            self.mv[:, :], self.recs[:, :, :, :].rearrange("p a b c -> p (a b c)")))

    def pe_group_means(self, pe, m):
        pe.wait_ge(self.chain, m * CHAIN + AT_MEANS)
        self.nc.tensor.matmul(self.ps_mean, self.avg[:, :], self.mv[:, 0:1], start=True,
                              stop=True).then_inc(self.mm, 1)

    def quarter_spread(self, dve, m):
        v = self.nc.vector
        dve.wait_ge(self.mm, m * 3 + 1)
        v.tensor_copy(self.pair[:, 0:1], self.ps_mean)
        self.link(dve, m, 2, v.tensor_tensor(self.dev[:, :], self.mv[:, 0:1], self.ps_mean, ALU.subtract))
        self.link(dve, m, 3, v.tensor_tensor(self.dev[:, :], self.dev[:, :], self.dev[:, :], ALU.mult))
        self.link(dve, m, AT_PAIR, v.tensor_tensor(self.pair[:, 1:2], self.dev[:, :], self.mv[:, 1:2], ALU.add))

    def pe_channels(self, pe, m):
        pe.wait_ge(self.chain, m * CHAIN + AT_PAIR)
        for h in range(2):
            ins = self.nc.tensor.matmul(self.ps_chan[:, h, :], self.avg_ch[:, h * HC:(h + 1) * HC],
                                        self.pair[:, :], start=True, stop=True)
        ins.then_inc(self.mm, 1)

    def channel_var(self, dve, m):
        v = self.nc.vector
        dve.wait_ge(self.mm, m * 3 + 2)
        self.link(dve, m, 5, v.tensor_copy(self.chan[:, :, :], self.ps_chan))
        self.link(dve, m, AT_VAR, v.tensor_scalar(self.var[:, :], self.chan[:, :, 1], EPS, None, ALU.add))

    def act_root(self, act, m):
        act.wait_ge(self.chain, m * CHAIN + AT_VAR)
        self.nc.scalar.activation(self.root[:, :], self.var[:, :], ACT.Sqrt).then_inc(self.rooted, 1)

    def scaled_weights(self, dve, m):
        v, k = self.nc.vector, self.k
        dve.wait_ge(self.rooted, m + 1)
        self.link(dve, m, 7, v.reciprocal(self.ratio[:, :], self.root[:, :]))
        self.link(dve, m, 8, v.tensor_tensor(self.ratio[:, :], self.ratio[:, :], self.var[:, :], ALU.mult))
        self.link(dve, m, 9, v.tensor_tensor(self.root[:, :], self.root[:, :], self.ratio[:, :], ALU.add))
        self.link(dve, m, 10, v.tensor_scalar(self.root[:, :], self.root[:, :], 0.5, None, ALU.mult))
        self.link(dve, m, 11, v.reciprocal(self.scale[:, :], self.root[:, :]))
        for h in range(2):
            v.tensor_scalar(k.w_proj[:, m, h, :], self.w_raw[:, h, :], self.scale[:, h:h + 1], None, ALU.mult)
            ins = v.tensor_scalar(self.w_now[:, h, :], self.w_raw[:, h, :], self.scale[:, h:h + 1], None, ALU.mult)
        self.link(dve, m, AT_SCALED, ins)

    def pe_bias(self, pe, m):
        pe.wait_ge(self.chain, m * CHAIN + AT_SCALED)
        for ho in range(2):
            for h in range(2):
                ins = self.nc.tensor.matmul(self.ps_bias[:, ho:ho + 1], self.w_now[:, h, ho * HC:(ho + 1) * HC],
                                            self.chan[:, h, 0:1], start=(h == 0), stop=(h == 1))
        ins.then_inc(self.mm, 1)

    def bias(self, dve, m):
        dve.wait_ge(self.mm, m * 3 + 3)
        for h in range(2):
            ins = self.nc.vector.tensor_scalar(self.k.bias0[:, h, bass.ds(m, 1)], self.ps_bias[:, h:h + 1],
                                               self.flat[:, h:h + 1], -1.0, ALU.mult, ALU.mult)
        self.link(dve, m, CHAIN, ins)


def first_statistics(k, norm):
    nc, d = k.nc, k.dram
    with ExitStack() as st:
        taps = k.sbuf(st, "taps", [40, P])
        filt = k.sbuf(st, "filt", [40, C])
        ps_gain = k.psum(st, "ps_gain", [P, C])
        consts, gains, gains_moved = k.sem("s_consts"), k.sem("s_gains"), k.sem("s_gains_moved")
        loads = ((taps[:, :], d["c_taps"]), (filt[:, :], d["filter_t"]), (norm.avg[:, :], d["c_group_x"]),
                 (norm.avg_ch[:, :], d["c_group_x_ch"]), (norm.flat[:, :], d["flat_gain"]),
                 (norm.w_raw[:, :, :], d["w_proj_t"].rearrange("(h c) o -> c h o", h=2)),
                 (k.basis[:, :, :], d["c_basis"]), (k.avg_c[:, :], d["c_group_ch"]))

        with nc.Block() as block:

            @block.sync
            def _(sp):
                with sp.Fori(0, STAT_CHUNKS // 2) as j:
                    for slot in range(2):
                        norm.load(sp, norm.loaded_first, 0, j * 2 + slot, slot)

            @block.vector
            def _(dve):
                dve.sem_inc(norm.chunk_done, 2)
                with dve.Fori(0, STAT_CHUNKS // 2) as j:
                    for slot in range(2):
                        norm.wait_chunk(dve, norm.loaded_first, 0, j, slot)
                        norm.records(j * 2 + slot, slot, 0, STAT_RECS)
                norm.wait_records(dve, 0)
                norm.quarter_means(dve, 0)
                norm.quarter_spread(dve, 0)
                norm.channel_var(dve, 0)
                dve.wait_ge(gains, 1)
                nc.vector.tensor_copy(k.gain[:, :], ps_gain[:, :]).then_inc(gains_moved, 1)
                norm.scaled_weights(dve, 0)
                norm.bias(dve, 0)
                dve.wait_ge(gains_moved, 1)

            @block.scalar
            def _(act):
                for dst, src in loads:
                    act.dma_start(dst, src).then_inc(consts, 16)
                norm.act_root(act, 0)

            @block.tensor
            def _(pe):
                pe.wait_ge(consts, 16 * len(loads))
                nc.tensor.matmul(ps_gain[:, :], taps[:, :], filt[:, :], start=True, stop=True).then_inc(gains, 1)
                norm.pe_group_means(pe, 0)
                norm.pe_channels(pe, 0)
                norm.pe_bias(pe, 0)


def patch_filter(k, norm):
    nc, d = k.nc, k.dram
    GPS = QUADS
    GPI = STRIPES * GPS
    TQ = TILES // QUADS
    COLS = TQ * 16
    SLOTS = 4
    BODY = SLOTS * GPS
    with ExitStack() as st:
        xt = k.sbuf(st, "x_rows", [HC, SLOTS, 2, SPX])
        xr = k.sbuf(st, "x_tiles", [HC, 2, 2, SPX])
        y_sb = k.sbuf(st, "y_px", [P, 2, TQ * C])
        z_sb = k.sbuf(st, "z_basis", [P, 2, TQ * C])
        y_ps = k.psum(st, "ps_y", [P, 2, 512])
        z_ps = k.psum(st, "ps_z", [P, 2, 512])
        o_ps = k.psum(st, "ps_o", [HC, 2, 512])
        loaded = [k.sem(f"p_loaded{s}") for s in range(SLOTS)]
        stored = [k.sem(f"p_stored{s}") for s in range(SLOTS)]
        tiled = k.sem("p_tiled")
        y_made, y_moved = k.sem("p_y_made"), k.sem("p_y_moved")
        z_made, z_moved = k.sem("p_z_made"), k.sem("p_z_moved")
        o_made, o_added = k.sem("p_o_made"), k.sem("p_o_added")
        measured = k.sem("p_measured")
        Y_MOVED, Z_MADE, Z_MOVED, O_MADE, O_ADDED = 1, 2, 1, 2, 1
        xv = d["x"].rearrange("n (h c) (s r) w -> n s c h (r w)", h=2, r=PATCH)
        x1v = d["x1"].rearrange("n (h c) (s r) w -> n s c h (r w)", h=2, r=PATCH)

        with nc.Block() as block:

            @block.sync
            def _(sp):
                for slot in range(SLOTS):
                    sp.dma_start(xt[:, slot, :, :], xv[0, slot]).then_inc(loaded[slot], 16)

                def turn(n, i, load_n, load_i):
                    for slot in range(SLOTS):
                        sp.wait_ge(measured, n * GPI + i * BODY + slot * GPS + GPS)
                        sp.dma_start(x1v[n, i * SLOTS + slot], xt[:, slot, :, :]).then_inc(stored[slot], 16)
                        if load_n is not None:
                            sp.wait_ge(stored[slot], n * (STRIPES // SLOTS * 16) + i * 16 + 16)
                            sp.dma_start(xt[:, slot, :, :], xv[load_n, load_i * SLOTS + slot]).then_inc(loaded[slot], 16)

                LAST = STRIPES // SLOTS - 1
                with sp.Fori(0, NB - 1) as n:
                    with sp.Fori(0, LAST) as i:
                        turn(n, i, n, i + 1)
                    turn(n, LAST, n + 1, 0)
                with sp.Fori(0, LAST) as i:
                    turn(NB - 1, i, NB - 1, i + 1)
                turn(NB - 1, LAST, None, None)
                for slot in range(SLOTS):
                    sp.wait_ge(stored[slot], NB * (STRIPES // SLOTS * 16))

            @block.gpsimd
            def _(pool):
                with pool.Fori(1, NB) as m:
                    with pool.Fori(0, STAT_CHUNKS // 2) as j:
                        for slot in range(2):
                            norm.load(pool, norm.loaded_ahead, m, j * 2 + slot, slot)

            @block.tensor
            def _(pe):
                pe.sem_inc(z_made, Z_MADE)
                pe.sem_inc(o_made, O_MADE)

                def to_pixels(n, g, at):
                    slot, q = at // GPS % 2, at % GPS
                    pe.wait_ge(tiled, n * GPI + g + 1)
                    pe.wait_ge(y_moved, n * GPI + g + Y_MOVED)
                    for t in range(TQ):
                        for h in range(2):
                            px = (q * TQ + t) * P
                            ins = nc.tensor.matmul(y_ps[:, t // 2, t % 2 * C:(t % 2 + 1) * C],
                                                   xr[:, slot, h, px:px + P], k.w_proj[:, n, h, :],
                                                   start=(h == 0), stop=(h == 1))
                    ins.then_inc(y_made, 1)

                def to_basis(n, g, at):
                    pe.wait_ge(y_moved, n * GPI + g + 1 + Y_MOVED)
                    pe.wait_ge(z_moved, n * GPI + g + Z_MOVED)
                    for j in range(2):
                        w = TQ * C // 2
                        ins = nc.tensor.matmul(z_ps[:, j, 0:w], k.basis[:, 0, :], y_sb[:, at % 2, j * w:(j + 1) * w],
                                               start=True, stop=True)
                    ins.then_inc(z_made, 1)

                def to_channels(n, g, at):
                    pe.wait_ge(z_moved, n * GPI + g + 1 + Z_MOVED)
                    pe.wait_ge(o_added, n * GPI + g + O_ADDED)
                    for h in range(2):
                        rows = o_ps[:, h, :].rearrange("o (y t x) -> o y t x", y=PATCH, t=TQ)
                        for t in range(TQ):
                            at_z = t * C + h * HC
                            ins = nc.tensor.matmul(rows[:, :, t, :], z_sb[:, at % 2, at_z:at_z + HC],
                                                   k.basis[:, 1, :], start=True, stop=True)
                    ins.then_inc(o_made, 1)

                def image(n, more):
                    pe.wait_ge(norm.chain, n * CHAIN + AT_SCALED)
                    to_pixels(n, 0, 0)
                    to_pixels(n, 1, 1)
                    to_basis(n, 0, 0)
                    with pe.Fori(0, STRIPES // SLOTS - 1) as i:
                        for at in range(BODY):
                            g = i * BODY + at
                            to_pixels(n, g + 2, at + 2)
                            to_basis(n, g + 1, at + 1)
                            to_channels(n, g, at)
                    for at in range(BODY):
                        g = GPI - BODY + at
                        if g + 2 < GPI:
                            to_pixels(n, g + 2, at + 2)
                        if g + 1 < GPI:
                            to_basis(n, g + 1, at + 1)
                        to_channels(n, g, at)
                        if more and at == BODY - 6:
                            norm.pe_group_means(pe, n + 1)
                        if more and at == BODY - 4:
                            norm.pe_channels(pe, n + 1)
                    if more:
                        norm.pe_bias(pe, n + 1)

                with pe.Fori(0, NB - 1) as n:
                    image(n, True)
                image(NB - 1, False)

            @block.scalar
            def _(act):
                act.sem_inc(y_moved, Y_MOVED)
                def to_tiles(slot, q):
                    for h in range(2):
                        ins = nc.scalar.activation(
                            xr[:, slot % 2, h, :].rearrange("c (t y x) -> c t y x", t=TILES, y=PATCH)[:, q * TQ:(q + 1) * TQ],
                            xt[:, slot, h, :].rearrange("c (y t x) -> c t y x", t=TILES, y=PATCH)[:, q * TQ:(q + 1) * TQ],
                            ACT.Copy)
                    ins.then_inc(tiled, 1)

                def turn(n, i, tail, more):
                    for at in range(BODY):
                        slot, q = at // GPS, at % GPS
                        act.wait_ge(y_made, n * GPI + i * BODY + at + 1)
                        act.wait_ge(z_made, n * GPI + i * BODY + at - 1 + Z_MADE)
                        nc.scalar.activation(y_sb[:, at % 2, :].rearrange("p (b f) -> p b f", b=2),
                                             y_ps[:, :, 0:TQ * C // 2], ACT.Copy).then_inc(y_moved, 1)
                        if q >= GPS // 2 and (more or not tail or slot < SLOTS - 1):
                            to = (slot + 1) % SLOTS
                            if q == GPS // 2:
                                act.wait_ge(loaded[to], n * (STRIPES // SLOTS * 16) + (i + (slot + 1) // SLOTS) * 16 + 16)
                            for piece in (2 * q - GPS, 2 * q - GPS + 1):
                                to_tiles(to, piece)
                        if tail and more and at == BODY - 2:
                            norm.act_root(act, n + 1)

                act.wait_ge(loaded[0], 16)
                for q in range(GPS):
                    to_tiles(0, q)
                LAST = STRIPES // SLOTS - 1
                with act.Fori(0, NB - 1) as n:
                    with act.Fori(0, LAST) as i:
                        turn(n, i, False, True)
                    turn(n, LAST, True, True)
                with act.Fori(0, LAST) as i:
                    turn(NB - 1, i, False, False)
                turn(NB - 1, LAST, True, False)

            @block.vector
            def _(dve):
                dve.sem_inc(z_moved, Z_MOVED)
                dve.sem_inc(o_added, O_ADDED)

                def times_filter(n, g, at):
                    dve.wait_ge(z_made, n * GPI + g + 1 + Z_MADE)
                    dve.wait_ge(o_made, n * GPI + g - 1 + O_MADE)
                    half = z_ps[:, :, 0:TQ * C // 2].rearrange("p b (t o) -> p b t o", o=C)
                    nc.vector.tensor_tensor(z_sb[:, at % 2, :].rearrange("p (b t o) -> p b t o", b=2, o=C), half,
                                            bcast(bcast(k.gain[:, :], 1, 2), 1, 2), ALU.mult).then_inc(z_moved, 1)

                def add_x(n, g, at):
                    dve.wait_ge(o_made, n * GPI + g + 1 + O_MADE)
                    slot, q = at // GPS % SLOTS, at % GPS
                    for h in range(2):
                        part = xt[:, slot, h, :].rearrange("c (y x) -> c y x", y=PATCH)[:, :, q * COLS:(q + 1) * COLS]
                        ins = nc.vector.scalar_tensor_tensor(
                            out=part, in0=o_ps[:, h, :].rearrange("c (y x) -> c y x", y=PATCH),
                            scalar=k.bias0[:, h, bass.ds(n, 1)], in1=part, op0=ALU.add, op1=ALU.add)
                    ins.then_inc(o_added, 1)

                def measure(n, g, at, stripe):
                    slot, q = at // GPS % SLOTS, at % GPS
                    dve.wait_ge(o_added, n * GPI + g + 1 + O_ADDED)
                    for h in range(2):
                        part = xt[:, slot, h, :].rearrange("c (y x) -> c y x", y=PATCH)[:, :, q * COLS:(q + 1) * COLS]
                        ins = nc.vector.bn_stats(k.x1_recs[:, n, h, stripe, q, :], part)
                    ins.then_inc(measured, 1)

                def ahead(n, i, at):
                    if isinstance(i, int):
                        chunk, part = at // 2, at % 2
                        pieces = ((0, 3), (3, 6))[part]
                        if chunk >= SLOTS:
                            return
                    else:
                        chunk, part = at // GPS, at % GPS
                        pieces = ((0, 2), (2, 3), (3, 5), (5, 6))[part]
                    if part == 0:
                        norm.wait_chunk(dve, norm.loaded_ahead, n, i * (SLOTS // 2) + chunk // 2, chunk % 2)
                    norm.records(i * SLOTS + chunk, chunk % 2, *pieces)

                def image(n, more):
                    times_filter(n, 0, 0)
                    with dve.Fori(0, STRIPES // SLOTS - 1) as i:
                        for at in range(BODY):
                            g = i * BODY + at
                            times_filter(n, g + 1, at + 1)
                            add_x(n, g, at)
                            measure(n, g, at, i * SLOTS + at // GPS)
                            if more:
                                ahead(n, i, at)
                    for at in range(BODY):
                        g = GPI - BODY + at
                        if more and at == BODY - 8:
                            norm.wait_records(dve, n + 1)
                        if g + 1 < GPI:
                            times_filter(n, g + 1, at + 1)
                        add_x(n, g, at)
                        measure(n, g, at, STRIPES - SLOTS + at // GPS)
                        if more:
                            ahead(n, STRIPES // SLOTS - 1, at)
                            if at == BODY - 8:
                                norm.quarter_means(dve, n + 1)
                            if at == BODY - 5:
                                norm.quarter_spread(dve, n + 1)
                            if at == BODY - 3:
                                norm.channel_var(dve, n + 1)
                            if at == BODY - 1:
                                norm.scaled_weights(dve, n + 1)
                    if more:
                        norm.bias(dve, n + 1)

                with dve.Fori(0, NB - 1) as n:
                    image(n, True)
                image(NB - 1, False)


TAPS = 9
IN_BLOCK, FROM_PREV, FROM_NEXT, OUTER, ANGLE, FOURIER = 0, 3, 6, 9, 10, 11
B_INNER, B_OUTER, B_ANGLE, B_FOURIER, B_FOURIER_TURNS = range(5)


def mixing_weights(k):
    nc, d = k.nc, k.dram
    N_SMALL = TAPS + 3
    with ExitStack() as st:
        conv_s = k.sbuf(st, "mag_s_w_sb", [C0, C0, TAPS])
        mag_t = k.sbuf(st, "mag_w_sb", [C0, C0])
        mag_f = k.sbuf(st, "mag_f_w_sb", [C0, C0])
        first = k.sbuf(st, "conv1_first", [C0, C])
        conv0_t = k.sbuf(st, "conv0_sb", [C0, C0])
        bias_in = k.sbuf(st, "bias_in", [C0, 5])
        conv0_b = k.sbuf(st, "conv0_b_sb", [1, C0])
        small = k.sbuf(st, "small", [C0, N_SMALL, C0])
        bias = k.sbuf(st, "bias_small", [C0, 5])
        rep = k.sbuf(st, "rep", [C0, P])
        band = k.sbuf(st, "band", [P, 5, BLK])
        wide = k.sbuf(st, "wide", [P, N_SMALL, C0])
        part = k.sbuf(st, "part", [P, P])
        zero = k.sbuf(st, "zero_row", [P, SIDE])
        ones = k.sbuf(st, "ones_rows", [HC, P])
        mv = k.sbuf(st, "x1_mv", [HC, NB, 2, 2])
        dev = k.sbuf(st, "x1_dev", [HC, NB, 2])
        spread = k.sbuf(st, "x1_spread", [HC, NB, 2])
        mean = k.sbuf(st, "x1_mean", [HC, NB, 2])
        var = k.sbuf(st, "x1_var", [HC, NB, 2])
        root = k.sbuf(st, "x1_root", [HC, NB, 2])
        ratio = k.sbuf(st, "x1_ratio", [HC, NB, 2])
        scale = k.sbuf(st, "x1_scale", [HC, NB, 2])
        minus = k.sbuf(st, "x1_minus_mean", [HC, NB, 2, P])
        w_raw = k.sbuf(st, "conv1_raw", [HC, 2, C1])
        ps_small = k.psum(st, "ps_small", [C0, TAPS + 1, C0])
        ps_b = k.psum(st, "ps_small_b", [C0, 2])
        ps_w0 = k.psum(st, "ps_w0", [HC, 2, C0])
        ps_wide = k.psum(st, "ps_wide", [P, N_SMALL, C0])
        ps_wb = k.psum(st, "ps_wide_b", [P, 5])
        ps_mean = k.psum(st, "ps_x1_mean", [HC, NB, 2])
        ps_var = k.psum(st, "ps_x1_var", [HC, NB, 2])
        ps_row = k.psum(st, "ps_bias_row", [P, NB, C1])
        consts, cleared, chain, mm, rooted = (k.sem("m_" + s) for s in
                                              ("consts", "cleared", "chain", "products", "rooted"))
        placed = k.sem("m_placed")
        col = lambda name: d[name].rearrange("(p o) -> p o", o=1)
        loads = [(conv_s[:, :, :], d["mag_s_w"].rearrange("m c a b -> m c (a b)")),
                 (mag_t[:, :], d["mag_w_t"]), (mag_f[:, :], d["mag_f_w"]), (first[:, :], d["conv1_w"][0:C0, :]),
                 (conv0_t[:, :], d["conv_0_w_t"]), (conv0_b[:, :], d["conv_0_b"].rearrange("(o p) -> o p", o=1)),
                 (small[:, TAPS + 1, :], d["pha_w_t"]), (small[:, TAPS + 2, :], d["conv_1_w_t"]),
                 (rep[:, :], d["c_rep"]), (band[:, :, :], d["c_band"]),
                 (w_raw[:, :, C0:C1], d["conv1_w_t"].rearrange("(h c) o -> c h o", h=2)[:, :, C0:C1])]
        loads += [(bias_in[:, i:i + 1], col(b)) for i, b in
                  enumerate(("mag_s_b", "mag_f_b", "mag_b", "pha_b", "conv_1_b"))]
        mark = {}

        with nc.Block() as block:

            @block.sync
            def _(sp):
                for dst, src in loads:
                    sp.dma_start(dst, src).then_inc(consts, 16)
                sp.wait_ge(cleared, 1)
                for s in range(2):
                    sp.dma_start(k.mix2[s * C1:(s + 1) * C1, :, s * 64:(s + 1) * 64],
                                 d["conv2_w_t"].rearrange("k (q o) -> k q o", q=3)).then_inc(placed, 16)
                sp.wait_ge(placed, 32)

            @block.vector
            def _(dve):
                done = [0]

                def link(ins, name=None):
                    done[0] += 1
                    ins.then_inc(chain, 1)
                    dve.wait_ge(chain, done[0])
                    if name:
                        mark[name] = done[0]

                v = nc.vector
                v.memset(k.mix2[:, :, :], 0.0).then_inc(cleared, 1)
                link(v.memset(ones[:, :], 1.0))
                link(v.memset(zero[:, :], 0.0))
                for n in range(NB):
                    for h in range(2):
                        ins = v.bn_aggr(mv[:, n, h, :], k.x1_recs[:, n, h].rearrange("c s q r -> c (s q r)"))
                link(ins, "means")
                dve.wait_ge(mm, 1)
                link(v.tensor_copy(mean[:, :, :], ps_mean[:, :, :]))
                link(v.tensor_tensor(dev[:, :, :], mv[:, :, :, 0], mean[:, :, :], ALU.subtract))
                link(v.tensor_tensor(dev[:, :, :], dev[:, :, :], dev[:, :, :], ALU.mult))
                link(v.tensor_tensor(spread[:, :, :], dev[:, :, :], mv[:, :, :, 1], ALU.add), "spread")
                dve.wait_ge(mm, 2)
                link(v.tensor_scalar(var[:, :, :], ps_var[:, :, :], EPS, None, ALU.add), "var")
                dve.wait_ge(rooted, 1)
                link(v.reciprocal(ratio[:, :, :], root[:, :, :]))
                link(v.tensor_tensor(ratio[:, :, :], ratio[:, :, :], var[:, :, :], ALU.mult))
                link(v.tensor_tensor(root[:, :, :], root[:, :, :], ratio[:, :, :], ALU.add))
                link(v.tensor_scalar(root[:, :, :], root[:, :, :], 0.5, None, ALU.mult))
                link(v.reciprocal(scale[:, :, :], root[:, :, :]))
                dve.wait_ge(consts, 16 * len(loads))
                dve.wait_ge(mm, 3)
                link(v.tensor_copy(w_raw[:, :, 0:C0], ps_w0[:, :, :]))
                link(v.tensor_copy(small[:, 0:TAPS + 1, :], ps_small[:, :, :]))
                for i in range(2):
                    link(v.tensor_scalar(bias[:, i:i + 1], ps_b[:, i:i + 1], bias_in[:, 2:3], None, ALU.add))
                link(v.tensor_scalar(bias[:, B_ANGLE:B_ANGLE + 1], bias_in[:, 3:4], 1 / (2 * math.pi), None, ALU.mult))
                link(v.tensor_copy(bias[:, B_FOURIER:B_FOURIER + 1], bias_in[:, 4:5]))
                link(v.tensor_scalar(bias[:, B_FOURIER_TURNS:5], bias_in[:, 4:5], 1 / (2 * math.pi), None, ALU.mult),
                     "small")
                for n in range(NB):
                    for h in range(2):
                        v.tensor_scalar(k.w1[:, n, h, :], w_raw[:, h, :], scale[:, n, h:h + 1], None, ALU.mult)
                        ins = v.tensor_scalar(minus[:, n, h, :], ones[:, :], mean[:, n, h:h + 1], -1.0,
                                              ALU.mult, ALU.mult)
                link(ins, "w1")
                dve.wait_ge(mm, 4)
                link(v.tensor_copy(wide[:, :, :], ps_wide[:, :, :]))
                link(v.tensor_copy(k.mix_bias[:, :], ps_wb[:, :]))

                def place(dst, small_index, band_index):
                    return v.tensor_tensor(dst.rearrange("p (u o) -> p u o", u=BLK),
                                           bcast(wide[:, small_index, :], 1, BLK),
                                           bcast(band[:, band_index, :], 2, C0), ALU.mult)

                for dy in range(3):
                    link(place(k.mix[:, IN_BLOCK + dy, :], dy * 3 + 1, 1))
                    for dx in (0, 2):
                        link(place(part[:, :], dy * 3 + dx, dx))
                        link(v.tensor_tensor(k.mix[:, IN_BLOCK + dy, :], k.mix[:, IN_BLOCK + dy, :], part[:, :],
                                             ALU.add))
                    link(place(k.mix[:, FROM_PREV + dy, :], dy * 3 + 0, 3))
                    link(place(k.mix[:, FROM_NEXT + dy, :], dy * 3 + 2, 4))
                for i in range(3):
                    link(place(k.mix[:, OUTER + i, :], TAPS + i, 1))
                for row, (a, b) in enumerate(((B_INNER, B_OUTER), (B_OUTER, B_OUTER))):
                    link(v.tensor_scalar(k.bias_row[:, row, :], zero[:, :], k.mix_bias[:, b:b + 1], None, ALU.add))
                    link(v.tensor_scalar(k.bias_row[:, row, LO:HI], zero[:, LO:HI], k.mix_bias[:, a:a + 1], None,
                                         ALU.add))
                dve.wait_ge(mm, 5)
                link(v.tensor_copy(k.conv1_row[:, :, :], ps_row[:, :, :]))

            @block.scalar
            def _(act):
                act.wait_ge(chain, mark["var"])
                nc.scalar.activation(root[:, :, :], var[:, :, :], ACT.Sqrt).then_inc(rooted, 1)

            @block.tensor
            def _(pe):
                t = nc.tensor
                pe.wait_ge(chain, mark["means"])
                t.matmul(ps_mean[:, :, :], k.avg_c[:, :], mv[:, :, :, 0], start=True, stop=True).then_inc(mm, 1)
                pe.wait_ge(chain, mark["spread"])
                t.matmul(ps_var[:, :, :], k.avg_c[:, :], spread[:, :, :], start=True, stop=True).then_inc(mm, 1)
                pe.wait_ge(consts, 16 * len(loads))
                for tap in range(TAPS):
                    t.matmul(ps_small[:, tap, :], conv_s[:, :, tap], mag_t[:, :], start=True, stop=True)
                t.matmul(ps_small[:, TAPS, :], mag_f[:, :], mag_t[:, :], start=True, stop=True)
                t.matmul(ps_b[:, :], mag_t[:, :], bias_in[:, 0:2], start=True, stop=True)
                for h in range(2):
                    ins = t.matmul(ps_w0[:, h, :], first[:, h * HC:(h + 1) * HC], conv0_t[:, :], start=True, stop=True)
                ins.then_inc(mm, 1)
                pe.wait_ge(chain, mark["small"])
                t.matmul(ps_wide[:, :, :], rep[:, :], small[:, :, :], start=True, stop=True)
                t.matmul(ps_wb[:, :], rep[:, :], bias[:, :], start=True, stop=True).then_inc(mm, 1)
                pe.wait_ge(chain, mark["w1"])
                for n in range(NB):
                    t.matmul(ps_row[:, n, :], minus[:, n, 0, :], k.w1[:, n, 0, :], start=True, stop=False)
                    t.matmul(ps_row[:, n, 0:C0], ones[0:1, :], conv0_b[:, :], start=False, stop=False)
                    ins = t.matmul(ps_row[:, n, :], minus[:, n, 1, :], k.w1[:, n, 1, :], start=False, stop=True)
                ins.then_inc(mm, 1)


CREDITS = {
    "sync": {"c_sent0": 16, "c_sent1": 16},
    "tensor": {"c_made": 2, "c_mixed": 2, "c_flipped": 2, "c_backed": 2, "r_conv_made": 4, "r_rows_made": 2,
               "o_made": 24},
    "scalar": {"c_waved": 2, "c_lifted": 2, "c_spread": 1, "c_rowed": 1, "r_rows_moved": 1,
               **{f"r_stored_{b}{s}": 16 for b in "fri" for s in range(2)}, **{f"o_stored{s}": 32 for s in range(4)}},
    "vector": {"c_freed": 2, "c_halved": 2, "c_phased": 2, "c_turned": 2, "c_formed": 1, "r_conv_moved": 1, "o_summed": 3},
}
CREDIT = {name: value for by_name in CREDITS.values() for name, value in by_name.items()}


def give_credits(k):
    d = k.dram
    tables = ((k.frft, "c_frft"), (k.ifrft, "c_ifrft"), (k.dft, "c_dft"), (k.irfft, "c_irfft"), (k.eye, "c_eye"))
    with k.nc.Block() as block:

        @block.sync
        def _(sp):
            tabled = k.sem("tables_loaded")
            for table, name in tables:
                sp.dma_start(table[(slice(None),) * len(table.shape)], d[name]).then_inc(tabled, 16)
            sp.wait_ge(tabled, 16 * len(tables))
            for name, value in CREDITS["sync"].items():
                sp.sem_inc(k.sem(name), value)

        @block.tensor
        def _(pe):
            for name, value in CREDITS["tensor"].items():
                pe.sem_inc(k.sem(name), value)

        @block.gpsimd
        def _(pool):
            filled = k.sem("constants_filled")
            k.nc.gpsimd.memset(k.quarter[:, :], math.pi / 2).then_inc(filled, 1)
            k.nc.gpsimd.memset(k.ones[:, :], 1.0).then_inc(filled, 1)
            pool.wait_ge(filled, 2)

        @block.scalar
        def _(act):
            for name, value in CREDITS["scalar"].items():
                act.sem_inc(k.sem(name), value)

        @block.vector
        def _(dve):
            for name, value in CREDITS["vector"].items():
                dve.sem_inc(k.sem(name), value)


def rows_and_output(k, rn, on):
    nc, d = k.nc, k.dram
    F, R = 2 * SIDE, 2 * NFREQ
    SLOTS, HALF, SUMS = 4, SPX // 2, 6
    TURNS = STRIPES // SLOTS
    LAST = TURNS - 1
    with ExitStack() as st:
        if rn is not None:
            xt = k.sbuf(st, "x1_rows", [HC, SLOTS, 2, SPX])
            s_sb = k.sbuf(st, "conv1_px", [P, 2, 2, 3, P])
            rfft = k.sbuf(st, "rfft_rows", [P, 2, R])
            frft, eye = k.frft, k.eye
            f_sb = k.sbuf(st, "rows_f", [P, 2, F])
            r_sb = k.sbuf(st, "rows_r", [P, 2, R])
            i_sb = k.sbuf(st, "rows_i", [P, 2, SIDE])
            s_ps = k.psum(st, "ps_conv1", [P, 2, 512])
            f_ps = k.psum(st, "ps_rows_f", [P, F])
            r_ps = k.psum(st, "ps_rows_r", [P, 512])
            i_ps = k.psum(st, "ps_rows_i", [P, 512])
            stage = [(f_sb, f_ps, F), (r_sb, r_ps, R), (i_sb, i_ps, SIDE)]
        if on is not None:
            br = k.sbuf(st, "branches", [2 * C1, SLOTS, HALF])
            xo = k.sbuf(st, "x1_out", [P, SLOTS, 3, HALF])
            o_ps = k.psum(st, "ps_out", [P, 3, 512])
        consts = k.sem("r_consts")
        loaded = [k.sem(f"r_loaded{s}") for s in range(SLOTS)]
        stored = [[k.sem(f"r_stored_{b}{slot}") for slot in range(2)] for b in "fri"]
        conv_made, conv_moved, rows_made, rows_moved = (
            k.sem("r_" + s) for s in ("conv_made", "conv_moved", "rows_made", "rows_moved"))
        CONV_MADE, CONV_MOVED, ROWS_MADE, ROWS_MOVED, STORED = (
            CREDIT[s] for s in ("r_conv_made", "r_conv_moved", "r_rows_made", "r_rows_moved", "r_stored_f0"))
        o_loaded = [k.sem(f"o_loaded{s}") for s in range(SLOTS)]
        o_stored = [k.sem(f"o_stored{s}") for s in range(SLOTS)]
        o_made, o_summed = k.sem("o_made"), k.sem("o_summed")
        O_MADE, O_SUMMED, O_STORED = CREDIT["o_made"], CREDIT["o_summed"], CREDIT["o_stored0"]
        x1v = d["x1"].rearrange("n (h c) (s r) w -> n s c h (r w)", h=2, r=PATCH)
        rows_v = [d[name].rearrange("n (s y) c f -> n s (y c) f", y=PATCH) for name in ("t_f", "t_r", "r_0")]
        view = lambda name: d[name].rearrange("n (q o) (s r) w -> n s o q (r w)", q=3, r=PATCH // 2)
        x1o, outv = view("x1"), view("out")
        brv = [d[name].rearrange("n (s r) c w -> n s c r w", r=PATCH // 2) for name in ("r_0", "r_f", "r_r")]

        with nc.Block() as block:

            @block.sync
            def _(sp):
                if rn is not None:
                    sp.dma_start(rfft[:, :, :], d["c_rfft"]).then_inc(consts, 16)
                with sp.Fori(0, TURNS) as i:
                    for slot in range(SLOTS):
                        if rn is not None:
                            sp.wait_ge(conv_made, rn * STRIPES + i * SLOTS + slot + 1 - SLOTS + CONV_MADE)
                            sp.dma_start(xt[:, slot, :, :], x1v[rn, i * SLOTS + slot]).then_inc(loaded[slot], 16)
                        if on is not None:
                            s = i * SLOTS + slot
                            sp.wait_ge(o_made, on * (SUMS * STRIPES) + s * SUMS + SUMS - SUMS * SLOTS + O_MADE)
                            sp.wait_ge(o_stored[slot], on * (TURNS * 32) + i * 32 + O_STORED)
                            for half in range(2):
                                for b in range(3):
                                    at = half * C1 + b * C0
                                    sp.dma_start(br[at:at + C0, slot, :].rearrange("c (r w) -> c r w", w=SIDE),
                                                 brv[b][on, s * 2 + half]).then_inc(o_loaded[slot], 16)
                                sp.dma_start(xo[half * 64:(half + 1) * 64, slot, :, :],
                                             x1o[on, s * 2 + half]).then_inc(o_loaded[slot], 16)

            @block.tensor
            def _(pe):

                def conv2(i, slot, number):
                    part, q = number // 3, number % 3
                    if number == 0:
                        pe.wait_ge(o_loaded[slot], on * (TURNS * 128) + i * 128 + 128)
                    pe.wait_ge(o_summed, on * (SUMS * STRIPES) + (i * SLOTS + slot) * SUMS + number - 2 + O_SUMMED)
                    nc.tensor.matmul(o_ps[:, q, :], k.mix2[:, q, :], br[:, slot, part * 512:(part + 1) * 512],
                                     start=True, stop=True).then_inc(o_made, 1)

                def conv1(i, slot, other=None):
                    s = rn * STRIPES + i * SLOTS + slot
                    pe.wait_ge(loaded[slot], rn * (TURNS * 16) + i * 16 + 16)
                    pe.wait_ge(conv_moved, s + CONV_MOVED)
                    for y in range(PATCH):
                        for xh in range(2):
                            for h in range(2):
                                px = y * SIDE + xh * P
                                ins = nc.tensor.matmul(s_ps[:, xh, y * C1:(y + 1) * C1], xt[:, slot, h, px:px + P],
                                                       k.w1[:, rn, h, :], start=(h == 0), stop=(h == 1))
                        if y == PATCH - 1:
                            ins.then_inc(conv_made, 1)
                        if other is not None and y < SUMS:
                            conv2(*other, y)

                def rows(i, slot):
                    s = rn * STRIPES + i * SLOTS + slot
                    slot = slot % 2
                    pe.wait_ge(conv_moved, s + 1 + CONV_MOVED)
                    pe.wait_ge(rows_moved, s + ROWS_MOVED)
                    for xh in range(2):
                        nc.tensor.matmul(f_ps[:, :], s_sb[:, slot, xh, 1, :], frft[:, xh, SIDE:3 * SIDE],
                                         start=(xh == 0), stop=(xh == 1))
                    for xh in range(2):
                        nc.tensor.matmul(r_ps[:, 0:R], s_sb[:, slot, xh, 2, :], rfft[:, xh, :],
                                         start=(xh == 0), stop=(xh == 1))
                    for xh in range(2):
                        ins = nc.tensor.transpose(i_ps[:, xh * P:(xh + 1) * P], s_sb[:, slot, xh, 0, :], eye[:, :])
                    ins.then_inc(rows_made, 1)

                if rn is None:
                    with pe.Fori(0, TURNS) as i:
                        for slot in range(SLOTS):
                            for number in range(SUMS):
                                conv2(i, slot, number)
                else:
                    pe.wait_ge(consts, rn * 16 + 16)
                    conv1(0, 0)
                    with pe.Fori(0, LAST) as i:
                        for slot in range(SLOTS):
                            conv1(i + (slot + 1) // SLOTS, (slot + 1) % SLOTS, None if on is None else (i, slot))
                            rows(i, slot)
                    for slot in range(SLOTS):
                        if slot + 1 < SLOTS:
                            conv1(LAST, slot + 1, None if on is None else (LAST, slot))
                        elif on is not None:
                            for number in range(SUMS):
                                conv2(LAST, slot, number)
                        rows(LAST, slot)

            @block.vector
            def _(dve):

                def sums(i, slot):
                    for number in range(SUMS):
                        part, q = number // 3, number % 3
                        dve.wait_ge(o_made, on * (SUMS * STRIPES) + (i * SLOTS + slot) * SUMS + number + 1 + O_MADE)
                        x1p = xo[:, slot, q, part * 512:(part + 1) * 512]
                        nc.vector.tensor_tensor(x1p, o_ps[:, q, :], x1p, ALU.add).then_inc(o_summed, 1)

                def move_conv1(i, slot):
                    s = rn * STRIPES + i * SLOTS + slot
                    dve.wait_ge(conv_made, s + 1 + CONV_MADE)
                    dve.wait_ge(rows_made, s - 1 + ROWS_MADE)
                    for xh in range(2):
                        ins = nc.vector.tensor_tensor(
                            s_sb[:, slot % 2, xh].rearrange("p b (y c) -> p b y c", y=PATCH),
                            s_ps[:, xh, 0:PATCH * C1].rearrange("p (y b c) -> p b y c", y=PATCH, b=3),
                            bcast(k.conv1_row[:, rn, :].rearrange("p (b c) -> p b c", b=3), 2, PATCH), ALU.add)
                    ins.then_inc(conv_moved, 1)

                if rn is None:
                    with dve.Fori(0, TURNS) as i:
                        for slot in range(SLOTS):
                            sums(i, slot)
                else:
                    move_conv1(0, 0)
                    with dve.Fori(0, LAST) as i:
                        for slot in range(SLOTS):
                            if on is not None:
                                sums(i, slot)
                            move_conv1(i + (slot + 1) // SLOTS, (slot + 1) % SLOTS)
                    for slot in range(SLOTS):
                        if on is not None:
                            sums(LAST, slot)
                        if slot + 1 < SLOTS:
                            move_conv1(LAST, slot + 1)

            @block.scalar
            def _(act):
                with act.Fori(0, TURNS) as i:
                    for slot in range(SLOTS):
                        if on is not None:
                            s = i * SLOTS + slot
                            act.wait_ge(o_summed, on * (SUMS * STRIPES) + s * SUMS + SUMS + O_SUMMED)
                            for half in range(2):
                                act.dma_start(outv[on, s * 2 + half],
                                              xo[half * 64:(half + 1) * 64, slot, :, :]).then_inc(o_stored[slot], 16)
                        if rn is not None:
                            s = rn * STRIPES + i * SLOTS + slot
                            act.wait_ge(rows_made, s + 1 + ROWS_MADE)
                            for b, (sb, ps, w) in enumerate(stage):
                                act.wait_ge(stored[b][slot % 2], rn * (8 * STRIPES) + i * 32 + slot // 2 * 16 + STORED)
                                ins = nc.scalar.activation(sb[:, slot % 2, :], ps[:, 0:w], ACT.Copy)
                            ins.then_inc(rows_moved, 1)
                            act.wait_ge(rows_moved, s + 1 + ROWS_MOVED)
                            for b, (sb, ps, w) in enumerate(stage):
                                act.dma_start(rows_v[b][rn, i * SLOTS + slot],
                                              sb[:, slot % 2, :]).then_inc(stored[b][slot % 2], 16)
                if rn is not None:
                    for b in range(3):
                        for slot in range(2):
                            act.wait_ge(stored[b][slot], rn * (8 * STRIPES) + 8 * STRIPES + STORED)
                if on is not None:
                    for slot in range(SLOTS):
                        act.wait_ge(o_stored[slot], on * (TURNS * 32) + TURNS * 32 + O_STORED)
                act.sem_inc(k.sem("r_in_dram"), 1)


N_F = 33
N_R = 17
F_RUNS = ((0, 5, 0), (5, 23, LO), (28, 4, HI), (32, 1, SIDE - BLK))
R_LAST = NFREQ - BLK
IN_LAST = HI - (LO + 22 * BLK)
OUT_LAST = LO - 4 * BLK
MAGIC = 1.5 * 2.0**23
TURN = 6.2831850
FRFT, DFT, IFRFT, IRFFT = range(4)


def paired(eng, first, count, body):
    if count > 2:
        with eng.Fori(0, count // 2) as i:
            for p in range(2):
                body(i * 2 + p, (first + p) % 2)
    else:
        for j in range(count // 2 * 2):
            body(j, (first + j) % 2)
    if count % 2:
        body(count - 1, (first + count - 1) % 2)


def spectra(k, n):
    nc, d = k.nc, k.dram
    COLS_A_F, COLS_A_R, COLS_C_F, COLS_C_R = 0, N_F, N_F + N_R, N_F + N_R + STRIPES
    N_COLS = N_F + N_R + 2 * STRIPES
    N_ROOT = N_F + N_R + STRIPES
    N_MIX = N_F + N_R
    N_C = 2 * STRIPES
    OUT_C_F, OUT_C_R = N_MIX, N_MIX + STRIPES
    N_OUT = N_MIX + STRIPES + STRIPES // 2
    assert N_COLS % 2 == 0 and N_MIX % 2 == 0 and N_OUT % 2 == 0
    with ExitStack() as st:
        plane = k.sbuf(st, "plane", [P, 2, C0 * 2 * SIDE])
        mag = k.sbuf(st, "magnitude", [P, N_F, SIDE])
        half_tan = k.sbuf(st, "half_tangent", [P, N_F, SIDE])
        left = k.sbuf(st, "real_negative", [P, N_F, SIDE], U8)
        frft, ifrft, dft, irfft, eye = k.frft, k.ifrft, k.dft, k.irfft, k.eye
        quarter, ones = k.quarter, k.ones
        cols = k.sbuf(st, "cols", [P, 2, 2, 2, P])
        squares = k.sbuf(st, "squares", [P, 2, 2 * SIDE])
        angle = k.sbuf(st, "half_angle", [P, 2, SIDE])
        work = k.sbuf(st, "work", [P, SIDE])
        phase = k.sbuf(st, "phase", [P, 2, SIDE])
        mixed_mag = k.sbuf(st, "mixed_mag", [P, SIDE])
        turns = k.sbuf(st, "turns", [P, SIDE])
        whole = k.sbuf(st, "whole_turns", [P, SIDE])
        rest = k.sbuf(st, "rest", [P, 2, 2, SIDE])
        wave = k.sbuf(st, "wave", [P, 2, 2, SIDE])
        flat = wave
        flip = k.sbuf(st, "flipped", [P, 2, 2, 2, P])
        out_sb = k.sbuf(st, "out_rows", [P, 2, 2 * SIDE])
        cols_ps = k.psum(st, "ps_cols", [P, 2, 2 * SIDE])
        mix_ps = k.psum(st, "ps_mix", [P, 2, 2, SIDE])
        flip_ps = k.psum(st, "ps_flip", [P, 2, 2, P])
        back_ps = k.psum(st, "ps_back", [P, 2 * SIDE])
        S = lambda name: k.sem("c_" + name)
        first_in, plane_in = S("first_in"), S("plane_in")
        staged, made, squared, added, rooted, freed, chain_a = (
            S(n) for n in ("staged", "made", "squared", "added", "rooted", "freed", "chain_a"))
        angled, phased, mixed, turned, waved, formed, flipped, spread, backed, rowed = (
            S(n) for n in ("angled", "phased", "mixed", "turned", "waved", "formed", "flipped", "spread",
                           "backed", "rowed"))
        chain_phase, chain_turn = S("chain_phase"), S("chain_turn")
        lifted, halved = S("lifted"), S("halved")
        sent = [S("sent0"), S("sent1")]
        nyquist_sent = S("nyquist_sent")
        MADE, FREED, LIFTED, HALVED, PHASED, MIXED, TURNED, WAVED, FLIPPED, BACKED, SPREAD, ROWED, FORMED, SENT = (
            CREDIT["c_" + s] for s in ("made", "freed", "lifted", "halved", "phased", "mixed", "turned", "waved", "flipped", "backed",
                                       "spread", "rowed", "formed", "sent0"))
        plane_f = lambda h: plane[:, h, :].rearrange("p (c r w) -> p r w c", c=C0, r=2)
        plane_back = lambda h: mag[:, 0:STRIPES, :].rearrange("p b x -> p (b x)").rearrange(
            "p (c r w) -> p r w c", c=C0, r=2)
        plane_r = lambda h: plane[:, h, 0:C0 * 2 * NFREQ].rearrange("p (c r w) -> p r w c", c=C0, r=2)
        flat_f = d["w_f"].rearrange("n u c f -> n (u c) f")
        flat_r = d["w_r"].rearrange("n u c f -> n (u c) f")
        rows_f = d["r_f"].rearrange("n y c x -> n (y c) x")
        rows_r = d["r_r"].rearrange("n y c x -> n (y c) x")

        PIECES_T_R, PIECES_W_F, PIECES_W_R = 4, 8, 4
        FIRST_W = 64
        THERE = [0, 32]
        for pieces in (PIECES_T_R, PIECES_W_F, PIECES_W_R):
            THERE.append(THERE[-1] + 16 * pieces)

        half_rows = lambda name, n: d[name][n].rearrange("(h u) c f -> u h (c f)", h=2)

        def load_piece(eng, dst, src, piece, pieces, width):
            size = C0 // pieces * width
            at = (slice(None),) * (len(src.shape) - 1) + (bass.ds(piece * size, size),)
            eng.dma_start(dst[at], src[at]).then_inc(plane_in, 16)

        def sent_before(n, out, j, slot):
            p = (slot - out) % 2
            return n * (N_OUT // 2 * 16) + (j - p) * 8 + (out + p - slot) // 2 * 16 + SENT

        with nc.Block() as block:

            @block.sync
            def _(sp):

                def rows_out(n, out, j, slot, dst, lo=0, hi=P):
                    sp.dma_start(dst, out_sb[lo:hi, slot, 0:dst.shape[-1]]).then_inc(sent[slot], 16)

                sp.wait_ge(made, n * N_COLS + MADE)
                for lo, hi in ((0, FIRST_W), (FIRST_W, SIDE)):
                    for h in range(2):
                        sp.dma_start(plane[:, h, :].rearrange("p (f w) -> p f w", w=SIDE)[:, :, lo:hi],
                                     half_rows("t_f", n)[:, h].rearrange("p (f w) -> p f w", w=SIDE)[:, :, lo:hi]
                                     ).then_inc(first_in if lo == 0 else plane_in, 16)
                sp.wait_ge(made, n * N_COLS + COLS_A_R + MADE)
                for first, count, u0 in F_RUNS:
                    def store(j, slot, first=first, u0=u0, lo=0, hi=P):
                        b = first + j
                        sp.wait_ge(rowed, n * N_MIX + b + 1 + ROWED)
                        rows_out(n, b, 0, slot, flat_f[n, bass.ds((u0 + j * BLK) * C0 + lo, hi - lo), :], lo, hi)

                    if first == 0:
                        for j in range(4):
                            load_piece(sp, plane, half_rows("t_r", n), j, PIECES_T_R, 2 * NFREQ)
                            store(j, j % 2)
                        store(4, 0, hi=OUT_LAST * C0)
                    elif first == 5:
                        paired(sp, 5, 22, store)
                        store(22, 1, hi=IN_LAST * C0)
                    elif first == 28:
                        paired(sp, 28, 4, store)
                    else:
                        store(0, 0, lo=(HI + 4 * BLK - u0) * C0)
                def store_r(j, slot):
                    sp.wait_ge(rowed, n * N_MIX + N_F + j + 1 + ROWED)
                    sp.dma_start(flat_r[n, bass.ds(j * (BLK * C0), P), :], out_sb[:, slot, :]).then_inc(sent[slot], 16)

                sp.wait_ge(rowed, n * N_MIX + N_F + 1 + ROWED)
                sp.dma_start(flat_r[n, 0:P, 0:SIDE], out_sb[:, 1, 0:SIDE]).then_inc(sent[1], 16)
                sp.dma_start(flat_r[n, C0:P, SIDE:2 * SIDE], out_sb[C0:P, 1, SIDE:2 * SIDE]).then_inc(nyquist_sent, 16)
                paired(sp, N_F + 1, N_R - 2, lambda j, slot: store_r(j + 1, slot))
                sp.wait_ge(rowed, n * N_MIX + N_MIX + ROWED)
                sp.dma_start(flat_r[n, 0:C0, SIDE:2 * SIDE], out_sb[P - C0:P, 1, 0:SIDE]).then_inc(sent[1], 16)

                def store_c(j, slot):
                    sp.wait_ge(rooted, n * N_ROOT + COLS_C_F + j + 1)
                    sp.dma_start(rows_f[n, bass.ds(j * P, P), :], out_sb[:, slot, 0:SIDE]).then_inc(sent[slot], 16)

                paired(sp, OUT_C_F, STRIPES, store_c)
                def store_cr(pair, slot):
                    sp.wait_ge(freed, n * N_C + STRIPES + pair * 2 + 2 + FREED)
                    sp.dma_start(rows_r[n, bass.ds(pair * (2 * P), 2 * P), :].rearrange("(b p) x -> p b x", b=2),
                                 out_sb[:, slot, :].rearrange("p (b x) -> p b x", b=2)).then_inc(sent[slot], 16)

                paired(sp, OUT_C_R, STRIPES // 2, store_cr)
                for slot in range(2):
                    sp.wait_ge(sent[slot], n * (N_OUT // 2 * 16) + N_OUT // 2 * 16 + SENT)
                sp.sem_inc(S("in_dram"), 1)

            @block.gpsimd
            def _(pool):
                def stage(n, number, slot, source, halves, pos, planes):
                    if planes == 0:
                        pool.wait_ge(first_in, n * 32 + 32)
                    else:
                        pool.wait_ge(plane_in, n * THERE[4] + THERE[planes])
                    pool.wait_ge(made, n * N_COLS + number - 1 + MADE)
                    for h in range(halves):
                        dst = cols[:, slot, h, :, :].rearrange("p r (u c) -> p r u c", c=C0)
                        src = source(h)[:, :, bass.ds(pos, BLK), :]
                        if h == 0:
                            ins = nc.gpsimd.tensor_tensor(dst, src, bcast(bcast(ones[:, :], 1, BLK), 1, 2), ALU.mult)
                        else:
                            ins = nc.gpsimd.tensor_copy(dst, src)
                    ins.then_inc(staged, 1)

                for first, count, u0 in F_RUNS:
                    paired(pool, first, count, lambda j, slot: stage(n, first + j, slot, plane_f, 2, u0 + j * BLK,
                                                                          0 if first == 0 else 1))
                paired(pool, COLS_A_R, 16, lambda j, slot: stage(n, COLS_A_R + j, slot, plane_r, 2, j * BLK, 2))
                stage(n, COLS_A_R + 16, 1, plane_r, 2, R_LAST, 2)
                paired(pool, COLS_C_F, STRIPES, lambda j, slot: stage(n, COLS_C_F + j, slot, plane_f, 2, j * BLK, 3))
                paired(pool, COLS_C_R, STRIPES, lambda j, slot: stage(n, COLS_C_R + j, slot, plane_back, 1, j * BLK, 4))

            @block.tensor
            def _(pe):
                mm = nc.tensor.matmul
                wide = {FRFT: (frft, SIDE, 0), DFT: (dft, 3 * SIDE, 2 * SIDE), IFRFT: (ifrft, SIDE, 0)}

                def columns(n, number, slot, transform):
                    pe.wait_ge(staged, n * N_COLS + number + 1)
                    if transform in (FRFT, DFT):
                        pe.wait_ge(lifted, n * N_MIX + number - 1 + LIFTED)
                    else:
                        pe.wait_ge(freed, n * N_C + (number - N_MIX) - 1 + FREED)
                    if transform == IRFFT:
                        for ri in range(2):
                            ins = mm(cols_ps[:, slot, 0:SIDE], cols[:, slot, 0, ri, :], irfft[:, ri, :],
                                     start=(ri == 0), stop=(ri == 1))
                    else:
                        table, re, im = wide[transform]
                        for h in range(2):
                            for ri, at in enumerate((re, im)):
                                ins = mm(cols_ps[:, slot, :], cols[:, slot, h, ri, :],
                                         table[:, h, at:at + 2 * SIDE], start=(h + ri == 0), stop=(h + ri == 2))
                    ins.then_inc(made, 1)

                def mix(n, b, slot, kind, base=0, between=None):
                    pe.wait_ge(phased, n * N_MIX + base + b + 1 + PHASED)
                    pe.wait_ge(turned, n * N_MIX + base + b - 1 + TURNED)
                    out = lambda lo, hi: mix_ps[:, slot, 0, lo:hi]
                    if kind in ("first", "inner", "last"):
                        rows = IN_LAST * C0 if kind == "last" else P
                        terms = [(rows, IN_BLOCK, b)]
                        if kind != "first":
                            terms.append((P, FROM_PREV, b - 1))
                        if kind != "last":
                            terms.append((P, FROM_NEXT, b + 1))
                        todo = [(r, w + dy, at, dy) for r, w, at in terms for dy in (1, 0, 2)]
                        for i, (r, w, at, dy) in enumerate(todo):
                            if i == len(todo) // 2:
                                between()
                            lo, hi = LO + (dy == 0), HI - (dy == 2)
                            mm(out(lo, hi), k.mix[0:r, w, :], mag[0:r, at, lo + dy - 1:hi + dy - 1],
                               start=(i == 0), stop=(i == len(todo) - 1))
                        for lo, hi in ((0, LO), (HI, SIDE)):
                            mm(out(lo, hi), k.mix[:, OUTER, :], mag[:, b, lo:hi], start=True, stop=True)
                    else:
                        w = FOURIER if kind == "fourier" else OUTER
                        mm(out(0, SIDE), k.mix[:, w, :], mag[:, b, :], start=True, stop=True)
                        if between is not None:
                            between()
                    w = FOURIER if kind == "fourier" else ANGLE
                    mm(mix_ps[:, slot, 1, :], k.mix[:, w, :], phase[:, slot, :],
                       start=True, stop=True).then_inc(mixed, 1)

                def to_partitions(n, b, slot):
                    pe.wait_ge(formed, n * N_MIX + b + 1 + FORMED)
                    pe.wait_ge(spread, n * N_MIX + b + SPREAD)
                    for h in range(2):
                        for ri in range(2):
                            ins = nc.tensor.transpose(flip_ps[:, h, ri, :], wave[:, slot, ri, h * P:(h + 1) * P],
                                                      eye[:, :])
                    ins.then_inc(flipped, 1)

                def back(n, b, slot, table, re, im):
                    pe.wait_ge(spread, n * N_MIX + b + 1 + SPREAD)
                    pe.wait_ge(rowed, n * N_MIX + b + ROWED)
                    for h in range(2):
                        for ri, at in enumerate((re, im)):
                            ins = mm(back_ps[:, :], flip[:, slot, h, ri, :], table[:, h, at:at + 2 * SIDE],
                                     start=(h + ri == 0), stop=(h + ri == 2))
                    ins.then_inc(backed, 1)

                for first, count, u0 in F_RUNS:
                    paired(pe, first, count, lambda j, slot: columns(n, first + j, slot, FRFT))

                def step_f(b, slot, kind):
                    mix(n, b, slot, kind, between=lambda: to_partitions(n, b - 2, slot))
                    back(n, b - 2, slot, ifrft, SIDE, 0)

                mix(n, 0, 0, "outer")
                mix(n, 1, 1, "outer")
                paired(pe, 2, 3, lambda j, slot: step_f(j + 2, slot, "outer"))
                step_f(5, 1, "first")
                paired(pe, 6, 21, lambda j, slot: step_f(j + 6, slot, "inner"))
                step_f(27, 1, "last")
                paired(pe, 28, 5, lambda j, slot: step_f(j + 28, slot, "outer"))
                for b in (N_F - 2, N_F - 1):
                    to_partitions(n, b, b % 2)
                    back(n, b, b % 2, ifrft, SIDE, 0)

                paired(pe, COLS_A_R, 16, lambda j, slot: columns(n, COLS_A_R + j, slot, DFT))
                columns(n, COLS_A_R + 16, 1, DFT)
                mix(n, 0, 1, "fourier", base=N_F)
                mix(n, 1, 0, "fourier", base=N_F)

                def step_r(j, slot):
                    mix(n, j, slot, "fourier", base=N_F, between=lambda: to_partitions(n, N_F + j - 2, slot))
                    back(n, N_F + j - 2, slot, dft, SIDE, 0)

                paired(pe, N_F + 2, 14, lambda j, slot: step_r(j + 2, slot))
                step_r(16, 1)
                for b in (N_MIX - 2, N_MIX - 1):
                    to_partitions(n, b, b % 2)
                    back(n, b, b % 2, dft, SIDE, 0)

                pe.wait_ge(lifted, n * N_MIX + N_MIX + LIFTED)
                pe.sem_inc(S("a_is_over"), 1)
                paired(pe, COLS_C_F, STRIPES, lambda j, slot: columns(n, COLS_C_F + j, slot, IFRFT))
                paired(pe, COLS_C_R, STRIPES, lambda j, slot: columns(n, COLS_C_R + j, slot, IRFFT))

            @block.scalar
            def _(act):
                a = nc.scalar.activation

                def root(n, number, slot, dst, out=None, j=None):
                    act.wait_ge(made, n * N_COLS + number + 1 + MADE)
                    if out is None:
                        act.wait_ge(halved, n * N_MIX + number - 1 + HALVED)
                    a(squares[:, slot, :], cols_ps[:, slot, :], ACT.Square).then_inc(squared, 1)
                    if out is None:
                        a(flat[:, slot, :, :], cols_ps[:, slot, :].rearrange("p (r x) -> p r x", r=2),
                          ACT.Copy).then_inc(lifted, 1)
                    else:
                        act.wait_ge(sent[slot], sent_before(n, out, j, slot))
                    act.wait_ge(added, n * N_ROOT + number + 1)
                    if out is None:
                        act.wait_ge(lifted, n * N_MIX + number + 1 + LIFTED)
                        a(squares[:, slot, SIDE:2 * SIDE], flat[:, slot, 0, :], ACT.Abs)
                    a(dst, squares[:, slot, 0:SIDE], ACT.Sqrt).then_inc(rooted, 1)

                def half_angle(n, b, slot, base):
                    act.wait_ge(phased, n * N_MIX + base + b - 1 + PHASED)
                    a(angle[:, slot, :], half_tan[:, b, :], ACT.Arctan).then_inc(angled, 1)

                def waves(n, b, slot):
                    act.wait_ge(turned, n * N_MIX + b + 1 + TURNED)
                    act.wait_ge(flipped, n * N_MIX + b - 1 + FLIPPED)
                    a(wave[:, slot, 0, :], rest[:, slot, 1, :], ACT.Sin, scale=-TURN, bias=quarter[:, :])
                    a(wave[:, slot, 1, :], rest[:, slot, 0, :], ACT.Sin, scale=TURN).then_inc(waved, 1)

                def move_flip(n, b, slot):
                    act.wait_ge(flipped, n * N_MIX + b + 1 + FLIPPED)
                    act.wait_ge(backed, n * N_MIX + b - 1 + BACKED)
                    a(flip[:, slot, :, :, :], flip_ps[:, :, :, :], ACT.Copy).then_inc(spread, 1)

                def move_back(n, base, j, slot, nyquist=False):
                    act.wait_ge(backed, n * N_MIX + base + j + 1 + BACKED)
                    act.wait_ge(sent[slot], sent_before(n, base, j, slot))
                    if nyquist:
                        act.wait_ge(nyquist_sent, n * 16 + 16)
                    a(out_sb[:, slot, :], back_ps[:, :], ACT.Copy).then_inc(rowed, 1)

                for first, count, u0 in F_RUNS:
                    paired(act, first, count,
                           lambda j, slot: root(n, first + j, slot, mag[:, first + j, :]))

                def turn_f(b, slot, ahead=True):
                    move_flip(n, b - 2, slot)
                    if ahead:
                        half_angle(n, b + 2, slot, 0)
                    waves(n, b, slot)
                    move_back(n, 0, b - 2, slot)

                act.wait_ge(halved, n * N_MIX + 2 + HALVED)
                half_angle(n, 0, 0, 0)
                half_angle(n, 1, 1, 0)
                for b in range(2):
                    half_angle(n, b + 2, b, 0)
                    waves(n, b, b)
                paired(act, 2, 29, lambda j, slot: turn_f(j + 2, slot))
                turn_f(31, 1, False)
                turn_f(32, 0, False)
                for b in (N_F - 2, N_F - 1):
                    move_flip(n, b, b % 2)
                    move_back(n, 0, b, b % 2)

                paired(act, COLS_A_R, 16, lambda j, slot: root(n, COLS_A_R + j, slot, mag[:, j, :]))
                root(n, COLS_A_R + 16, 1, mag[:, 16, :])
                act.wait_ge(halved, n * N_MIX + N_F + 2 + HALVED)
                for slot in range(2):
                    act.wait_ge(sent[slot], n * (N_OUT // 2 * 16) + (N_F + 1 - slot) // 2 * 16 + SENT)
                w_f_piece = lambda piece: load_piece(act, plane, half_rows("w_f", n), piece, PIECES_W_F, 2 * SIDE)
                w_f_piece(0)

                def turn_r(j, slot, ahead=True, nyquist=True):
                    move_flip(n, N_F + j - 2, slot)
                    if ahead:
                        half_angle(n, j + 2, slot, N_F)
                    waves(n, N_F + j, slot)
                    move_back(n, N_F, j - 2, slot, nyquist=nyquist)

                half_angle(n, 0, 1, N_F)
                half_angle(n, 1, 0, N_F)
                for j in range(2):
                    half_angle(n, j + 2, 1 - j, N_F)
                    waves(n, N_F + j, 1 - j)
                w_f_piece(1)
                turn_r(2, 1, nyquist=False)
                w_f_piece(2)
                turn_r(3, 0)
                with act.Fori(3, PIECES_W_F) as piece:
                    turn_r(piece * 2 - 2, 1)
                    w_f_piece(piece)
                    turn_r(piece * 2 - 1, 0)
                turn_r(14, 1, ahead=True)
                turn_r(15, 0, ahead=False)
                turn_r(16, 1, ahead=False)
                for j in (15, 16):
                    move_flip(n, N_F + j, (N_F + j) % 2)
                    move_back(n, N_F, j, (N_F + j) % 2, nyquist=True)

                def root_back(j, slot):
                    root(n, COLS_C_F + j, slot, out_sb[:, slot, 0:SIDE], out=OUT_C_F, j=j)

                for j in range(2):
                    root_back(j, j)
                act.wait_ge(mixed, n * N_MIX + N_MIX + MIXED)
                for slot in range(2):
                    act.wait_ge(sent[slot], n * (N_OUT // 2 * 16) + N_MIX // 2 * 16 + SENT)
                act.wait_ge(nyquist_sent, n * 16 + 16)
                for piece in range(PIECES_W_R):
                    load_piece(act, mag[:, 0:STRIPES, :].rearrange("p b x -> p (b x)"),
                               d["w_r"][n].rearrange("u c f -> u (c f)"), piece, PIECES_W_R, 2 * SIDE)
                    for j in range(2):
                        root_back(2 + piece * 2 + j, j)
                DONE = 2 + 2 * PIECES_W_R
                paired(act, COLS_C_F + DONE, STRIPES - DONE, lambda j, slot: root_back(j + DONE, slot))

            @block.vector
            def _(dve):
                v = nc.vector

                def add_squares(n, number, slot):
                    dve.wait_ge(squared, n * N_ROOT + number + 1)
                    v.tensor_tensor(squares[:, slot, 0:SIDE], squares[:, slot, 0:SIDE],
                                    squares[:, slot, SIDE:2 * SIDE], ALU.add).then_inc(added, 1)

                def negative(n, number, slot, b):
                    dve.wait_ge(lifted, n * N_MIX + number + 1 + LIFTED)
                    v.tensor_scalar(left[:, b, :], flat[:, slot, 0, :], 0.0, None, ALU.is_lt)

                def polar(n, number, slot, b, more=True):
                    dve.wait_ge(rooted, n * N_ROOT + number + 1)
                    dve.wait_ge(halved, n * N_MIX + number + HALVED)
                    link = n * (2 * N_MIX) + number * 2
                    v.scalar_tensor_tensor(out=work[:, :], in0=squares[:, slot, SIDE:2 * SIDE], scalar=1e-30,
                                           in1=mag[:, b, :], op0=ALU.max, op1=ALU.add).then_inc(chain_a, 1)
                    if more:
                        add_squares(n, number + 1, 1 - slot)
                    dve.wait_ge(chain_a, link + 1)
                    v.reciprocal(work[:, :], work[:, :]).then_inc(chain_a, 1)
                    if more:
                        negative(n, number + 1, 1 - slot, b + 1)
                    dve.wait_ge(chain_a, link + 2)
                    v.tensor_tensor(half_tan[:, b, :], flat[:, slot, 1, :], work[:, :],
                                    ALU.mult).then_inc(halved, 1)

                def polar_all(n, first, count):
                    add_squares(n, first, first % 2)
                    negative(n, first, first % 2, 0)
                    paired(dve, first, count - 1, lambda j, slot: polar(n, first + j, slot, j))
                    polar(n, first + count - 1, (first + count - 1) % 2, count - 1, more=False)

                def full_angle(n, b, slot, base):
                    dve.wait_ge(angled, n * N_MIX + base + b + 1)
                    dve.wait_ge(mixed, n * N_MIX + base + b - 1 + MIXED)
                    dve.wait_ge(phased, n * N_MIX + base + b + PHASED)
                    link = (n * N_MIX + base + b) * 3
                    v.tensor_scalar(work[:, :], half_tan[:, b, :], 0.0, 2 * math.pi, ALU.is_ge,
                                    ALU.mult).then_inc(chain_phase, 1)
                    dve.wait_ge(chain_phase, link + 1)
                    v.scalar_tensor_tensor(out=work[:, :], in0=angle[:, slot, :], scalar=-4.0, in1=work[:, :],
                                           op0=ALU.mult, op1=ALU.add).then_inc(chain_phase, 1)
                    dve.wait_ge(chain_phase, link + 2)
                    v.scalar_tensor_tensor(out=work[:, :], in0=work[:, :], scalar=-math.pi, in1=left[:, b, :],
                                           op0=ALU.add, op1=ALU.mult).then_inc(chain_phase, 1)
                    dve.wait_ge(chain_phase, link + 3)
                    v.scalar_tensor_tensor(out=phase[:, slot, :], in0=angle[:, slot, :], scalar=2.0,
                                           in1=work[:, :], op0=ALU.mult, op1=ALU.add).then_inc(phased, 1)

                def turn_of(n, b, slot, row):
                    dve.wait_ge(mixed, n * N_MIX + b + 1 + MIXED)
                    dve.wait_ge(waved, n * N_MIX + b - 1 + WAVED)
                    dve.wait_ge(formed, n * N_MIX + b + FORMED)
                    link = (n * N_MIX + b) * 3
                    if row is None:
                        v.tensor_scalar(mixed_mag[:, :], mix_ps[:, slot, 0, :],
                                        k.mix_bias[:, B_FOURIER:B_FOURIER + 1], None, ALU.add)
                        shift = k.mix_bias[:, B_FOURIER_TURNS:B_FOURIER_TURNS + 1]
                    else:
                        v.tensor_tensor(mixed_mag[:, :], mix_ps[:, slot, 0, :], k.bias_row[:, row, :], ALU.add)
                        shift = k.mix_bias[:, B_ANGLE:B_ANGLE + 1]
                    v.tensor_scalar(turns[:, :], mix_ps[:, slot, 1, :], 1 / (2 * math.pi), shift, ALU.mult,
                                    ALU.add).then_inc(chain_turn, 1)
                    dve.wait_ge(chain_turn, link + 1)
                    v.tensor_scalar(whole[:, :], turns[:, :], MAGIC, MAGIC, ALU.add,
                                    ALU.subtract).then_inc(chain_turn, 1)
                    dve.wait_ge(chain_turn, link + 2)
                    v.tensor_tensor(rest[:, slot, 0, :], turns[:, :], whole[:, :],
                                    ALU.subtract).then_inc(chain_turn, 1)
                    dve.wait_ge(chain_turn, link + 3)
                    v.scalar_tensor_tensor(out=rest[:, slot, 1, :], in0=rest[:, slot, 0, :], scalar=-1.0,
                                           in1=rest[:, slot, 0, :], op0=ALU.mult, op1=ALU.max).then_inc(turned, 1)

                def form(n, b, slot):
                    dve.wait_ge(waved, n * N_MIX + b + 1 + WAVED)
                    v.tensor_tensor(wave[:, slot, :, :], wave[:, slot, :, :], bcast(mixed_mag[:, :], 1, 2),
                                    ALU.mult).then_inc(formed, 1)

                def turn(n, base, j, slot, row, ahead=True):
                    turn_of(n, base + j, slot, row)
                    if ahead:
                        full_angle(n, j + 2, slot, base)
                    form(n, base + j, slot)

                polar_all(n, 0, N_F)
                dve.wait_ge(halved, n * N_MIX + N_F + HALVED)
                full_angle(n, 0, 0, 0)
                full_angle(n, 1, 1, 0)
                paired(dve, 0, 5, lambda j, slot: turn(n, 0, j, slot, 1))
                paired(dve, 5, 23, lambda j, slot: turn(n, 0, j + 5, slot, 0))
                paired(dve, 28, 3, lambda j, slot: turn(n, 0, j + 28, slot, 1))
                turn(n, 0, 31, 1, 1, ahead=False)
                turn(n, 0, 32, 0, 1, ahead=False)

                polar_all(n, COLS_A_R, N_R)
                dve.wait_ge(halved, n * N_MIX + N_MIX + HALVED)
                full_angle(n, 0, 1, N_F)
                full_angle(n, 1, 0, N_F)
                paired(dve, N_F, 14, lambda j, slot: turn(n, N_F, j, slot, None))
                turn(n, N_F, 14, 1, None, ahead=True)
                turn(n, N_F, 15, 0, None, ahead=False)
                turn(n, N_F, 16, 1, None, ahead=False)

                def sum_squares(j, slot):
                    dve.wait_ge(squared, n * N_ROOT + COLS_C_F + j + 1)
                    v.tensor_tensor(squares[:, slot, 0:SIDE], squares[:, slot, 0:SIDE],
                                    squares[:, slot, SIDE:2 * SIDE], ALU.add).then_inc(added, 1)
                    dve.wait_ge(added, n * N_ROOT + COLS_C_F + j + 1)
                    dve.sem_inc(freed, 1)

                paired(dve, COLS_C_F, STRIPES, sum_squares)

                def move_rows(pair, slot):
                    for p in range(2):
                        dve.wait_ge(made, n * N_COLS + COLS_C_R + pair * 2 + p + 1 + MADE)
                        if p == 0:
                            dve.wait_ge(sent[slot], sent_before(n, OUT_C_R, pair, slot))
                        v.tensor_copy(out_sb[:, slot, p * SIDE:(p + 1) * SIDE], cols_ps[:, p, 0:SIDE]).then_inc(freed, 1)

                paired(dve, OUT_C_R, STRIPES // 2, move_rows)


def build(nc, dram):
    k = Core(nc, dram)
    with k.stack:
        k.mix2 = k.sbuf(k.stack, "mix_conv2", [2 * C1, 3, P])
        k.mix = k.sbuf(k.stack, "mix", [P, TAPS + 3, P])
        k.mix_bias = k.sbuf(k.stack, "mix_bias", [P, 5])
        k.bias_row = k.sbuf(k.stack, "bias_row", [P, 2, SIDE])
        k.w1 = k.sbuf(k.stack, "w_conv1", [HC, NB, 2, C1])
        k.conv1_row = k.sbuf(k.stack, "conv1_row", [P, NB, C1])
        k.quarter = k.sbuf(k.stack, "quarter_turn", [P, 1])
        k.ones = k.sbuf(k.stack, "ones_channels", [P, C0])
        with ExitStack() as first:
            k.basis = k.sbuf(first, "basis", [P, 2, P])
            k.avg_c = k.sbuf(first, "avg_group", [HC, HC])
            k.gain = k.sbuf(first, "gain", [P, C])
            k.w_proj = k.sbuf(first, "w_proj", [HC, NB, 2, C])
            k.bias0 = k.sbuf(first, "bias0", [HC, 2, NB])
            k.x1_recs = k.sbuf(first, "x1_recs", [HC, NB, 2, STRIPES, QUADS, 6])
            with ExitStack() as both:
                norm = InputNorm(k, both)
                first_statistics(k, norm)
                patch_filter(k, norm)
            mixing_weights(k)
        k.frft = k.sbuf(k.stack, "frft", [P, 2, 3 * SIDE])
        k.ifrft = k.sbuf(k.stack, "ifrft", [P, 2, 3 * SIDE])
        k.dft = k.sbuf(k.stack, "dft", [P, 2, 5 * SIDE])
        k.irfft = k.sbuf(k.stack, "irfft", [P, 2, SIDE])
        k.eye = k.sbuf(k.stack, "eye", [P, P])
        give_credits(k)
        rows_and_output(k, 0, None)
        with nc.Fori(0, NB - 1) as n:
            spectra(k, n)
            rows_and_output(k, n + 1, n)
        spectra(k, NB - 1)
        rows_and_output(k, None, NB - 1)


def layout(inputs):
    flat = inputs["L0_conv_fft_filter"].reshape(C, -1)
    w = {n[8:]: a for n, a in inputs.items() if n.startswith("L1_conv_")}
    arrays = {
        "x": inputs["x"], "filter_t": flat.T, "flat_gain": flat[:, 0].reshape(2, HC).T,
        "w_proj_t": inputs["L0_conv_w_proj"].T, "conv1_w": w["conv1_w"], "conv1_w_t": w["conv1_w"].T,
        "mag_s_w": w["mag_s_w"], "mag_w_t": w["mag_w"].T, "mag_f_w": w["mag_f_w"], "pha_w_t": w["pha_w"].T,
        "conv_0_w_t": w["conv_0_w"].T, "conv_1_w_t": w["conv_1_w"].T, "conv2_w_t": w["conv2_w"].T,
    }
    for name in ("mag_s_b", "mag_f_b", "mag_b", "pha_b", "conv_0_b", "conv_1_b"):
        arrays[name] = w[name]
    return arrays


SCRATCH = {
    "x1": [NB, C, SIDE, SIDE],
    "t_f": [NB, SIDE, C0, 2 * SIDE], "t_r": [NB, SIDE, C0, 2 * NFREQ],
    "w_f": [NB, SIDE, C0, 2 * SIDE], "w_r": [NB, P, C0, 2 * SIDE],
    "r_0": [NB, SIDE, C0, SIDE], "r_f": [NB, SIDE, C0, SIDE], "r_r": [NB, SIDE, C0, SIDE],
}


def kernel(**inputs):
    import concourse.bacc as bacc
    from concourse.bass_utils import run_bass_kernel_spmd

    nc = bacc.Bacc("TRN2", target_bir_lowering=False, num_devices=1)
    inputs = {n: np.asarray(a) for n, a in inputs.items()}
    arrays = {n: np.ascontiguousarray(a) for n, a in {**layout(inputs), **constants()}.items()}
    dram = {n: nc.dram_tensor(n, a.shape, mybir.dt.from_np(a.dtype), kind="ExternalInput").ap()
            for n, a in arrays.items()}
    for n, shape in SCRATCH.items():
        dram[n] = nc.dram_tensor(n, shape, F32).ap()
    dram["out"] = nc.dram_tensor("out", [NB, C, SIDE, SIDE], F32, kind="ExternalOutput").ap()
    build(nc, dram)
    result = run_bass_kernel_spmd(nc, [arrays], core_ids=[0])
    return result.results[0]["out"]
```
